# Optimizing a Trainium2 kernel written in Bass

```python
import numpy as np
import jax
import jax.numpy as jnp

def _softmax(x, axis=-1):
    return jax.nn.softmax(x, axis=axis)

def _gelu(x):
    return jax.nn.gelu(x, approximate=True)

def _silu(x):
    return jax.nn.silu(x)

def _sigmoid(x):
    return jax.nn.sigmoid(x)

def _layernorm(x, axis=-1, eps=1e-05):
    m = jnp.mean(x, axis=axis, keepdims=True)
    v = jnp.var(x, axis=axis, keepdims=True)
    return (x - m) / jnp.sqrt(v + eps)

def _scatter_add(tgt, idx, src, axis=0):
    return tgt.at[idx].add(src)

def _segment_sum(src, seg, n):
    return jax.ops.segment_sum(src, seg, n)
kernel_name = 'mk_flamingo_gated_d2_seqx_r4_c39691'

def setup_inputs(seed: int=0):
    np.random.seed(seed)
    _w = jnp.asarray

    def _rec_inputs():
        import jax
        import jax.numpy as jnp
        _rk = jax.random.key(seed)
        x = -0.000125 + 0.9999 * jax.random.normal(jax.random.fold_in(_rk, 1), (2, 512, 1024), jnp.float32)
        _lenS = 512 - jax.random.randint(jax.random.fold_in(_rk, 7), (2,), 0, max(1, 512 // 4) + 1, jnp.int32)
        _lenS2 = 1024 - jax.random.randint(jax.random.fold_in(_rk, 8), (2,), 0, max(1, 1024 // 4) + 1, jnp.int32)
        _ctx_4096P = jax.random.normal(jax.random.fold_in(_rk, 11), (2, 16, 1024), jnp.float32)
        _ctx_4096c = jax.random.dirichlet(jax.random.fold_in(_rk, 511), 0.3 * jnp.ones((16,), jnp.float32), (2, 1024))
        _ctx_4096t = jnp.einsum('bsk,bkd->bsd', _ctx_4096c, _ctx_4096P)
        _ctx_4096t = _ctx_4096t * jax.lax.rsqrt(jnp.mean(jnp.square(_ctx_4096t)) + 1e-12) * 0.953939
        ctx_4096 = -5.72187e-05 + 0.999849 * (_ctx_4096t + 0.3 * jax.random.normal(jax.random.fold_in(_rk, 611), (2, 1024, 1024), jnp.float32))
        _g = jax.random.normal(jax.random.fold_in(_rk, 9001), (2, 2), jnp.float32)
        _g = jnp.sign(_g) * jnp.maximum(jnp.abs(_g), 1.0) + (_g == 0) * 1.0
        g_xattn = _g[0]
        g_ffn = _g[1]
        return (x, ctx_4096, g_xattn, g_ffn)
    x, ctx_4096, g_xattn, g_ffn = _rec_inputs()

    def _L0_xattn_setup():
        import jax, jax.numpy as jnp
        import numpy as np
        QMIN = 0.0
        QMAX = 255.0

        def fake_quant(x, scale, zp):
            s = scale.reshape(())
            z = zp.reshape(())
            q = jnp.clip(jnp.round(x / s + z), QMIN, QMAX)
            return (q - z) * s
        key = jax.random.key(seed)
        k1, k2 = jax.random.split(key)
        B, M, K, N = (4, 512, 1024, 1024)
        x1 = jax.random.normal(k1, (B, M, K), dtype=jnp.float32)
        x2 = jax.random.normal(k2, (B, K, N), dtype=jnp.float32)
        x1_scale = jnp.full((1,), 8.0 / 255.0, dtype=jnp.float32)
        x1_zp = jnp.full((1,), 128.0, dtype=jnp.float32)
        x2_scale = jnp.full((1,), 8.0 / 255.0, dtype=jnp.float32)
        x2_zp = jnp.full((1,), 128.0, dtype=jnp.float32)
        return {'x1': x1, 'x2': x2, 'x1_scale': x1_scale, 'x1_zp': x1_zp, 'x2_scale': x2_scale, 'x2_zp': x2_zp}
    _L0_xattn_all = _L0_xattn_setup()
    _L0_xattn_in = {k: v for k, v in _L0_xattn_all.items() if k in ('x1_scale', 'x1_zp', 'x2_scale', 'x2_zp')}
    del _L0_xattn_all

    def _L0_ffn_setup():
        import jax, jax.numpy as jnp
        import numpy as np
        import math
        B, S, IN, OUT = (4, 512, 1024, 1024)
        E, R, K = (8, 64, 128)
        SCALE = 64.0 / 64.0
        MULTIPLIER = 1.0
        key = jax.random.key(seed)
        ks = jax.random.split(key, 6)
        return {'x': jax.random.normal(ks[0], (B, S, IN), jnp.float32), 'W_org': jax.random.normal(ks[1], (OUT, IN), jnp.float32) * 0.02, 'lora_down': jax.random.normal(ks[2], (E, IN, R), jnp.float32) * 0.02, 'lora_up': jax.random.normal(ks[3], (E, R, OUT), jnp.float32) * 0.02, 'lora_keys': jax.random.normal(ks[4], (E, K), jnp.float32), 'Wq': jax.random.normal(ks[5], (K, IN), jnp.float32) * 0.02}
    _L0_ffn_all = _L0_ffn_setup()
    _L0_ffn_in = {k: v for k, v in _L0_ffn_all.items() if k in ('W_org', 'lora_down', 'lora_up', 'lora_keys', 'Wq')}
    del _L0_ffn_all

    def _L1_xattn_setup():
        import jax, jax.numpy as jnp
        import numpy as np
        DIM = 1024
        NUM_HEADS = 32
        NUM_KV_HEADS = 8
        HEAD_DIM = DIM // NUM_HEADS
        KV_DIM = DIM // (NUM_HEADS // NUM_KV_HEADS)
        B, S = (1, 512)
        key = jax.random.key(seed)
        ks = jax.random.split(key, 7)
        w_scale = DIM ** (-0.5)
        return {'query': jax.random.normal(ks[0], (B, S, DIM), jnp.float32), 'key': jax.random.normal(ks[1], (B, S, DIM), jnp.float32), 'value': jax.random.normal(ks[2], (B, S, DIM), jnp.float32), 'Wq': jax.random.normal(ks[3], (DIM, DIM), jnp.float32) * w_scale, 'Wk': jax.random.normal(ks[4], (DIM, KV_DIM), jnp.float32) * w_scale, 'Wv': jax.random.normal(ks[5], (DIM, KV_DIM), jnp.float32) * w_scale, 'Wo': jax.random.normal(ks[6], (DIM, DIM), jnp.float32) * w_scale}
    _L1_xattn_all = _L1_xattn_setup()
    _L1_xattn_in = {k: v for k, v in _L1_xattn_all.items() if k in ('Wq', 'Wk', 'Wv', 'Wo')}
    del _L1_xattn_all

    def _L1_ffn_setup():
        import jax, jax.numpy as jnp
        import numpy as np
        B, S, D = (4, 512, 1024)
        NUM_EXPERTS, TOP_K = (3, 2)

        def _expert_outputs(h, w1, b1, w2, b2):
            pre = jnp.einsum('bsd,edf->ebsf', h, w1) + b1[:, None, None, :]
            act = jnp.stack([jnp.tanh(pre[0]), jax.nn.gelu(pre[1], approximate=False), jax.nn.silu(pre[2])])
            return jnp.einsum('ebsf,efd->ebsd', act, w2) + b2[:, None, None, :]
        key = jax.random.key(seed)
        ks = jax.random.split(key, 8)
        scale_in = 1.0 / np.sqrt(D)
        scale_gate = 1.0 / np.sqrt(D + 1)
        return {'h': jax.random.normal(ks[0], (B, S, D), dtype=jnp.float32), 'gate_w': jax.random.uniform(ks[1], (D + 1, NUM_EXPERTS), minval=-scale_gate, maxval=scale_gate, dtype=jnp.float32), 'gate_b': jnp.zeros((NUM_EXPERTS,), dtype=jnp.float32), 'w1': jax.random.uniform(ks[2], (NUM_EXPERTS, D, D), minval=-scale_in, maxval=scale_in, dtype=jnp.float32), 'b1': jnp.zeros((NUM_EXPERTS, D), dtype=jnp.float32), 'w2': jax.random.uniform(ks[3], (NUM_EXPERTS, D, D), minval=-scale_in, maxval=scale_in, dtype=jnp.float32), 'b2': jnp.zeros((NUM_EXPERTS, D), dtype=jnp.float32)}
    _L1_ffn_all = _L1_ffn_setup()
    _L1_ffn_in = {k: v for k, v in _L1_ffn_all.items() if k in ('gate_w', 'gate_b', 'w1', 'b1', 'w2', 'b2')}
    del _L1_ffn_all
    return {'x': x, 'ctx_4096': ctx_4096, 'g_xattn': g_xattn, 'g_ffn': g_ffn, 'L0_xattn_x1_scale': _L0_xattn_in['x1_scale'], 'L0_xattn_x1_zp': _L0_xattn_in['x1_zp'], 'L0_xattn_x2_scale': _L0_xattn_in['x2_scale'], 'L0_xattn_x2_zp': _L0_xattn_in['x2_zp'], 'L0_ffn_W_org': _L0_ffn_in['W_org'], 'L0_ffn_lora_down': _L0_ffn_in['lora_down'], 'L0_ffn_lora_up': _L0_ffn_in['lora_up'], 'L0_ffn_lora_keys': _L0_ffn_in['lora_keys'], 'L0_ffn_Wq': _L0_ffn_in['Wq'], 'L1_xattn_Wq': _L1_xattn_in['Wq'], 'L1_xattn_Wk': _L1_xattn_in['Wk'], 'L1_xattn_Wv': _L1_xattn_in['Wv'], 'L1_xattn_Wo': _L1_xattn_in['Wo'], 'L1_ffn_gate_w': _L1_ffn_in['gate_w'], 'L1_ffn_gate_b': _L1_ffn_in['gate_b'], 'L1_ffn_w1': _L1_ffn_in['w1'], 'L1_ffn_b1': _L1_ffn_in['b1'], 'L1_ffn_w2': _L1_ffn_in['w2'], 'L1_ffn_b2': _L1_ffn_in['b2']}

def reference(x, ctx_4096, g_xattn, g_ffn, L0_xattn_x1_scale, L0_xattn_x1_zp, L0_xattn_x2_scale, L0_xattn_x2_zp, L0_ffn_W_org, L0_ffn_lora_down, L0_ffn_lora_up, L0_ffn_lora_keys, L0_ffn_Wq, L1_xattn_Wq, L1_xattn_Wk, L1_xattn_Wv, L1_xattn_Wo, L1_ffn_gate_w, L1_ffn_gate_b, L1_ffn_w1, L1_ffn_b1, L1_ffn_w2, L1_ffn_b2):
    import jax
    import jax.numpy as jnp

    def _L0_xattn_ref(x1, x2, x1_scale, x1_zp, x2_scale, x2_zp):
        import jax, jax.numpy as jnp
        import numpy as np
        QMIN = 0.0
        QMAX = 255.0

        def fake_quant(x, scale, zp):
            s = scale.reshape(())
            z = zp.reshape(())
            q = jnp.clip(jnp.round(x / s + z), QMIN, QMAX)
            return (q - z) * s
        q1 = fake_quant(x1, x1_scale, x1_zp)
        q2 = fake_quant(x2, x2_scale, x2_zp)
        return jnp.matmul(q1, q2)

    def _L0_ffn_ref(x, W_org, lora_down, lora_up, lora_keys, Wq):
        import jax, jax.numpy as jnp
        import numpy as np
        import math
        B, S, IN, OUT = (4, 512, 1024, 1024)
        E, R, K = (8, 64, 128)
        SCALE = 64.0 / 64.0
        MULTIPLIER = 1.0
        base = jnp.einsum('bsi,oi->bso', x, W_org)
        q = jnp.einsum('bi,ki->bk', x.mean(axis=1), Wq)
        scores = jnp.einsum('bk,ek->be', q, lora_keys) / math.sqrt(K)
        coeffs = jax.nn.softmax(scores, axis=-1)
        h = jnp.einsum('bsi,eir->bser', x, lora_down)
        delta = jnp.einsum('be,bser,ero->bso', coeffs, h, lora_up)
        return base + delta * (SCALE * MULTIPLIER)

    def _L1_xattn_ref(query, key, value, Wq, Wk, Wv, Wo):
        import jax, jax.numpy as jnp
        import numpy as np
        DIM = 1024
        NUM_HEADS = 32
        NUM_KV_HEADS = 8
        HEAD_DIM = DIM // NUM_HEADS
        KV_DIM = DIM // (NUM_HEADS // NUM_KV_HEADS)
        B, S = (1, 512)
        b, sq, _ = query.shape
        _, sk, _ = key.shape
        rep = NUM_HEADS // NUM_KV_HEADS
        q = (query @ Wq).reshape(b, sq, NUM_HEADS, HEAD_DIM).transpose(0, 2, 1, 3)
        k = (key @ Wk).reshape(b, sk, NUM_KV_HEADS, HEAD_DIM).transpose(0, 2, 1, 3)
        v = (value @ Wv).reshape(b, sk, NUM_KV_HEADS, HEAD_DIM).transpose(0, 2, 1, 3)
        k = jnp.repeat(k, rep, axis=1)
        v = jnp.repeat(v, rep, axis=1)
        scale = HEAD_DIM ** (-0.5)
        scores = jnp.einsum('bhqd,bhkd->bhqk', q, k) * scale
        probs = jax.nn.softmax(scores, axis=-1)
        out = jnp.einsum('bhqk,bhkd->bhqd', probs, v)
        out = out.transpose(0, 2, 1, 3).reshape(b, sq, DIM)
        return out @ Wo

    def _L1_ffn_ref(h, gate_w, gate_b, w1, b1, w2, b2):
        import jax, jax.numpy as jnp
        import numpy as np
        B, S, D = (4, 512, 1024)
        NUM_EXPERTS, TOP_K = (3, 2)

        def _expert_outputs(h, w1, b1, w2, b2):
            pre = jnp.einsum('bsd,edf->ebsf', h, w1) + b1[:, None, None, :]
            act = jnp.stack([jnp.tanh(pre[0]), jax.nn.gelu(pre[1], approximate=False), jax.nn.silu(pre[2])])
            return jnp.einsum('ebsf,efd->ebsd', act, w2) + b2[:, None, None, :]
        b, s, d = h.shape
        vision_len = int(s * 0.3)
        text_strength = jnp.mean(jnp.abs(h[:, vision_len:, :]), axis=(1, 2), keepdims=True)
        vision_strength = jnp.mean(jnp.abs(h[:, :vision_len, :]), axis=(1, 2), keepdims=True)
        modality_ratio = text_strength / (vision_strength + 1e-08)
        modality_ratio = jnp.broadcast_to(modality_ratio, (b, s, 1))
        router_input = jnp.concatenate([h, modality_ratio], axis=-1)
        gate_logits = router_input @ gate_w + gate_b
        gate_scores = jax.nn.softmax(gate_logits, axis=-1)
        top_val, top_idx = jax.lax.top_k(gate_scores, TOP_K)
        top_val = top_val / (jnp.sum(top_val, axis=-1, keepdims=True) + 1e-08)
        expert_out = _expert_outputs(h, w1, b1, w2, b2)
        moe_out = jnp.zeros_like(h)
        batch_idx = jnp.arange(b)
        for i in range(TOP_K):
            j = top_idx[:, 0, i]
            out_i = expert_out[j, batch_idx]
            moe_out = moe_out + top_val[..., i:i + 1] * out_i
        return moe_out
    x = x + jnp.tanh(g_xattn[0]) * _L0_xattn_ref(_layernorm(x, axis=-1), ctx_4096, L0_xattn_x1_scale, L0_xattn_x1_zp, L0_xattn_x2_scale, L0_xattn_x2_zp)
    x = x + jnp.tanh(g_ffn[0]) * _L0_ffn_ref(_layernorm(x, axis=-1), L0_ffn_W_org, L0_ffn_lora_down, L0_ffn_lora_up, L0_ffn_lora_keys, L0_ffn_Wq)
    x = x + jnp.tanh(g_xattn[1]) * _L1_xattn_ref(_layernorm(x, axis=-1), ctx_4096, ctx_4096, L1_xattn_Wq, L1_xattn_Wk, L1_xattn_Wv, L1_xattn_Wo)
    x = x + jnp.tanh(g_ffn[1]) * _L1_ffn_ref(_layernorm(x, axis=-1), L1_ffn_gate_w, L1_ffn_gate_b, L1_ffn_w1, L1_ffn_b1, L1_ffn_w2, L1_ffn_b2)
    return x

_drawn_inputs = setup_inputs


def setup_inputs(seed=0):
    import zlib

    import numpy as np

    out = dict(_drawn_inputs(seed))
    spreads = {'g_ffn': (-1.0, 0.6),
     'L1_ffn_gate_b': (0.0, 0.8),
     'L1_ffn_b1': (0.0, 0.8),
     'L1_ffn_b2': (0.0, 2.0)}
    factors = {'L0_ffn_lora_down': 8.0,
     'L0_ffn_lora_up': 8.0,
     'L0_ffn_lora_keys': 8.0,
     'L0_ffn_Wq': 8.0,
     'L1_xattn_Wq': 6.585,
     'L1_xattn_Wk': 6.633,
     'L1_ffn_gate_w': 8.0,
     'L1_ffn_w1': 8.0,
     'L1_ffn_w2': 8.0}
    for name, (base, spread) in spreads.items():
        noise = np.random.default_rng([zlib.crc32(name.encode()), seed]).standard_normal(out[name].shape)
        drawn = base * np.exp(spread * noise) if base else spread * noise
        out[name] = jnp.asarray(drawn.astype(out[name].dtype))
    for name, factor in factors.items():
        out[name] = (out[name] * factor).astype(out[name].dtype)
    return out
```

```python
from contextlib import ExitStack

import numpy as np
import concourse.bass as bass
from concourse import mybir

F32 = mybir.dt.float32
BF16 = mybir.dt.bfloat16
I32 = mybir.dt.int32
ALU = mybir.AluOpType
ACT = mybir.ActivationFunctionType
AX = mybir.AxisListType

P = 128
B, S, D = 2, 512, 1024
SC = 1024
KT = D // P
TT = B * S // P
TB = S // P
HALF = 512
E_LORA, R_LORA, K_LORA = 8, 64, 128
ER = E_LORA * R_LORA
JT = ER // P
HEADS, KV_HEADS, HD = 32, 8, 32
REP = HEADS // KV_HEADS
KVD = KV_HEADS * HD
GROUPS = B * KV_HEADS
STEPS = REP * SC // P
EXPERTS, TOPK = 3, 2
VISION = int(S * 0.3)
MAGIC = 1.5 * 2.0 ** 23
MID = 128.0
QMAX = 255.0
EPS = 1e-5
WT_LAYOUT = [("kv", 4), ("down", 4), ("org", 8), ("up", 4), ("q", 8), ("o", 8)]
N_WT = sum(n for _, n in WT_LAYOUT)
WT_AT = {name: sum(n for _, n in WT_LAYOUT[:i]) for i, (name, _) in enumerate(WT_LAYOUT)}
SC_S1, SC_Z1, SC_S2, SC_Z2, SC_GX, SC_GF, SC_GB, SC_GL = 0, 1, 2, 3, 4, 6, 8, 11
N_SC = 14
RT_READ = 5 + 2 * B
RT_SHIFTED = RT_READ + 2


def ds(i, n):
    return bass.ds(i * n, n)


def per_tile(v):
    return v[:, :].rearrange("p (k n) -> p k n", k=KT)


def xt_tile(xt, t, i):
    return per_tile(xt)[:, 4 * i:4 * i + 4, ds(t, P)]


def build(nc, x, ctx_nat, ctx_t, wts, lora_q, lora_keys, scalars, gate_w, w1, b1, w2, b2, out):
    with ExitStack() as ctx:
        def sb(name, shape, dt):
            return ctx.enter_context(nc.sbuf_tensor(name, shape, dt))

        def sem(name):
            return ctx.enter_context(nc.semaphore(name))

        X = sb("X", [P, TT * D], F32)
        XTh = sb("XTh", [P, KT * TT * P], BF16)
        XTl = sb("XTl", [P, KT * TT * P], BF16)
        R = [sb(f"R{i}", [P, KT * D], BF16) for i in range(6)]
        V = sb("V", [P, B * KT * KVD], F32)
        stage_w = [sb(f"stage_w{i}", [P, D], F32) for i in range(2)]
        stage_c = [sb(f"stage_c{i}", [P, D], F32) for i in range(2)]
        xn = [sb(f"xn{i}", [P, D], F32) for i in range(2)]
        identf = sb("identf", [P, P], F32)
        identb = sb("identb", [P, P], BF16)
        onesf = sb("onesf", [P, P], F32)
        onesb = sb("onesb", [P, P], BF16)
        zero = sb("zero", [P, 1], F32)
        sc = sb("sc", [P, N_SC], F32)
        rs1 = sb("rs1", [P, 1], F32)
        rs2 = sb("rs2", [P, 1], F32)
        tg = sb("tg", [P, 4], F32)
        qc = sb("qc", [P, 8], F32)
        stats = [sb(f"stats{i}", [P, 2, 6], F32) for i in range(2)]
        mv = [sb(f"mv{i}", [P, 2], F32) for i in range(2)]
        lnv = [sb(f"lnv{i}", [P, 6], F32) for i in range(2)]
        carrier = sb("carrier", [P, 1], F32)
        rterm = sb("rterm", [P, TT], F32)
        msum = sb("msum", [P, 2, B * KT], F32)
        mean = sb("mean", [P, B, KT], F32)
        lq = sb("lq", [P, B], F32)
        keys = sb("keys", [P, E_LORA], F32)
        coef = sb("coef", [1, 4, B * E_LORA], F32)
        coefs = sb("coefs", [1, 8], F32)
        cvec = sb("cvec", [P, B * JT], F32)
        mxp = sb("mxp", [P, 2, TB, 2], F32)
        mxc = sb("mxc", [P, 2, TB], F32)
        nm = sb("nm", [P, 2, TB, 2], BF16)
        gwf = sb("gwf", [P, KT * EXPERTS], F32)
        gwh = sb("gwh", [P, KT * EXPERTS], BF16)
        gwl = sb("gwl", [P, KT * EXPERTS], BF16)
        b1t = sb("b1t", [P, EXPERTS * KT], F32)
        rowabs = sb("rowabs", [P, TT], F32)
        AM = sb("AM", [P, 2, TT], F32)
        AS = sb("AS", [P, 2, B], F32)
        rt = sb("rt", [P, 8], F32)
        rb = sb("rb", [P, B, EXPERTS], F32)
        L = sb("L", [P, TT, EXPERTS], F32)
        G = sb("G", [P, TT, EXPERTS], F32)
        rv = sb("rv", [P, 9, TT], F32)
        TV = sb("TV", [P, TOPK * TT], F32)
        rk = sb("rk", [1, 9, B], F32)
        idxf = sb("idxf", [1, B, TOPK], F32)
        idx = sb("idx", [1, B * TOPK], I32)

        half_r = KT * D // 2
        kv_h, kv_l = R[0][:, 0:half_r], R[0][:, half_r:]
        down_h, down_l = R[1][:, 0:half_r], R[1][:, half_r:]
        ct_h, ct_l = R[2], R[3]
        Q2 = [R[4], R[5]]
        XQ = XTl
        kb_h = xn[0][:, :].bitcast(BF16)
        kb_l = xn[1][:, :].bitcast(BF16)
        CB = V[:, KT * KVD:].rearrange("p (b n) -> p b n", b=B)
        org_h, org_l = R[2], R[3]
        up_h, up_l = R[0][:, 0:half_r], R[0][:, half_r:]
        HT_h, HT_l = R[4][:, 0:half_r], R[4][:, half_r:]
        LQW = R[5][:, 0:2 * KT * P].bitcast(F32)
        q_h, q_l = R[1], R[5]
        qb_h, qb_l = R[4][:, 0:half_r], R[4][:, half_r:]
        o_h, o_l = R[2], R[3]
        PB = [R[i // 2][:, :].bitcast(F32)[:, (i % 2) * REP * S:(i % 2 + 1) * REP * S] for i in range(4)]
        QS = [R[5][:, i * REP * S:(i + 1) * REP * S] for i in range(2)]
        KS = [R[5][:, 2 * REP * S + i * SC:2 * REP * S + (i + 1) * SC] for i in range(2)]
        at = 2 * REP * S + 2 * SC
        VS = [R[5][:, at + i * 2 * KT * HD:at + (i + 1) * 2 * KT * HD].bitcast(F32) for i in range(2)]
        rec, onat = xn[0][:, 0:S], xn[1][:, 0:S]
        w1_h, w1_l, w2_h, w2_l = R[0], R[1], R[2], R[3]
        hid = R[5][:, :].bitcast(F32)
        b2b = xn[0]
        eo = [xn[1][:, 0:HALF], xn[1][:, HALF:]]
        junk = R[0][:, 0:D]

        bank = [ctx.enter_context(nc.psum_tensor(f"bank{i}", [P, HALF], F32)) for i in range(8)]
        bank_b = [b[:, :].bitcast(BF16) for b in bank]

        k_scr = nc.dram_tensor("k_scr", [B, 2, KVD, SC], BF16, kind="Internal").ap()
        q_scr = nc.dram_tensor("q_scr", [KT, B, 2, P, S], BF16, kind="Internal").ap()

        const_in = sem("const_in")
        w_in = [sem(f"w_in{i}") for i in range(2)]
        c_in = [sem(f"c_in{i}") for i in range(2)]
        x_in = [sem(f"x_in{i}") for i in range(TT)]
        lqw_in = sem("lqw_in")
        wt_hi = sem("wt_hi")
        wt_done = sem("wt_done")
        made = sem("made")
        madeb = sem("madeb")
        qc_step = sem("qc_step")
        tg_done = sem("tg_done")
        c_act = sem("c_act")
        c_clip = sem("c_clip")
        c_done = sem("c_done")
        ln_step = sem("ln_step")
        ln_sd = sem("ln_sd")
        xn_done = sem("xn_done")
        xq_sc = sem("xq_sc")
        xq_clip = sem("xq_clip")
        xq_done = sem("xq_done")
        xq_turned = sem("xq_turned")
        xq_t = sem("xq_t")
        kv_mm = sem("kv_mm")
        k_hi = sem("k_hi")
        k_lo = sem("k_lo")
        v_act = sem("v_act")
        v_dve = sem("v_dve")
        k_out = sem("k_out")
        cs_mm = sem("cs_mm")
        cb_done = sem("cb_done")
        row_mm = sem("row_mm")
        rterm_done = sem("rterm_done")
        x_pre = sem("x_pre")
        nat_mm = sem("nat_mm")
        x_up = sem("x_up")
        turned = sem("turned")
        t_hi = sem("t_hi")
        t_lo = sem("t_lo")
        mean_step = sem("mean_step")
        lq_mm = sem("lq_mm")
        sc_mm = sem("sc_mm")
        bc_mm = sem("bc_mm")
        co_step = sem("co_step")
        co_exp = sem("co_exp")
        cv_done = sem("cv_done")
        h_mm = sem("h_mm")
        h_hi = sem("h_hi")
        h_lo = sem("h_lo")
        q_mm = sem("q_mm")
        q_hi = sem("q_hi")
        q_lo = sem("q_lo")
        q_out = [sem(f"q_out{i}") for i in range(4)]
        ones_row = sem("ones_row")
        qk_in = [sem(f"qk_in{i}") for i in range(2)]
        vs_done = sem("vs_done")
        s_mm = sem("s_mm")
        s_max = sem("s_max")
        nm_step = sem("nm_step")
        nm_turned = sem("nm_turned")
        nm_row = sem("nm_row")
        st_mm = sem("st_mm")
        exp_done = sem("exp_done")
        pv_mm = sem("pv_mm")
        o_step = sem("o_step")
        abs_done = sem("abs_done")
        lg_mm = sem("lg_mm")
        as_mm = sem("as_mm")
        am_done = sem("am_done")
        rt_step = sem("rt_step")
        rt_exp = sem("rt_exp")
        idx_done = sem("idx_done")
        a_mm = sem("a_mm")
        act_done = sem("act_done")
        e_hi = sem("e_hi")
        e_lo = sem("e_lo")
        b2_in = sem("b2_in")
        b_mm = sem("b_mm")
        eo_done = sem("eo_done")
        x_fin = sem("x_fin")
        x_out = sem("x_out")

        block = ctx.enter_context(nc.Block())
        N_CONST = 5
        W_O_END = N_WT

        @block.sync
        def _(sp):
            sp.dma_start(sc[:, :], scalars.to_broadcast([P, N_SC])).then_inc(const_in, 16)
            sp.dma_start(keys[:, :], lora_keys).then_inc(const_in, 16)
            sp.dma_start(gwf[:, :], gate_w).then_inc(const_in, 16)
            sp.dma_start(b1t[:, :], b1).then_inc(const_in, 16)

            def load_weights(first, count):
                for n in range(first, first + count):
                    if n >= 2:
                        sp.wait_ge(wt_done, n - 1)
                    sp.dma_start(stage_w[n % 2][:, :], wts[n]).then_inc(w_in[n % 2], 16)

            def load_context(n, src):
                if n >= 2:
                    sp.wait_ge(c_done, n - 1)
                sp.dma_start(stage_c[n % 2][:, :], src).then_inc(c_in[n % 2], 16)

            for k in range(KT):
                if k % 2 == 0:
                    load_weights(WT_AT["kv"] + k // 2, 1)
                load_context(k, ctx_t[0, k])
            for t in range(TT):
                sp.dma_start(X[:, t * D:(t + 1) * D], x[t]).then_inc(x_in[t], 16)
            for n in range(B * KT):
                load_context(KT + n, ctx_nat[n // KT, n % KT])
            load_weights(WT_AT["down"], 4)

            def keys_out(b):
                sp.wait_ge(k_lo, 4 * (b + 1))
                for part, src in enumerate((kb_h, kb_l)):
                    sp.dma_start(k_scr[b, part].rearrange("(c p) s -> p c s", c=2),
                                 src.rearrange("p (c s) -> p c s", c=2)).then_inc(k_out, 16)

            keys_out(0)
            for k in range(KT):
                load_context(3 * KT + k, ctx_t[1, k])
            sp.wait_ge(nat_mm, TT)
            sp.dma_start(LQW, lora_q).then_inc(lqw_in, 16)
            load_weights(WT_AT["org"], 2)
            keys_out(1)
            load_weights(WT_AT["org"] + 2, 6)
            load_weights(WT_AT["up"], 4)
            load_weights(WT_AT["q"], 8)

            def queries_out(b, c):
                sp.wait_ge(q_lo, KT * b + (c + 2))
                for part, src in enumerate((qb_h, qb_l)):
                    sp.dma_start(q_scr[c, bass.ds(b, 1), part].rearrange("o p s -> (o p) s"),
                                 src[:, (c % 4) * S:(c % 4 + 1) * S]).then_inc(q_out[c % 4], 16)

            with sp.Fori(0, B) as b:
                for c in range(KT):
                    queries_out(b, c)
            load_weights(WT_AT["o"], 8)

            for slot in range(4):
                sp.wait_ge(q_out[slot], 1 + 16 * 2 * B * KT // 4)
            sp.wait_ge(k_out, 16 * 2 * B)

            def group_in(kv, b):
                for row, part in ((0, 0), (32, 0), (64, 1)):
                    src = q_scr[bass.ds(kv, 1), b, part].rearrange("o p s -> (o p) s")
                    sp.dma_start(QS[b][row:row + HD, :].rearrange("p (h s) -> p h s", h=REP),
                                 src.rearrange("(h d) s -> d h s", h=REP)).then_inc(qk_in[b], 16)
                for row, part in ((0, 0), (32, 1), (64, 0)):
                    sp.dma_start(KS[b][row:row + HD, :],
                                 k_scr[b, part, ds(kv, HD), :]).then_inc(qk_in[b], 16)

            sp.wait_ge(q_mm, B * KT)
            group_in(0, 0)
            group_in(0, 1)
            with sp.Fori(1, KV_HEADS) as kv:
                for b in range(B):
                    sp.wait_ge(st_mm, STEPS * (2 * kv + b - 1))
                    group_in(kv, b)

            sp.wait_ge(idx_done, 1)
            reg = sp.alloc_register("expert_sp")
            with sp.Fori(0, B * TOPK) as s:
                sp.reg_load(reg, idx[0:1, bass.ds(s, 1)])
                e = sp.snap(reg, min_val=0, max_val=EXPERTS - 1)
                for c in range(KT):
                    n = W_O_END + 2 * KT * s + c
                    sp.wait_ge(wt_done, n - 1)
                    sp.dma_start(stage_w[c % 2][:, :], w1[bass.ds(e, 1), c].rearrange("o p n -> (o p) n")).then_inc(w_in[c % 2], 16)
                sp.wait_ge(eo_done, 2 * TB * s + 1)
                sp.dma_start(b2b[:, :], b2[bass.ds(e, 1), :].to_broadcast([P, D])).then_inc(b2_in, 16)
                for c in range(KT):
                    n = W_O_END + 2 * KT * s + KT + c
                    sp.wait_ge(wt_done, n - 1)
                    sp.dma_start(stage_w[c % 2][:, :], w2[bass.ds(e, 1), c].rearrange("o p n -> (o p) n")).then_inc(w_in[c % 2], 16)
            sp.wait_ge(x_out, 16 * TT)

        @block.gpsimd
        def _(pool):
            pool.memset(zero[:, :], 0.0).then_inc(made, 1)
            pool.memset(identf[:, :], 0.0).then_inc(made, 1)
            pool.memset(onesf[:, :], 1.0).then_inc(made, 1)
            pool.wait_ge(made, 3)
            pool.affine_select(out=identf[:, :], in_=identf[:, :], compare_op=ALU.not_equal, fill=1.0, base=0,
                               pattern=[[-1, P]], channel_multiplier=1).then_inc(made, 1)

            def split(n, stage, hi, lo):
                pool.wait_ge(w_in[stage], 16 * ((n - stage) // 2 + 1) if isinstance(n, int) else 8 * n - 8 * stage + 16)
                pool.tensor_tensor(hi, stage_w[stage][:, :], zero[:, :].to_broadcast([P, D]), ALU.add).then_inc(wt_hi, 1)
                pool.wait_ge(wt_hi, n + 1)
                pool.tensor_tensor(lo, stage_w[stage][:, :], hi, ALU.subtract).then_inc(wt_done, 1)

            def split_group(name, hi, lo):
                first, count = WT_AT[name], dict(WT_LAYOUT)[name]
                with pool.Fori(0, count // 2) as i:
                    for j in range(2):
                        at_col = bass.ds(i * (2 * D) + j * D, D)
                        split(first + 2 * i + j, j, hi[:, at_col], lo[:, at_col])

            split_group("kv", kv_h, kv_l)
            split_group("down", down_h, down_l)
            pool.wait_ge(kv_mm, 2)
            split_group("org", org_h, org_l)
            split_group("up", up_h, up_l)
            pool.wait_ge(h_mm, B * JT)
            pool.wait_ge(lq_mm, 1)
            split_group("q", q_h, q_l)
            pool.wait_ge(nat_mm, 2 * TT)
            split_group("o", o_h, o_l)

            def stage_values(kv, b, g):
                if not isinstance(g, int) or g >= 2:
                    pool.wait_ge(pv_mm, KT * g + (1 - KT))
                src = V[:, b * KT * KVD:(b + 1) * KT * KVD].rearrange("p (t n) -> p t n", t=KT)
                pool.tensor_copy(VS[b].rearrange("p (t n) -> p t n", t=KT), src[:, :, ds(kv, HD)]).then_inc(vs_done, 1)

            pool.wait_ge(q_mm, B * KT)
            stage_values(0, 0, 0)
            stage_values(0, 1, 1)
            with pool.Fori(1, KV_HEADS) as kv:
                for b in range(B):
                    stage_values(kv, b, 2 * kv + b)

            pool.wait_ge(idx_done, 1)
            with pool.Fori(0, B * TOPK) as s:
                pool.wait_ge(a_mm, KT * s + 1)
                for c in range(KT):
                    cols = slice(c * D, (c + 1) * D)
                    split(W_O_END + 2 * KT * s + c, c % 2, w1_h[:, cols], w1_l[:, cols])
                pool.wait_ge(b_mm, TB * s + 1)
                for c in range(KT):
                    cols = slice(c * D, (c + 1) * D)
                    split(W_O_END + 2 * KT * s + KT + c, c % 2, w2_h[:, cols], w2_l[:, cols])

        @block.tensor
        def _(pe):
            for counted in (pv_mm, a_mm, b_mm):
                pe.sem_inc(counted, 1)
            pe.wait_ge(madeb, 2)

            def triple(outs, ah, al, bh, bl, first, last):
                for a, bs in ((ah, bh), (ah, bl), (al, bh)):
                    for o, m in zip(outs, bs):
                        mm = pe.matmul(o, a, m, start=first and a is ah and bs is bh,
                                       stop=last and a is al)
                return mm

            def kv_tile(k, first):
                def c(t, n0, n):
                    return t[:, bass.ds(k * D + n0, n)] if not isinstance(k, int) else t[:, k * D + n0:k * D + n0 + n]

                def w(t, n0, n):
                    return t[:, bass.ds(k * HALF + n0, n)] if not isinstance(k, int) else t[:, k * HALF + n0:k * HALF + n0 + n]

                for m in range(2):
                    for a, r in ((kv_h, ct_h), (kv_h, ct_l), (kv_l, ct_h)):
                        for h in range(2):
                            mm = pe.matmul(bank[2 * m + h][:, :], w(a, m * P, P), c(r, h * HALF, HALF),
                                           start=first and a is kv_h and r is ct_h, stop=False, skip_group_check=True)
                for t in range(KT):
                    for a, r in ((ct_h, kv_h), (ct_h, kv_l), (ct_l, kv_h)):
                        mm = pe.matmul(bank[4 + t // 2][:, (t % 2) * KVD:(t % 2 + 1) * KVD], c(a, t * P, P),
                                       w(r, KVD, KVD), start=first and t % 2 == 0 and a is ct_h and r is kv_h,
                                       stop=False, skip_group_check=True)
                return mm

            def keys_values(b):
                at_c = (0, 3 * KT)[b]
                pe.wait_ge(wt_done, 1)
                pe.wait_ge(c_done, at_c + 1)
                kv_tile(0, True)
                pe.wait_ge(c_done, at_c + 2)
                kv_tile(1, False)
                with pe.Fori(1, KT // 2 - 1) as c:
                    pe.wait_ge(wt_done, c + 1)
                    for j in range(2):
                        pe.wait_ge(c_done, at_c + 2 * c + j + 1)
                        kv_tile(2 * c + j, False)
                pe.wait_ge(wt_done, KT // 2)
                for k in (KT - 2, KT - 1):
                    pe.wait_ge(c_done, at_c + k + 1)
                    mm = kv_tile(k, False)
                mm.then_inc(kv_mm, 1)

            keys_values(0)

            for t in range(TT):
                pe.wait_ge(xq_done, t + 1)
                if t < 2:
                    pe.wait_ge(v_dve, 2)
                else:
                    pe.wait_ge(xq_t, t - 1)
                for k in range(KT):
                    mm = pe.transpose(bank_b[6 + t % 2][:, k * P:(k + 1) * P], XQ[:, t * D + k * P:t * D + (k + 1) * P],
                                      identb[:, :])
                mm.then_inc(xq_turned, 1)
            pe.wait_ge(k_lo, 4)
            pe.wait_ge(xq_t, TT)
            for t in range(TT):
                for k in range(KT):
                    mm = pe.matmul(bank[3][:, t:t + 1], XTh[:, k * D + t * P:k * D + (t + 1) * P], onesb[:, 0:1],
                                   start=k == 0, stop=k == KT - 1)
            mm.then_inc(row_mm, 1)
            pe.wait_ge(v_act, 2)
            for b in range(B):
                pe.wait_ge(c_done, KT * (2 + b))
                for h in range(2):
                    for k in range(KT):
                        mm = pe.matmul(bank[4 + 2 * b + h][:, :], onesb[:, :],
                                       Q2[b][:, k * D + h * HALF:k * D + (h + 1) * HALF], start=k == 0, stop=k == KT - 1)
                mm.then_inc(cs_mm, 1)

            def pair(m):
                return bank[2 * (m % 2)], bank[2 * (m % 2) + 1]

            def turn_behind(n, par):
                pe.wait_ge(xn_done, TT + n + 1)
                pe.wait_ge(t_lo, 2 * n)
                for k in range(KT):
                    mm = pe.transpose(bank[4 + k // 4][:, (k % 4) * P:(k % 4 + 1) * P], xn[par][:, k * P:(k + 1) * P],
                                      identf[:, :])
                mm.then_inc(turned, 1)

            pe.wait_ge(rterm_done, 1)
            pe.wait_ge(cb_done, 4)
            for t in range(TT):
                if t >= 2:
                    pe.wait_ge(x_up, 2 * (t - 1))
                for h in range(2):
                    for k in range(KT):
                        mm = pe.matmul(pair(t)[h][:, :], XTh[:, k * D + t * P:k * D + (t + 1) * P],
                                       Q2[t // TB][:, k * D + h * HALF:k * D + (h + 1) * HALF],
                                       start=k == 0, stop=k == KT - 1)
                mm.then_inc(nat_mm, 1)
                if t >= 1:
                    turn_behind(t - 1, (t - 1) % 2)
            turn_behind(TT - 1, (TT - 1) % 2)

            pe.wait_ge(x_up, 2 * TT)
            pe.wait_ge(t_lo, 2 * TT)
            keys_values(1)

            pe.wait_ge(k_lo, 8)
            pe.wait_ge(v_act, 4)
            pe.wait_ge(v_dve, 4)
            pe.wait_ge(lqw_in, 16)
            pe.wait_ge(mean_step, 2 * B + 2)
            for k in range(KT):
                mm = pe.matmul(bank[4][:, 0:B], LQW[:, k * P:(k + 1) * P], mean[:, :, k], start=k == 0, stop=k == KT - 1)
            mm.then_inc(lq_mm, 1)

            def lora_hidden(u):
                b, j = divmod(u, JT)
                if u >= 4:
                    pe.wait_ge(h_lo, u - 3)
                for k in range(KT):
                    mm = triple([bank[u % 4][:, :]], down_h[:, k * ER + j * P:k * ER + (j + 1) * P],
                                down_l[:, k * ER + j * P:k * ER + (j + 1) * P],
                                [XTh[:, k * D + b * S:k * D + (b + 1) * S]], [XTl[:, k * D + b * S:k * D + (b + 1) * S]],
                                k == 0, k == KT - 1)
                mm.then_inc(h_mm, 1)

            pe.wait_ge(wt_done, WT_AT["org"])
            lora_hidden(0)
            pe.wait_ge(co_step, 1)
            for b in range(B):
                mm = pe.matmul(bank[5][0:1, b * E_LORA:(b + 1) * E_LORA], lq[:, b:b + 1], keys[:, :], start=True, stop=True)
            mm.then_inc(sc_mm, 1)
            lora_hidden(1)
            pe.wait_ge(co_step, 6)
            pe.matmul(bank[6][:, 0:B * E_LORA], onesf[0:1, :], coef[0:1, 3, :], start=True, stop=True).then_inc(bc_mm, 1)
            for u in range(2, B * JT):
                lora_hidden(u)

            def token_tile(m, t, par, w_h, w_l, lora):
                pe.wait_ge(x_up, 2 * (m - 1))
                outs = [bank[2 * par][:, :], bank[2 * par + 1][:, :]]
                for k in range(KT):
                    cols = bass.ds(k * D + t * P, P)
                    mm = triple(outs, XTh[:, cols], XTl[:, cols],
                                [w_h[:, k * D + h * HALF:k * D + (h + 1) * HALF] for h in range(2)],
                                [w_l[:, k * D + h * HALF:k * D + (h + 1) * HALF] for h in range(2)],
                                k == 0, k == KT - 1 and not lora)
                if lora:
                    for j in range(JT):
                        cols = bass.ds(j * D + t * P, P)
                        mm = triple(outs, HT_h[:, cols], HT_l[:, cols],
                                    [up_h[:, j * D + h * HALF:j * D + (h + 1) * HALF] for h in range(2)],
                                    [up_l[:, j * D + h * HALF:j * D + (h + 1) * HALF] for h in range(2)],
                                    False, j == JT - 1)
                mm.then_inc(nat_mm, 1)

            def token_phase(m0, w_h, w_l, lora):
                token_tile(m0, 0, 0, w_h, w_l, lora)
                with pe.Fori(0, TT // 2 - 1) as i:
                    token_tile(2 * i + (m0 + 1), 2 * i + 1, 1, w_h, w_l, lora)
                    turn_behind(2 * i + m0, 0)
                    token_tile(2 * i + (m0 + 2), 2 * i + 2, 0, w_h, w_l, lora)
                    turn_behind(2 * i + (m0 + 1), 1)
                token_tile(m0 + TT - 1, TT - 1, 1, w_h, w_l, lora)
                turn_behind(m0 + TT - 2, 0)
                turn_behind(m0 + TT - 1, 1)

            pe.wait_ge(h_lo, B * JT)
            pe.wait_ge(wt_done, WT_AT["q"])
            token_phase(TT, org_h, org_l, True)

            pe.wait_ge(wt_done, WT_AT["o"])
            pe.wait_ge(x_up, 4 * TT)
            pe.wait_ge(t_lo, 4 * TT)
            with pe.Fori(0, B) as b:
                for c in range(KT):
                    pe.wait_ge(q_lo, KT * b + (1 + max(c - 3, 0)))
                    for k in range(KT):
                        w, r = slice(k * D + c * P, k * D + (c + 1) * P), bass.ds(b * S + k * D, S)
                        mm = triple([bank[c % 4][:, :]], q_h[:, w], q_l[:, w], [XTh[:, r]], [XTl[:, r]],
                                    k == 0, k == KT - 1)
                    mm.then_inc(q_mm, 1)

            def score_step(g, par, n):
                h, qt, kh = n // 8, n // 2 % 4, n % 2
                if not isinstance(g, int) or g > 0 or n >= 2:
                    pe.wait_ge(s_max, STEPS * g + (n - 1))
                pe.matmul(bank[n % 2][:, :], QS[par][0:96, h * S + qt * P:h * S + (qt + 1) * P],
                          KS[par][0:96, kh * HALF:(kh + 1) * HALF], start=True, stop=True).then_inc(s_mm, 1)

            def max_row(g, par, h):
                pe.wait_ge(nm_step, 3 * (REP * g + (h + 1)))
                if not isinstance(g, int) or g > 0 or h > 0:
                    pe.wait_ge(nm_row, REP * g + h)
                for qt in range(TB):
                    mm = pe.transpose(bank_b[4][96:98, qt * P:(qt + 1) * P], nm[:, h % 2, qt, :], identb[:, :])
                mm.then_inc(nm_turned, 1)

            def weigh(g, par, kt):
                pe.wait_ge(exp_done, STEPS * g + (4 * kt + 4))
                if kt == 0:
                    pe.wait_ge(vs_done, g + 1)
                    if isinstance(g, int) and g == GROUPS - 1:
                        pe.wait_ge(o_step, 4 * g)
                for bk, a in ((5, VS[par][:, kt * HD:(kt + 1) * HD]), (6, onesf[:, 0:HD])):
                    for h in range(REP):
                        mm = pe.matmul(bank[bk][h * HD:(h + 1) * HD, :], a, PB[kt % 4][:, h * S:(h + 1) * S],
                                       start=kt == 0, stop=kt == KT - 1)
                mm.then_inc(pv_mm, 1)

            def group(g, par, scores_of_next):
                nxt, npar = g + 1, 1 - par
                for t in range(STEPS):
                    kt, h = divmod(t, REP)
                    if scores_of_next:
                        if t == 0:
                            loaded(nxt, npar)
                        for n in ((2 * t, 2 * t + 1) if t < 4 else (t + 4,) if t < STEPS - 4 else ()):
                            score_step(nxt, npar, n)
                    if t < REP:
                        pe.wait_ge(nm_row, REP * g + (t + 1))
                    if t >= 2:
                        pe.wait_ge(exp_done, STEPS * g + (t - 1))
                    pe.matmul(bank[2 + t % 2][:, :], KS[par][0:98, kt * P:(kt + 1) * P],
                              QS[par][0:98, h * S:(h + 1) * S], start=True, stop=True).then_inc(st_mm, 1)
                    if scores_of_next and t % 8 == 6:
                        max_row(nxt, npar, t // 8)
                    if t >= 5 and t % 4 == 1:
                        weigh(g, par, t // 4 - 1)
                weigh(g, par, KT - 1)

            def loaded(g, par):
                pe.wait_ge(qk_in[par], 96 * (g // 2 + 1) if isinstance(g, int) else 48 * g + (96 - 48 * par))

            pe.wait_ge(q_lo, 1 + B * KT)
            pe.wait_ge(ones_row, 2)
            loaded(0, 0)
            for h in range(REP):
                for n in range(8 * h, 8 * h + 8):
                    score_step(0, 0, n)
                max_row(0, 0, h)
            with pe.Fori(0, GROUPS // 2 - 1) as i:
                group(2 * i, 0, True)
                group(2 * i + 1, 1, True)
            group(GROUPS - 2, 0, True)
            group(GROUPS - 1, 1, False)

            pe.wait_ge(o_step, 4 * GROUPS)
            pe.wait_ge(wt_done, N_WT)
            token_phase(2 * TT, o_h, o_l, False)

            pe.wait_ge(x_up, 6 * TT)
            pe.wait_ge(t_lo, 6 * TT)
            pe.wait_ge(am_done, 4)
            pe.matmul(bank[1][:, 0:2 * TT], onesf[:, :], AM[:, :, :].rearrange("p a t -> p (a t)"), start=True,
                      stop=True).then_inc(as_mm, 1)
            for t in range(TT):
                for k in range(KT):
                    cols = slice(k * D + t * P, k * D + (t + 1) * P)
                    e3 = slice(k * EXPERTS, (k + 1) * EXPERTS)
                    mm = triple([bank[0][:, t * EXPERTS:(t + 1) * EXPERTS]], XTh[:, cols], XTl[:, cols],
                                [gwh[:, e3]], [gwl[:, e3]], k == 0, k == KT - 1)
            mm.then_inc(lg_mm, 1)
            pe.wait_ge(rt_step, RT_READ)

            with pe.Fori(0, B) as b:
                with pe.Fori(0, TOPK) as j:
                    s = b * TOPK + j
                    for f in range(KT):
                        pe.wait_ge(act_done, KT * s + (1 + max(f - 3, 0)))
                        for k in range(KT):
                            if f == 0:
                                pe.wait_ge(wt_done, W_O_END + 2 * KT * s + (k + 1))
                            cols = bass.ds(b * S + k * D, S)
                            w = slice(k * D + f * P, k * D + (f + 1) * P)
                            mm = triple([bank[f % 4][:, :]], w1_h[:, w], w1_l[:, w], [XTh[:, cols]], [XTl[:, cols]],
                                        k == 0, k == KT - 1)
                        mm.then_inc(a_mm, 1)
                    for i in range(TB):
                        pe.wait_ge(eo_done, 2 * TB * s + (1 + 2 * max(i - 1, 0)))
                        outs = [bank[4 + 2 * (i % 2)][:, :], bank[5 + 2 * (i % 2)][:, :]]
                        for f in range(KT):
                            if i == 0:
                                pe.wait_ge(e_lo, KT * s + (f + 2))
                                pe.wait_ge(wt_done, W_O_END + 2 * KT * s + (KT + f + 1))
                            cols = slice(f * S + i * P, f * S + (i + 1) * P)
                            mm = triple(outs, HT_h[:, cols], HT_l[:, cols],
                                        [w2_h[:, f * D + h * HALF:f * D + (h + 1) * HALF] for h in range(2)],
                                        [w2_l[:, f * D + h * HALF:f * D + (h + 1) * HALF] for h in range(2)],
                                        f == 0, f == KT - 1)
                        mm.then_inc(b_mm, 1)

        @block.scalar
        def _(act):
            for counted in (abs_done, act_done, *q_out):
                act.sem_inc(counted, 1)
            act.wait_ge(const_in, 64)
            act.activation(tg[:, :], sc[:, SC_GX:SC_GX + 4], ACT.Tanh).then_inc(tg_done, 1)

            def chunk_hi(n, k):
                act.wait_ge(c_in[n % 2], 16 * (n // 2 + 1))
                act.activation(ct_h[:, k * D:(k + 1) * D], stage_c[n % 2][:, :], ACT.Copy).then_inc(c_act, 1)

            for k in range(KT):
                chunk_hi(k, k)
            act.wait_ge(qc_step, 2)

            def root(n, par):
                act.wait_ge(ln_step, 8 * n + 4)
                act.activation(lnv[par][:, 1:2], lnv[par][:, 0:1], ACT.Sqrt).then_inc(ln_sd, 1)

            for t in range(TT):
                root(t, t % 2)
                act.wait_ge(xn_done, t + 1)
                act.activation(xn[t % 2][:, :], xn[t % 2][:, :], ACT.Identity, bias=sc[:, SC_Z1:SC_Z1 + 1],
                               scale=rs1[:, 0:1]).then_inc(xq_sc, 1)

            def kv_out(b):
                act.wait_ge(kv_mm, b + 1)
                for i in range(4):
                    act.activation(kb_h[:, i * HALF:(i + 1) * HALF], bank[i][:, :], ACT.Copy).then_inc(k_hi, 1)
                for i in range(2):
                    at_v = b * KT * KVD + i * HALF
                    act.activation(V[:, at_v:at_v + HALF], bank[4 + i][:, :], ACT.Copy).then_inc(v_act, 1)

            act.wait_ge(xq_done, TT)
            kv_out(0)
            for t in range(TT):
                act.wait_ge(xq_turned, t + 1)
                act.activation(XTh[:, :].rearrange("p (k n) -> p k n", k=KT)[:, :, t * P:(t + 1) * P],
                               bank_b[6 + t % 2].rearrange("p (k n) -> p k n", k=KT), ACT.Copy).then_inc(xq_t, 1)
            for n in range(KT, 3 * KT):
                act.wait_ge(c_in[n % 2], 16 * (n // 2 + 1))
                act.activation(stage_c[n % 2][:, :], stage_c[n % 2][:, :], ACT.Identity, bias=sc[:, SC_Z2:SC_Z2 + 1],
                               scale=rs2[:, 0:1]).then_inc(c_act, 1)
            act.wait_ge(kv_mm, 1)
            for k in range(KT):
                chunk_hi(3 * KT + k, k)

            def normalise(n, t, par, sums):
                root(n + TT, par)
                if sums:
                    act.wait_ge(xn_done, TT + n + 1)
                    act.wait_ge(abs_done, t + 1)
                    act.activation(junk, xn[par][:, :], ACT.Abs, accum_out=rowabs[:, bass.ds(t, 1)]).then_inc(abs_done, 1)
                act.wait_ge(turned, n + 1)
                for i in range(2):
                    act.activation(xt_tile(XTh, t, i), bank[4 + i][:, :].rearrange("p (k n) -> p k n", k=4),
                                   ACT.Copy).then_inc(t_hi, 1)

            def normalise_all(n0, sums):
                with act.Fori(0, TT // 2) as i:
                    for j in range(2):
                        normalise(2 * i + (n0 + j), 2 * i + j, j, sums)

            normalise_all(0, False)
            kv_out(1)

            act.wait_ge(co_step, 3)
            act.activation(coef[0:1, 1, :], coef[0:1, 2, :], ACT.Exp, scale=float(K_LORA) ** -0.5).then_inc(co_exp, 1)
            act.wait_ge(cv_done, 2)
            for u in range(B * JT):
                b, j = divmod(u, JT)
                act.wait_ge(h_mm, u + 1)
                act.activation(HT_h[:, j * D + b * S:j * D + (b + 1) * S], bank[u % 4][:, :], ACT.Copy,
                               scale=cvec[:, u:u + 1]).then_inc(h_hi, 1)
            normalise_all(TT, False)

            act.wait_ge(nat_mm, 2 * TT)
            with act.Fori(0, B) as b:
                for c in range(KT):
                    act.wait_ge(q_mm, KT * b + (c + 1))
                    act.wait_ge(q_out[c % 4], 64 * b + (1 + 32 * (c // 4)))
                    act.activation(qb_h[:, (c % 4) * S:(c % 4 + 1) * S], bank[c % 4][:, :], ACT.Copy).then_inc(q_hi, 1)

            def row_out(g, par, h):
                act.wait_ge(nm_turned, REP * g + (h + 1))
                act.activation(QS[par][96:98, h * S:(h + 1) * S], bank_b[4][96:98, 0:S], ACT.Copy).then_inc(nm_row, 1)

            def exp_group(g, par, nxt):
                for t in range(STEPS):
                    kt, h = divmod(t, REP)
                    act.wait_ge(st_mm, STEPS * g + (t + 1))
                    if h == 0:
                        act.wait_ge(pv_mm, KT * g + (1 + max(kt - 3, 0)))
                    act.activation(PB[kt % 4][:, h * S:(h + 1) * S], bank[2 + t % 2][:, :], ACT.Exp,
                                   scale=float(HD) ** -0.5).then_inc(exp_done, 1)
                    if nxt and t % 8 == 6:
                        row_out(g + 1, 1 - par, t // 8)

            act.wait_ge(q_mm, B * KT)
            for h in range(REP):
                row_out(0, 0, h)
            act.wait_ge(nat_mm, 2 * TT)
            with act.Fori(0, GROUPS // 2 - 1) as i:
                exp_group(2 * i, 0, True)
                exp_group(2 * i + 1, 1, True)
            exp_group(GROUPS - 2, 0, True)
            exp_group(GROUPS - 1, 1, False)

            act.wait_ge(pv_mm, 1 + KT * GROUPS)
            normalise_all(2 * TT, True)

            act.wait_ge(rt_step, RT_SHIFTED)
            act.activation(G[:, :, :], L[:, :, :], ACT.Exp).then_inc(rt_exp, 1)

            act.wait_ge(idx_done, 1)
            reg = act.alloc_register("expert_act")
            with act.Fori(0, B) as b:
                with act.Fori(0, TOPK) as j:
                    s = b * TOPK + j
                    act.reg_load(reg, idx[0:1, bass.ds(s, 1)])
                    for e, func in enumerate((ACT.Tanh, ACT.Gelu, ACT.Silu)):
                        with act.If_eq(reg, e):
                            for f in range(KT):
                                act.wait_ge(a_mm, KT * s + (f + 2))
                                act.wait_ge(e_lo, KT * s + 1)
                                act.activation(hid[:, f * S:(f + 1) * S], bank[f % 4][:, :], func,
                                               bias=b1t[:, e * KT + f:e * KT + f + 1]).then_inc(act_done, 1)
                for i in range(TB):
                    act.wait_ge(x_fin, 4 * TB * b + (2 * TB + 2 * (i + 1) + 1))
                    t = b * TB + i
                    act.dma_start(out[bass.ds(t, 1)].rearrange("o p n -> (o p) n"), X[:, ds(t, D)]).then_inc(x_out, 16)

        @block.vector
        def _(dve):
            for counted in (q_lo, eo_done, e_lo, x_fin):
                dve.sem_inc(counted, 1)
            dve.wait_ge(made, 4)
            dve.tensor_copy(identb[:, :], identf[:, :]).then_inc(madeb, 1)
            dve.tensor_copy(onesb[:, :], onesf[:, :]).then_inc(madeb, 1)
            dve.wait_ge(const_in, 64)
            dve.reciprocal(rs1[:, :], sc[:, SC_S1:SC_S1 + 1]).then_inc(qc_step, 1)
            dve.reciprocal(rs2[:, :], sc[:, SC_S2:SC_S2 + 1]).then_inc(qc_step, 1)
            dve.tensor_copy(gwh[:, :], gwf[:, :]).then_inc(qc_step, 1)
            dve.wait_ge(qc_step, 3)
            dve.tensor_tensor(gwl[:, :], gwf[:, :], gwh[:, :], ALU.subtract).then_inc(qc_step, 1)
            dve.wait_ge(tg_done, 1)
            dve.tensor_tensor(qc[:, 0:1], sc[:, SC_S1:SC_S1 + 1], sc[:, SC_S2:SC_S2 + 1], ALU.mult).then_inc(qc_step, 1)
            dve.tensor_scalar(qc[:, 1:2], sc[:, SC_Z1:SC_Z1 + 1], -1.0, MID, ALU.mult, ALU.add).then_inc(qc_step, 1)
            dve.tensor_scalar(qc[:, 2:3], sc[:, SC_Z2:SC_Z2 + 1], -1.0, MID, ALU.mult, ALU.add).then_inc(qc_step, 1)
            dve.wait_ge(qc_step, 7)
            dve.tensor_scalar(qc[:, 6:7], qc[:, 0:1], tg[:, 0:1], None, ALU.mult).then_inc(qc_step, 1)
            dve.tensor_scalar(qc[:, 5:6], qc[:, 1:2], float(D), None, ALU.mult).then_inc(qc_step, 1)
            dve.wait_ge(qc_step, 9)
            dve.tensor_tensor(qc[:, 3:4], qc[:, 6:7], qc[:, 1:2], ALU.mult).then_inc(qc_step, 1)
            dve.tensor_tensor(qc[:, 4:5], qc[:, 6:7], qc[:, 2:3], ALU.mult).then_inc(qc_step, 1)

            def chunk_lo(n, k):
                dve.wait_ge(c_act, n + 1)
                cols = slice(k * D, (k + 1) * D)
                dve.tensor_tensor(ct_l[:, cols], stage_c[n % 2][:, :], ct_h[:, cols], ALU.subtract).then_inc(c_done, 1)

            for k in range(KT):
                chunk_lo(k, k)

            def carry_wait():
                dve.memset(carrier[:, :], 0.0)

            def normalise(n, xt, par, free):
                v = lnv[par]
                carry_wait()
                for h in range(2):
                    dve.bn_stats(stats[par][:, h, :], xt(h)).then_inc(ln_step, 1)
                dve.wait_ge(ln_step, 8 * n + 2)
                carry_wait()
                dve.bn_aggr(mv[par][:, :], stats[par][:, :, :]).then_inc(ln_step, 1)
                dve.wait_ge(ln_step, 8 * n + 3)
                dve.tensor_scalar(v[:, 0:1], mv[par][:, 1:2], EPS, None, ALU.add).then_inc(ln_step, 1)
                dve.wait_ge(ln_sd, n + 1)
                dve.reciprocal(v[:, 2:3], v[:, 1:2]).then_inc(ln_step, 1)
                dve.wait_ge(ln_step, 8 * n + 5)
                dve.scalar_tensor_tensor(out=v[:, 3:4], in0=v[:, 2:3], scalar=v[:, 2:3], in1=v[:, 0:1],
                                         op0=ALU.mult, op1=ALU.mult).then_inc(ln_step, 1)
                dve.wait_ge(ln_step, 8 * n + 6)
                dve.tensor_scalar(v[:, 4:5], v[:, 3:4], -0.5, 1.5, ALU.mult, ALU.add).then_inc(ln_step, 1)
                dve.wait_ge(ln_step, 8 * n + 7)
                dve.tensor_tensor(v[:, 5:6], v[:, 4:5], v[:, 2:3], ALU.mult).then_inc(ln_step, 1)
                dve.wait_ge(ln_step, 8 * n + 8)
                free()
                dve.tensor_scalar(xn[par][:, :], xt(None), mv[par][:, 0:1], v[:, 5:6], ALU.subtract,
                                  ALU.mult).then_inc(xn_done, 1)

            def clip_round(buf, dst, clip, n, done):
                dve.tensor_scalar(buf, buf, 0.0, QMAX, ALU.max, ALU.min).then_inc(clip, 1)
                dve.wait_ge(clip, n + 1)
                dve.tensor_scalar(dst, buf, MAGIC, MAGIC + MID, ALU.add, ALU.subtract).then_inc(done, 1)

            for t in range(TT):
                dve.wait_ge(x_in[t], 16)
                normalise(t, lambda h, t=t: X[:, t * D + (h or 0) * HALF:t * D + ((h or 0) + 1) * HALF] if h is not None
                          else X[:, t * D:(t + 1) * D], t % 2, lambda t=t: dve.wait_ge(xq_done, t - 1) if t >= 2 else None)
                dve.wait_ge(xq_sc, t + 1)
                clip_round(xn[t % 2][:, :], XQ[:, t * D:(t + 1) * D], xq_clip, t, xq_done)

            def kv_out(b):
                for i in range(2):
                    dve.wait_ge(kv_mm, b + 1)
                    at_v = b * KT * KVD + (2 + i) * HALF
                    dve.tensor_copy(V[:, at_v:at_v + HALF], bank[6 + i][:, :]).then_inc(v_dve, 1)
                for i in range(4):
                    dve.wait_ge(k_hi, 4 * b + i + 1)
                    cols = slice(i * HALF, (i + 1) * HALF)
                    dve.tensor_tensor(kb_l[:, cols], bank[i][:, :], kb_h[:, cols], ALU.subtract).then_inc(k_lo, 1)

            kv_out(0)
            for n in range(KT, 3 * KT):
                dve.wait_ge(c_act, n + 1)
                b, k = divmod(n - KT, KT)
                clip_round(stage_c[n % 2][:, :], Q2[b][:, k * D:(k + 1) * D], c_clip, n - KT, c_done)
            dve.wait_ge(row_mm, 1)
            dve.wait_ge(qc_step, 11)
            dve.tensor_scalar(rterm[:, :], bank[3][:, 0:TT], qc[:, 5:6], qc[:, 4:5], ALU.add, ALU.mult).then_inc(rterm_done, 1)
            for b in range(B):
                dve.wait_ge(cs_mm, b + 1)
                for h in range(2):
                    dve.tensor_scalar(CB[:, b, h * HALF:(h + 1) * HALF], bank[4 + 2 * b + h][:, :], qc[:, 3:4], None,
                                      ALU.mult).then_inc(cb_done, 1)
            for k in range(KT):
                chunk_lo(3 * KT + k, k)

            def lo_parts(n, t):
                for i in range(2):
                    dve.wait_ge(t_hi, 2 * n + (i + 1))
                    dve.tensor_tensor(xt_tile(XTl, t, i), bank[4 + i][:, :].rearrange("p (k n) -> p k n", k=4),
                                      xt_tile(XTh, t, i), ALU.subtract).then_inc(t_lo, 1)

            dve.wait_ge(rterm_done, 1)
            dve.wait_ge(cb_done, 4)
            dve.wait_ge(k_out, 32)
            for t in range(TT):
                xt = X[:, t * D:(t + 1) * D]
                dve.scalar_tensor_tensor(out=xt, in0=xt, scalar=rterm[:, t:t + 1], in1=CB[:, t // TB, :],
                                         op0=ALU.add, op1=ALU.add).then_inc(x_pre, 1)
                dve.wait_ge(x_pre, t + 1)
                dve.wait_ge(nat_mm, t + 1)
                for h in range(2):
                    xh = X[:, t * D + h * HALF:t * D + (h + 1) * HALF]
                    dve.scalar_tensor_tensor(out=xh, in0=bank[2 * (t % 2) + h][:, :], scalar=qc[:, 6:7], in1=xh,
                                             op0=ALU.mult, op1=ALU.add).then_inc(x_up, 1)
                dve.wait_ge(x_up, 2 * (t + 1))
                normalise(TT + t, lambda h, t=t: X[:, t * D + (h or 0) * HALF:t * D + ((h or 0) + 1) * HALF] if h is not None
                          else X[:, t * D:(t + 1) * D], t % 2, lambda t=t: dve.wait_ge(turned, t - 1) if t >= 2 else None)
                lo_parts(t, t)

            for part, src in enumerate((XTh, XTl)):
                for b in range(B):
                    dve.tensor_reduce(msum[:, part, b * KT:(b + 1) * KT],
                                      src[:, :].rearrange("p (k n) -> p k n", k=KT)[:, :, b * S:(b + 1) * S],
                                      AX.X, ALU.add).then_inc(mean_step, 1)
                    if part == 0 and b == 0:
                        dve.wait_ge(t_lo, 2 * TT)
            dve.wait_ge(mean_step, 2 * B)
            dve.tensor_tensor(msum[:, 0, :], msum[:, 0, :], msum[:, 1, :], ALU.add).then_inc(mean_step, 1)
            dve.wait_ge(mean_step, 2 * B + 1)
            dve.tensor_scalar(mean[:, :, :].rearrange("p b k -> p (b k)"), msum[:, 0, :], 1.0 / S, None,
                              ALU.mult).then_inc(mean_step, 1)
            kv_out(1)

            dve.wait_ge(lq_mm, 1)
            dve.tensor_copy(lq[:, :], bank[4][:, 0:B]).then_inc(co_step, 1)
            dve.wait_ge(sc_mm, 1)
            c3 = [coef[0:1, i, :].rearrange("p (b e) -> p b e", b=B) for i in range(4)]
            s5 = bank[5][0:1, 0:B * E_LORA].rearrange("p (b e) -> p b e", b=B)

            def over_e(col):
                return coefs[0:1, col:col + B].rearrange("p (b o) -> p b o", o=1).to_broadcast([1, B, E_LORA])

            dve.tensor_reduce(coefs[0:1, 0:B], s5, AX.X, ALU.max).then_inc(co_step, 1)
            dve.wait_ge(co_step, 2)
            dve.tensor_tensor(c3[2], s5, over_e(0), ALU.subtract).then_inc(co_step, 1)
            dve.wait_ge(co_exp, 1)
            dve.tensor_reduce(coefs[0:1, B:2 * B], c3[1], AX.X, ALU.add).then_inc(co_step, 1)
            dve.wait_ge(co_step, 4)
            dve.reciprocal(coefs[0:1, 2 * B:3 * B], coefs[0:1, B:2 * B]).then_inc(co_step, 1)
            dve.wait_ge(co_step, 5)
            dve.tensor_tensor(c3[3], c3[1], over_e(2 * B), ALU.mult).then_inc(co_step, 1)
            dve.wait_ge(bc_mm, 1)
            for i in range(2):
                rows = slice(i * R_LORA, (i + 1) * R_LORA)
                dve.tensor_copy(cvec[rows, :], bank[6][rows, i:B * E_LORA:2]).then_inc(cv_done, 1)
            dve.wait_ge(cv_done, 2)
            for u in range(B * JT):
                b, j = divmod(u, JT)
                cols = slice(j * D + b * S, j * D + (b + 1) * S)
                dve.wait_ge(h_hi, u + 1)
                dve.scalar_tensor_tensor(out=HT_l[:, cols], in0=bank[u % 4][:, :], scalar=cvec[:, u:u + 1],
                                         in1=HT_h[:, cols], op0=ALU.mult, op1=ALU.subtract).then_inc(h_lo, 1)

            def token_phase(m0, gain, sums):
                with dve.Fori(0, TT // 2) as i:
                    for j in range(2):
                        t, m = 2 * i + j, 2 * i + (m0 + j)
                        dve.wait_ge(nat_mm, m + 1)
                        for h in range(2):
                            xh = X[:, bass.ds(t * D + h * HALF, HALF)]
                            dve.scalar_tensor_tensor(out=xh, in0=bank[2 * j + h][:, :], scalar=gain, in1=xh,
                                                     op0=ALU.mult, op1=ALU.add).then_inc(x_up, 1)
                        dve.wait_ge(x_up, 2 * (m + 1))

                        def free(m=m, t=t):
                            dve.wait_ge(turned, m - 1)
                            if sums:
                                dve.wait_ge(abs_done, t + 1)

                        normalise(m + TT, lambda h, t=t: X[:, bass.ds(t * D, D)] if h is None
                                  else X[:, bass.ds(t * D + h * HALF, HALF)], j, free)
                        lo_parts(m, t)

            dve.wait_ge(k_out, 64)
            token_phase(TT, tg[:, 2:3], False)

            with dve.Fori(0, B) as b:
                for c in range(KT):
                    cols = slice((c % 4) * S, (c % 4 + 1) * S)
                    dve.wait_ge(q_hi, KT * b + (c + 1))
                    dve.tensor_tensor(qb_l[:, cols], bank[c % 4][:, :], qb_h[:, cols], ALU.subtract).then_inc(q_lo, 1)

            dve.wait_ge(q_mm, B * KT)
            for par in range(2):
                dve.memset(KS[par][96:98, :], 1.0).then_inc(ones_row, 1)

            def row_maxima(g):
                for h in range(REP):
                    for n in range(8 * h, 8 * h + 8):
                        dve.wait_ge(s_mm, STEPS * g + (n + 1))
                        dve.tensor_reduce(mxp[:, h % 2, n // 2 % 4, n % 2:n % 2 + 1], bank[n % 2][:, :], AX.X,
                                          ALU.max).then_inc(s_max, 1)
                    dve.wait_ge(s_max, STEPS * g + (8 * h + 8))
                    dve.tensor_tensor(mxc[:, h % 2, :], mxp[:, h % 2, :, 0], mxp[:, h % 2, :, 1], ALU.max).then_inc(nm_step, 1)
                    if not isinstance(g, int) or g > 0 or h >= 2:
                        dve.wait_ge(nm_turned, REP * g + (h - 1))
                    dve.wait_ge(nm_step, 3 * REP * g + (3 * h + 1))
                    dve.tensor_scalar(nm[:, h % 2, :, 0], mxc[:, h % 2, :], -1.0, None, ALU.mult).then_inc(nm_step, 1)
                    dve.wait_ge(nm_step, 3 * REP * g + (3 * h + 2))
                    dve.scalar_tensor_tensor(out=nm[:, h % 2, :, 1], in0=mxc[:, h % 2, :], scalar=-1.0,
                                             in1=nm[:, h % 2, :, 0], op0=ALU.mult, op1=ALU.subtract).then_inc(nm_step, 1)

            def outputs(g, kv, b):
                dve.wait_ge(pv_mm, KT * g + (KT + 1))
                dve.reciprocal(rec, bank[6][:, :]).then_inc(o_step, 1)
                dve.wait_ge(o_step, 4 * g + 1)
                dve.tensor_tensor(onat, bank[5][:, :], rec, ALU.mult).then_inc(o_step, 1)
                dve.wait_ge(o_step, 4 * g + 2)
                cols = bass.ds(kv * D + b * S, S)
                dve.tensor_copy(XTh[:, cols], onat).then_inc(o_step, 1)
                dve.wait_ge(o_step, 4 * g + 3)
                dve.tensor_tensor(XTl[:, cols], onat, XTh[:, cols], ALU.subtract).then_inc(o_step, 1)

            row_maxima(0)
            with dve.Fori(0, KV_HEADS - 1) as kv:
                row_maxima(2 * kv + 1)
                outputs(2 * kv, kv, 0)
                row_maxima(2 * kv + 2)
                outputs(2 * kv + 1, kv, 1)
            row_maxima(GROUPS - 1)
            outputs(GROUPS - 2, KV_HEADS - 1, 0)
            outputs(GROUPS - 1, KV_HEADS - 1, 1)

            token_phase(2 * TT, tg[:, 1:2], True)

            dve.wait_ge(abs_done, 1 + TT)
            dve.memset(AM[:, 0, :], 0.0).then_inc(am_done, 1)
            dve.wait_ge(am_done, 1)
            dve.tensor_copy(AM[:, 0, 0:TT:TB], rowabs[:, 0:TT:TB]).then_inc(am_done, 1)
            dve.tensor_copy(AM[0:VISION - P, 0, 1:TT:TB], rowabs[0:VISION - P, 1:TT:TB]).then_inc(am_done, 1)
            dve.wait_ge(am_done, 3)
            dve.tensor_tensor(AM[:, 1, :], rowabs[:, :], AM[:, 0, :], ALU.subtract).then_inc(am_done, 1)

            done = [0]

            def nxt(instruction, after=None):
                instruction.then_inc(rt_step, 1)
                done[0] += 1
                dve.wait_ge(rt_step, done[0])

            dve.wait_ge(as_mm, 1)
            nxt(dve.tensor_reduce(AS[:, :, :].rearrange("p a b -> p (a b)"),
                                  bank[1][:, 0:2 * TT].rearrange("p (a t) -> p a t", t=TB), AX.X, ALU.add))
            nxt(dve.tensor_scalar(rt[:, 0:2], AS[:, 0, :], 1.0 / (VISION * D), 1e-8, ALU.mult, ALU.add))
            nxt(dve.reciprocal(rt[:, 2:4], rt[:, 0:2]))
            nxt(dve.tensor_scalar(rt[:, 4:6], AS[:, 1, :], 1.0 / ((S - VISION) * D), None, ALU.mult))
            nxt(dve.tensor_tensor(rt[:, 6:8], rt[:, 4:6], rt[:, 2:4], ALU.mult))
            for b in range(B):
                nxt(dve.scalar_tensor_tensor(out=rb[:, b, :], in0=sc[:, SC_GL:SC_GL + EXPERTS], scalar=rt[:, 6 + b:7 + b],
                                             in1=sc[:, SC_GB:SC_GB + EXPERTS], op0=ALU.mult, op1=ALU.add))
            dve.wait_ge(lg_mm, 1)
            for b in range(B):
                nxt(dve.tensor_tensor(L[:, b * TB:(b + 1) * TB, :],
                                      bank[0][:, b * TB * EXPERTS:(b + 1) * TB * EXPERTS].rearrange("p (t e) -> p t e", e=EXPERTS),
                                      rb[:, b:b + 1, :].to_broadcast([P, TB, EXPERTS]), ALU.add))
            assert done[0] == RT_READ

            def over_experts(v):
                return v.rearrange("p (t o) -> p t o", o=1).to_broadcast([P, TT, EXPERTS])

            nxt(dve.tensor_reduce(rv[:, 0, :], L[:, :, :], AX.X, ALU.max))
            nxt(dve.tensor_tensor(L[:, :, :], L[:, :, :], over_experts(rv[:, 0, :]), ALU.subtract))
            assert done[0] == RT_SHIFTED
            dve.wait_ge(rt_exp, 1)
            nxt(dve.tensor_reduce(rv[:, 1, :], G[:, :, :], AX.X, ALU.add))
            nxt(dve.reciprocal(rv[:, 2, :], rv[:, 1, :]))
            nxt(dve.tensor_tensor(G[:, :, :], G[:, :, :], over_experts(rv[:, 2, :]), ALU.mult))
            g0, g1, g2 = (G[:, :, e] for e in range(EXPERTS))
            nxt(dve.tensor_tensor(rv[:, 3, :], g0, g1, ALU.max))
            nxt(dve.tensor_tensor(rv[:, 4, :], g0, g1, ALU.min))
            nxt(dve.tensor_tensor(rv[:, 5, :], rv[:, 3, :], g2, ALU.max))
            nxt(dve.tensor_tensor(rv[:, 3, :], rv[:, 3, :], g2, ALU.min))
            nxt(dve.tensor_tensor(rv[:, 6, :], rv[:, 3, :], rv[:, 4, :], ALU.max))
            nxt(dve.tensor_tensor(rv[:, 7, :], rv[:, 5, :], rv[:, 6, :], ALU.add))
            nxt(dve.tensor_scalar(rv[:, 7, :], rv[:, 7, :], 1e-8, None, ALU.add))
            nxt(dve.reciprocal(rv[:, 8, :], rv[:, 7, :]))
            nxt(dve.tensor_scalar(rv[:, 8, :], rv[:, 8, :], tg[:, 3:4], None, ALU.mult))
            for j in range(TOPK):
                nxt(dve.tensor_tensor(TV[:, j * TT:(j + 1) * TT], rv[:, 5 + j, :], rv[:, 8, :], ALU.mult))
            f0, f1, f2 = (G[0:1, 0:TT:TB, e] for e in range(EXPERTS))
            nxt(dve.tensor_tensor(rk[0:1, 0, :], f0, f1, ALU.is_ge))
            nxt(dve.tensor_tensor(rk[0:1, 1, :], f0, f2, ALU.is_ge))
            nxt(dve.tensor_tensor(rk[0:1, 2, :], f1, f2, ALU.is_ge))
            nxt(dve.tensor_tensor(rk[0:1, 3, :], rk[0:1, 0, :], rk[0:1, 2, :], ALU.subtract))
            nxt(dve.tensor_scalar(rk[0:1, 3, :], rk[0:1, 3, :], 1.0, None, ALU.add))
            nxt(dve.tensor_tensor(rk[0:1, 4, :], rk[0:1, 1, :], rk[0:1, 2, :], ALU.add))
            for j in range(TOPK):
                nxt(dve.tensor_scalar(rk[0:1, 5, :], rk[0:1, 3, :], float(j), None, ALU.is_equal))
                nxt(dve.tensor_scalar(rk[0:1, 6, :], rk[0:1, 4, :], float(j), 2.0, ALU.is_equal, ALU.mult))
                nxt(dve.tensor_tensor(idxf[0:1, :, j], rk[0:1, 5, :], rk[0:1, 6, :], ALU.add))
            dve.tensor_copy(idx[:, :], idxf[:, :, :].rearrange("p b j -> p (b j)")).then_inc(idx_done, 1)

            with dve.Fori(0, B) as b:
                with dve.Fori(0, TOPK) as j:
                    s = b * TOPK + j
                    for f in range(KT):
                        cols = slice(f * S, (f + 1) * S)
                        dve.wait_ge(act_done, KT * s + (f + 2))
                        dve.tensor_copy(HT_h[:, cols], hid[:, cols]).then_inc(e_hi, 1)
                        dve.wait_ge(e_hi, KT * s + (f + 1))
                        dve.tensor_tensor(HT_l[:, cols], hid[:, cols], HT_h[:, cols], ALU.subtract).then_inc(e_lo, 1)
                    dve.wait_ge(b2_in, 16 * s + 16)
                    dve.wait_ge(x_fin, 2 * TB * s + 1)
                    for i in range(TB):
                        dve.wait_ge(b_mm, TB * s + (i + 2))
                        t = b * TB + i
                        for h in range(2):
                            hc = slice(h * HALF, (h + 1) * HALF)
                            xh = X[:, bass.ds(t * D + h * HALF, HALF)]
                            dve.tensor_tensor(eo[h], bank[4 + 2 * (i % 2) + h][:, :], b2b[:, hc], ALU.add).then_inc(eo_done, 1)
                            dve.wait_ge(eo_done, 2 * TB * s + (2 * i + h + 2))
                            dve.scalar_tensor_tensor(out=xh, in0=eo[h], scalar=TV[:, bass.ds(j * TT + t, 1)], in1=xh,
                                                     op0=ALU.mult, op1=ALU.add).then_inc(x_fin, 1)

    return nc


_SHAPES = {"x": (TT, P, D), "ctx_nat": (B, KT, P, D), "ctx_t": (B, KT, P, SC), "wts": (N_WT, P, D),
           "lora_q": (P, KT * P), "lora_keys": (P, E_LORA), "scalars": (1, N_SC), "gate_w": (P, KT * EXPERTS),
           "w1": (EXPERTS, KT, P, D), "b1": (P, EXPERTS * KT), "w2": (EXPERTS, KT, P, D), "b2": (EXPERTS, D)}


def kernel(**a):
    import concourse.bacc as bacc
    from concourse.bass_utils import run_bass_kernel_spmd

    a = {k: np.asarray(v) for k, v in a.items()}

    def chunks(w):
        n = D // w.shape[1]
        return w.reshape(-1, n, P, w.shape[1]).transpose(0, 2, 1, 3).reshape(-1, P, D)

    arrays = {
        "x": a["x"].reshape(TT, P, D),
        "ctx_nat": a["ctx_4096"].reshape(B, KT, P, D),
        "ctx_t": a["ctx_4096"].transpose(0, 2, 1).reshape(B, KT, P, SC),
        "wts": np.concatenate([
            chunks(np.concatenate([a["L1_xattn_Wk"], a["L1_xattn_Wv"]], axis=1)),
            chunks(a["L0_ffn_lora_down"].transpose(1, 0, 2).reshape(D, ER)),
            chunks(a["L0_ffn_W_org"].T),
            chunks(a["L0_ffn_lora_up"].reshape(ER, D)),
            chunks(a["L1_xattn_Wq"]),
            chunks(a["L1_xattn_Wo"])]),
        "lora_q": a["L0_ffn_Wq"].T.reshape(KT, P, K_LORA).transpose(1, 0, 2).reshape(P, KT * P),
        "lora_keys": a["L0_ffn_lora_keys"].T,
        "scalars": np.concatenate([
            a["L0_xattn_x1_scale"], a["L0_xattn_x1_zp"], a["L0_xattn_x2_scale"], a["L0_xattn_x2_zp"],
            a["g_xattn"], a["g_ffn"], a["L1_ffn_gate_b"], a["L1_ffn_gate_w"][D]]).reshape(1, N_SC),
        "gate_w": a["L1_ffn_gate_w"][:D].reshape(KT, P, EXPERTS).transpose(1, 0, 2).reshape(P, KT * EXPERTS),
        "w1": a["L1_ffn_w1"].reshape(EXPERTS, KT, P, D),
        "b1": a["L1_ffn_b1"].reshape(EXPERTS, KT, P).transpose(2, 0, 1).reshape(P, EXPERTS * KT),
        "w2": a["L1_ffn_w2"].reshape(EXPERTS, KT, P, D),
        "b2": a["L1_ffn_b2"],
    }
    nc = bacc.Bacc("TRN2", target_bir_lowering=False, num_devices=1)
    arrays = {k: np.ascontiguousarray(v) for k, v in arrays.items()}
    args = [nc.dram_tensor(f"{k}_in", _SHAPES[k], F32, kind="ExternalInput").ap() for k in _SHAPES]
    args.append(nc.dram_tensor("y_out", (TT, P, D), F32, kind="ExternalOutput").ap())
    build(nc, *args)
    r = run_bass_kernel_spmd(nc, [{f"{k}_in": arrays[k] for k in _SHAPES}], core_ids=[0])
    return r.results[0]["y_out"].reshape(B, S, D)
```

```python
from contextlib import ExitStack

import numpy as np
import concourse.bass as bass
from concourse import mybir

F32 = mybir.dt.float32
BF16 = mybir.dt.bfloat16
I32 = mybir.dt.int32
ALU = mybir.AluOpType
ACT = mybir.ActivationFunctionType
AX = mybir.AxisListType

P = 128
B, S, D = 2, 512, 1024
SC = 1024
KT = D // P
TT = B * S // P
TB = S // P
HALF = 512
E_LORA, R_LORA, K_LORA = 8, 64, 128
ER = E_LORA * R_LORA
JT = ER // P
HEADS, KV_HEADS, HD = 32, 8, 32
REP = HEADS // KV_HEADS
KVD = KV_HEADS * HD
GROUPS = B * KV_HEADS
STEPS = REP * SC // P
EXPERTS, TOPK = 3, 2
VISION = int(S * 0.3)
MAGIC = 1.5 * 2.0 ** 23
MID = 128.0
QMAX = 255.0
EPS = 1e-5
WT_LAYOUT = [("kv", 4), ("down", 4), ("org", 8), ("up", 4), ("q", 8), ("o", 8)]
N_WT = sum(n for _, n in WT_LAYOUT)
WT_AT = {name: sum(n for _, n in WT_LAYOUT[:i]) for i, (name, _) in enumerate(WT_LAYOUT)}
SC_S1, SC_Z1, SC_S2, SC_Z2, SC_GX, SC_GF, SC_GB, SC_GL = 0, 1, 2, 3, 4, 6, 8, 11
N_SC = 14
RT_READ = 5 + 2 * B
O_STEPS = 3
RT_SHIFTED = RT_READ + 2


def ds(i, n):
    return bass.ds(i * n, n)


def per_tile(v):
    return v[:, :].rearrange("p (k n) -> p k n", k=KT)


def xt_tile(xt, t, i):
    return per_tile(xt)[:, 4 * i:4 * i + 4, ds(t, P)]


def build(nc, x, ctx_nat, ctx_t, wts, lora_q, lora_keys, scalars, gate_w, w1, b1, w2, b2, out):
    with ExitStack() as ctx:
        def sb(name, shape, dt):
            return ctx.enter_context(nc.sbuf_tensor(name, shape, dt))

        def sem(name):
            return ctx.enter_context(nc.semaphore(name))

        X = sb("X", [P, TT * D], F32)
        XTh = sb("XTh", [P, KT * TT * P], BF16)
        XTl = sb("XTl", [P, KT * TT * P], BF16)
        R = [sb(f"R{i}", [P, KT * D], BF16) for i in range(6)]
        V = sb("V", [P, B * KT * KVD], F32)
        stage_w = [sb(f"stage_w{i}", [P, D], F32) for i in range(2)]
        stage_c = [sb(f"stage_c{i}", [P, D], F32) for i in range(2)]
        xn = [sb(f"xn{i}", [P, D], F32) for i in range(2)]
        identf = sb("identf", [P, P], F32)
        identb = sb("identb", [P, P], BF16)
        onesf = sb("onesf", [P, P], F32)
        onesb = sb("onesb", [P, P], BF16)
        zero = sb("zero", [P, 1], F32)
        sc = sb("sc", [P, N_SC], F32)
        rs1 = sb("rs1", [P, 1], F32)
        rs2 = sb("rs2", [P, 1], F32)
        tg = sb("tg", [P, 4], F32)
        qc = sb("qc", [P, 8], F32)
        stats = [sb(f"stats{i}", [P, 2, 6], F32) for i in range(2)]
        mv = [sb(f"mv{i}", [P, 2], F32) for i in range(2)]
        lnv = [sb(f"lnv{i}", [P, 6], F32) for i in range(2)]
        carrier = sb("carrier", [P, 1], F32)
        rterm = sb("rterm", [P, TT], F32)
        msum = sb("msum", [P, 2, B * KT], F32)
        mean = sb("mean", [P, B, KT], F32)
        lq = sb("lq", [P, B], F32)
        keys = sb("keys", [P, E_LORA], F32)
        coef = sb("coef", [1, 4, B * E_LORA], F32)
        coefs = sb("coefs", [1, 8], F32)
        cvec = sb("cvec", [P, B * JT], F32)
        mxp = sb("mxp", [P, 2, TB, 2], F32)
        mxc = sb("mxc", [P, 2, TB], F32)
        nm = sb("nm", [P, 2, TB, 2], BF16)
        gwf = sb("gwf", [P, KT * EXPERTS], F32)
        gwh = sb("gwh", [P, KT * EXPERTS], BF16)
        gwl = sb("gwl", [P, KT * EXPERTS], BF16)
        b1t = sb("b1t", [P, EXPERTS * KT], F32)
        rowabs = sb("rowabs", [P, TT], F32)
        AM = sb("AM", [P, 2, TT], F32)
        AS = sb("AS", [P, 2, B], F32)
        rt = sb("rt", [P, 8], F32)
        rb = sb("rb", [P, B, EXPERTS], F32)
        L = sb("L", [P, TT, EXPERTS], F32)
        G = sb("G", [P, TT, EXPERTS], F32)
        rv = sb("rv", [P, 9, TT], F32)
        TV = sb("TV", [P, TOPK * TT], F32)
        rk = sb("rk", [1, 9, B], F32)
        idxf = sb("idxf", [1, B, TOPK], F32)
        idx = sb("idx", [1, B * TOPK], I32)

        half_r = KT * D // 2
        kv_h, kv_l = R[0][:, 0:half_r], R[0][:, half_r:]
        down_h, down_l = R[1][:, 0:half_r], R[1][:, half_r:]
        ct_h, ct_l = R[2], R[3]
        Q2 = [R[4], R[5]]
        XQ = XTl
        kb_h = xn[0][:, :].bitcast(BF16)
        kb_l = xn[1][:, :].bitcast(BF16)
        CB = V[:, KT * KVD:].rearrange("p (b n) -> p b n", b=B)
        org_h, org_l = R[2], R[3]
        up_h, up_l = R[0][:, 0:half_r], R[0][:, half_r:]
        HT_h, HT_l = R[4][:, 0:half_r], R[4][:, half_r:]
        LQW = R[5][:, 0:2 * KT * P].bitcast(F32)
        q_h, q_l = R[1], R[5]
        qb_h, qb_l = R[4][:, 0:half_r], R[4][:, half_r:]
        o_h, o_l = R[2], R[3]
        PB = [R[i // 2][:, :].bitcast(F32)[:, (i % 2) * REP * S:(i % 2 + 1) * REP * S] for i in range(4)]
        QS = [R[5][:, i * REP * S:(i + 1) * REP * S] for i in range(2)] + [stage_c[1][:, :].bitcast(BF16)]
        KS = [R[5][:, 2 * REP * S + i * SC:2 * REP * S + (i + 1) * SC] for i in range(2)] + [xn[0][:, S:].bitcast(BF16)]
        at = 2 * REP * S + 2 * SC
        VS = [R[5][:, at + i * 2 * KT * HD:at + (i + 1) * 2 * KT * HD].bitcast(F32) for i in range(2)]
        PS = [R[4][:, :].bitcast(F32)[:, i * REP * S:(i + 1) * REP * S] for i in range(2)]
        o_raw = [stage_c[0][:, i * S:(i + 1) * S] for i in range(2)]
        p_sum = xn[0][:, 0:S]
        s_bank = (0, 1, 7)
        rec, onat = xn[1][:, 0:S], xn[1][:, S:]
        w1_h, w1_l, w2_h, w2_l = R[0], R[1], R[2], R[3]
        hid = R[5][:, :].bitcast(F32)
        b2b = xn[0]
        eo = [xn[1][:, 0:HALF], xn[1][:, HALF:]]
        junk = R[0][:, 0:D]

        bank = [ctx.enter_context(nc.psum_tensor(f"bank{i}", [P, HALF], F32)) for i in range(8)]
        bank_b = [b[:, :].bitcast(BF16) for b in bank]

        k_scr = nc.dram_tensor("k_scr", [B, 2, KVD, SC], BF16, kind="Internal").ap()
        q_scr = nc.dram_tensor("q_scr", [KT, B, 2, P, S], BF16, kind="Internal").ap()

        const_in = sem("const_in")
        w_in = [sem(f"w_in{i}") for i in range(2)]
        c_in = [sem(f"c_in{i}") for i in range(2)]
        x_in = [sem(f"x_in{i}") for i in range(TT)]
        lqw_in = sem("lqw_in")
        wt_hi = sem("wt_hi")
        wt_done = sem("wt_done")
        made = sem("made")
        madeb = sem("madeb")
        qc_step = sem("qc_step")
        tg_done = sem("tg_done")
        c_act = sem("c_act")
        c_clip = sem("c_clip")
        c_done = sem("c_done")
        ln_step = sem("ln_step")
        ln_sd = sem("ln_sd")
        xn_done = sem("xn_done")
        xq_sc = sem("xq_sc")
        xq_clip = sem("xq_clip")
        xq_done = sem("xq_done")
        xq_turned = sem("xq_turned")
        xq_t = sem("xq_t")
        kv_mm = sem("kv_mm")
        k_hi = sem("k_hi")
        k_lo = sem("k_lo")
        v_act = sem("v_act")
        v_dve = sem("v_dve")
        k_out = sem("k_out")
        cs_mm = sem("cs_mm")
        cb_done = sem("cb_done")
        row_mm = sem("row_mm")
        rterm_done = sem("rterm_done")
        x_pre = sem("x_pre")
        nat_mm = sem("nat_mm")
        x_up = sem("x_up")
        turned = sem("turned")
        t_hi = sem("t_hi")
        t_lo = sem("t_lo")
        mean_step = sem("mean_step")
        lq_mm = sem("lq_mm")
        sc_mm = sem("sc_mm")
        bc_mm = sem("bc_mm")
        co_step = sem("co_step")
        co_exp = sem("co_exp")
        cv_done = sem("cv_done")
        h_mm = sem("h_mm")
        h_hi = sem("h_hi")
        h_lo = sem("h_lo")
        q_mm = sem("q_mm")
        q_hi = sem("q_hi")
        q_lo = sem("q_lo")
        q_out = [sem(f"q_out{i}") for i in range(4)]
        ones_row = sem("ones_row")
        qk_in = [sem(f"qk_in{i}") for i in range(3)]
        vs_done = sem("vs_done")
        s_mm = sem("s_mm")
        s_max = sem("s_max")
        nm_step = sem("nm_step")
        nm_turned = sem("nm_turned")
        nm_row = sem("nm_row")
        st_mm = sem("st_mm")
        exp_done = sem("exp_done")
        pv_mm = sem("pv_mm")
        p_add = sem("p_add")
        one_mm = sem("one_mm")
        o_out = sem("o_out")
        sum_out = sem("sum_out")
        rec_done = sem("rec_done")
        o_step = sem("o_step")
        abs_done = sem("abs_done")
        lg_mm = sem("lg_mm")
        as_mm = sem("as_mm")
        am_done = sem("am_done")
        rt_step = sem("rt_step")
        rt_exp = sem("rt_exp")
        idx_done = sem("idx_done")
        a_mm = sem("a_mm")
        act_done = sem("act_done")
        e_hi = sem("e_hi")
        e_lo = sem("e_lo")
        b2_in = sem("b2_in")
        b_mm = sem("b_mm")
        eo_done = sem("eo_done")
        x_fin = sem("x_fin")
        x_out = sem("x_out")

        block = ctx.enter_context(nc.Block())
        N_CONST = 5
        W_O_END = N_WT

        @block.sync
        def _(sp):
            sp.dma_start(sc[:, :], scalars.to_broadcast([P, N_SC])).then_inc(const_in, 16)
            sp.dma_start(keys[:, :], lora_keys).then_inc(const_in, 16)
            sp.dma_start(gwf[:, :], gate_w).then_inc(const_in, 16)
            sp.dma_start(b1t[:, :], b1).then_inc(const_in, 16)

            def load_weights(first, count):
                for n in range(first, first + count):
                    if n >= 2:
                        sp.wait_ge(wt_done, n - 1)
                    sp.dma_start(stage_w[n % 2][:, :], wts[n]).then_inc(w_in[n % 2], 16)

            def load_context(n, src):
                if n >= 2:
                    sp.wait_ge(c_done, n - 1)
                sp.dma_start(stage_c[n % 2][:, :], src).then_inc(c_in[n % 2], 16)

            for k in range(KT):
                if k % 2 == 0:
                    load_weights(WT_AT["kv"] + k // 2, 1)
                load_context(k, ctx_t[0, k])
            for t in range(TT):
                sp.dma_start(X[:, t * D:(t + 1) * D], x[t]).then_inc(x_in[t], 16)
            for n in range(B * KT):
                load_context(KT + n, ctx_nat[n // KT, n % KT])
            load_weights(WT_AT["down"], 4)

            def keys_out(b):
                sp.wait_ge(k_lo, 4 * (b + 1))
                for part, src in enumerate((kb_h, kb_l)):
                    sp.dma_start(k_scr[b, part].rearrange("(c p) s -> p c s", c=2),
                                 src.rearrange("p (c s) -> p c s", c=2)).then_inc(k_out, 16)

            keys_out(0)
            for k in range(KT):
                load_context(3 * KT + k, ctx_t[1, k])
            sp.wait_ge(nat_mm, TT)
            sp.dma_start(LQW, lora_q).then_inc(lqw_in, 16)
            load_weights(WT_AT["org"], 2)
            keys_out(1)
            load_weights(WT_AT["org"] + 2, 6)
            load_weights(WT_AT["up"], 4)
            load_weights(WT_AT["q"], 8)

            def queries_out(b, c):
                sp.wait_ge(q_lo, KT * b + (c + 2))
                for part, src in enumerate((qb_h, qb_l)):
                    sp.dma_start(q_scr[c, bass.ds(b, 1), part].rearrange("o p s -> (o p) s"),
                                 src[:, (c % 4) * S:(c % 4 + 1) * S]).then_inc(q_out[c % 4], 16)

            for b in range(B):
                for c in range(KT):
                    queries_out(b, c)
                    if c % 2 == 1:
                        load_weights(WT_AT["o"] + (b * KT + c) // 2, 1)

            for slot in range(4):
                sp.wait_ge(q_out[slot], 1 + 16 * 2 * B * KT // 4)
            sp.wait_ge(k_out, 16 * 2 * B)

            def group_in(g):
                kv, b = divmod(g, B)
                if g >= 3:
                    sp.wait_ge(st_mm, STEPS * (g - 2))
                for row, part in ((0, 0), (32, 0), (64, 1)):
                    sp.dma_start(QS[g % 3][row:row + HD, :].rearrange("p (h s) -> p h s", h=REP),
                                 q_scr[kv, b, part].rearrange("(h d) s -> d h s", h=REP)).then_inc(qk_in[g % 3], 16)
                for row, part in ((0, 0), (32, 1), (64, 0)):
                    sp.dma_start(KS[g % 3][row:row + HD, :],
                                 k_scr[b, part, ds(kv, HD), :]).then_inc(qk_in[g % 3], 16)

            sp.wait_ge(q_mm, B * KT)
            for g in range(GROUPS):
                group_in(g)

            sp.wait_ge(idx_done, 1)
            reg = sp.alloc_register("expert_sp")
            with sp.Fori(0, B * TOPK) as s:
                sp.reg_load(reg, idx[0:1, bass.ds(s, 1)])
                e = sp.snap(reg, min_val=0, max_val=EXPERTS - 1)
                for c in range(KT):
                    n = W_O_END + 2 * KT * s + c
                    sp.wait_ge(wt_done, n - 1)
                    sp.dma_start(stage_w[c % 2][:, :], w1[bass.ds(e, 1), c].rearrange("o p n -> (o p) n")).then_inc(w_in[c % 2], 16)
                sp.wait_ge(eo_done, 2 * TB * s + 1)
                sp.dma_start(b2b[:, :], b2[bass.ds(e, 1), :].to_broadcast([P, D])).then_inc(b2_in, 16)
                for c in range(KT):
                    n = W_O_END + 2 * KT * s + KT + c
                    sp.wait_ge(wt_done, n - 1)
                    sp.dma_start(stage_w[c % 2][:, :], w2[bass.ds(e, 1), c].rearrange("o p n -> (o p) n")).then_inc(w_in[c % 2], 16)
            sp.wait_ge(x_out, 16 * TT)

        @block.gpsimd
        def _(pool):
            pool.memset(zero[:, :], 0.0).then_inc(made, 1)
            pool.memset(identf[:, :], 0.0).then_inc(made, 1)
            pool.memset(onesf[:, :], 1.0).then_inc(made, 1)
            pool.wait_ge(made, 3)
            pool.affine_select(out=identf[:, :], in_=identf[:, :], compare_op=ALU.not_equal, fill=1.0, base=0,
                               pattern=[[-1, P]], channel_multiplier=1).then_inc(made, 1)

            def split(n, stage, hi, lo):
                pool.wait_ge(w_in[stage], 16 * ((n - stage) // 2 + 1) if isinstance(n, int) else 8 * n - 8 * stage + 16)
                pool.tensor_tensor(hi, stage_w[stage][:, :], zero[:, :].to_broadcast([P, D]), ALU.add).then_inc(wt_hi, 1)
                pool.wait_ge(wt_hi, n + 1)
                pool.tensor_tensor(lo, stage_w[stage][:, :], hi, ALU.subtract).then_inc(wt_done, 1)

            def split_group(name, hi, lo):
                first, count = WT_AT[name], dict(WT_LAYOUT)[name]
                with pool.Fori(0, count // 2) as i:
                    for j in range(2):
                        at_col = bass.ds(i * (2 * D) + j * D, D)
                        split(first + 2 * i + j, j, hi[:, at_col], lo[:, at_col])

            split_group("kv", kv_h, kv_l)
            split_group("down", down_h, down_l)
            pool.wait_ge(kv_mm, 2)
            split_group("org", org_h, org_l)
            split_group("up", up_h, up_l)
            pool.wait_ge(h_mm, B * JT)
            pool.wait_ge(lq_mm, 1)
            split_group("q", q_h, q_l)
            pool.wait_ge(nat_mm, 2 * TT)
            split_group("o", o_h, o_l)

            def stage_values(g):
                if g >= 2:
                    pool.wait_ge(pv_mm, KT * (g - 1))
                kv, b = divmod(g, B)
                src = V[:, b * KT * KVD:(b + 1) * KT * KVD].rearrange("p (t n) -> p t n", t=KT)
                pool.tensor_copy(VS[b].rearrange("p (t n) -> p t n", t=KT), src[:, :, ds(kv, HD)]).then_inc(vs_done, 1)

            def divide(g):
                kv, b = divmod(g, B)
                cols = slice(kv * D + b * S, kv * D + (b + 1) * S)
                if g > 0:
                    pool.wait_ge(o_step, O_STEPS * g)
                pool.wait_ge(rec_done, 4 * (g + 1))
                pool.tensor_tensor(onat, o_raw[g % 2], rec, ALU.mult).then_inc(o_step, 1)
                pool.wait_ge(o_step, O_STEPS * g + 1)
                pool.tensor_tensor(XTh[:, cols], onat, zero[:, :].to_broadcast([P, S]), ALU.add).then_inc(o_step, 1)
                pool.wait_ge(o_step, O_STEPS * g + 2)
                pool.tensor_tensor(XTl[:, cols], onat, XTh[:, cols], ALU.subtract).then_inc(o_step, 1)

            pool.wait_ge(q_mm, B * KT)
            stage_values(0)
            stage_values(1)
            for g in range(GROUPS):
                for j in range(KT // 2):
                    pool.wait_ge(exp_done, STEPS * g + 2 * REP * (j + 1))
                    if 4 * g + j >= 2:
                        pool.wait_ge(one_mm, 4 * g + j - 1)
                    pool.tensor_tensor(PS[j % 2], PB[2 * j % 4], PB[2 * j % 4 + 1], ALU.add).then_inc(p_add, 1)
                    if j == 0 and 1 <= g < GROUPS - 1:
                        stage_values(g + 1)
                if g > 0:
                    divide(g - 1)
            divide(GROUPS - 1)

            pool.wait_ge(idx_done, 1)
            with pool.Fori(0, B * TOPK) as s:
                pool.wait_ge(a_mm, KT * s + 1)
                for c in range(KT):
                    cols = slice(c * D, (c + 1) * D)
                    split(W_O_END + 2 * KT * s + c, c % 2, w1_h[:, cols], w1_l[:, cols])
                pool.wait_ge(b_mm, TB * s + 1)
                for c in range(KT):
                    cols = slice(c * D, (c + 1) * D)
                    split(W_O_END + 2 * KT * s + KT + c, c % 2, w2_h[:, cols], w2_l[:, cols])

        @block.tensor
        def _(pe):
            for counted in (a_mm, b_mm):
                pe.sem_inc(counted, 1)
            pe.wait_ge(madeb, 2)

            def triple(outs, ah, al, bh, bl, first, last):
                for a, bs in ((ah, bh), (ah, bl), (al, bh)):
                    for o, m in zip(outs, bs):
                        mm = pe.matmul(o, a, m, start=first and a is ah and bs is bh,
                                       stop=last and a is al)
                return mm

            def kv_tile(k, first):
                def c(t, n0, n):
                    return t[:, bass.ds(k * D + n0, n)] if not isinstance(k, int) else t[:, k * D + n0:k * D + n0 + n]

                def w(t, n0, n):
                    return t[:, bass.ds(k * HALF + n0, n)] if not isinstance(k, int) else t[:, k * HALF + n0:k * HALF + n0 + n]

                for m in range(2):
                    for a, r in ((kv_h, ct_h), (kv_h, ct_l), (kv_l, ct_h)):
                        for h in range(2):
                            mm = pe.matmul(bank[2 * m + h][:, :], w(a, m * P, P), c(r, h * HALF, HALF),
                                           start=first and a is kv_h and r is ct_h, stop=False, skip_group_check=True)
                for t in range(KT):
                    for a, r in ((ct_h, kv_h), (ct_h, kv_l), (ct_l, kv_h)):
                        mm = pe.matmul(bank[4 + t // 2][:, (t % 2) * KVD:(t % 2 + 1) * KVD], c(a, t * P, P),
                                       w(r, KVD, KVD), start=first and t % 2 == 0 and a is ct_h and r is kv_h,
                                       stop=False, skip_group_check=True)
                return mm

            def keys_values(b):
                at_c = (0, 3 * KT)[b]
                pe.wait_ge(wt_done, 1)
                pe.wait_ge(c_done, at_c + 1)
                kv_tile(0, True)
                pe.wait_ge(c_done, at_c + 2)
                kv_tile(1, False)
                with pe.Fori(1, KT // 2 - 1) as c:
                    pe.wait_ge(wt_done, c + 1)
                    for j in range(2):
                        pe.wait_ge(c_done, at_c + 2 * c + j + 1)
                        kv_tile(2 * c + j, False)
                pe.wait_ge(wt_done, KT // 2)
                for k in (KT - 2, KT - 1):
                    pe.wait_ge(c_done, at_c + k + 1)
                    mm = kv_tile(k, False)
                mm.then_inc(kv_mm, 1)

            keys_values(0)

            for t in range(TT):
                pe.wait_ge(xq_done, t + 1)
                if t < 2:
                    pe.wait_ge(v_dve, 2)
                else:
                    pe.wait_ge(xq_t, t - 1)
                for k in range(KT):
                    mm = pe.transpose(bank_b[6 + t % 2][:, k * P:(k + 1) * P], XQ[:, t * D + k * P:t * D + (k + 1) * P],
                                      identb[:, :])
                mm.then_inc(xq_turned, 1)
            pe.wait_ge(k_lo, 4)
            pe.wait_ge(xq_t, TT)
            for t in range(TT):
                for k in range(KT):
                    mm = pe.matmul(bank[3][:, t:t + 1], XTh[:, k * D + t * P:k * D + (t + 1) * P], onesb[:, 0:1],
                                   start=k == 0, stop=k == KT - 1)
            mm.then_inc(row_mm, 1)
            pe.wait_ge(v_act, 2)
            for b in range(B):
                pe.wait_ge(c_done, KT * (2 + b))
                for h in range(2):
                    for k in range(KT):
                        mm = pe.matmul(bank[4 + 2 * b + h][:, :], onesb[:, :],
                                       Q2[b][:, k * D + h * HALF:k * D + (h + 1) * HALF], start=k == 0, stop=k == KT - 1)
                mm.then_inc(cs_mm, 1)

            def pair(m):
                return bank[2 * (m % 2)], bank[2 * (m % 2) + 1]

            def turn_behind(n, par):
                pe.wait_ge(xn_done, TT + n + 1)
                pe.wait_ge(t_lo, 2 * n)
                for k in range(KT):
                    mm = pe.transpose(bank[4 + k // 4][:, (k % 4) * P:(k % 4 + 1) * P], xn[par][:, k * P:(k + 1) * P],
                                      identf[:, :])
                mm.then_inc(turned, 1)

            pe.wait_ge(rterm_done, 1)
            pe.wait_ge(cb_done, 4)
            for t in range(TT):
                if t >= 2:
                    pe.wait_ge(x_up, 2 * (t - 1))
                for h in range(2):
                    for k in range(KT):
                        mm = pe.matmul(pair(t)[h][:, :], XTh[:, k * D + t * P:k * D + (t + 1) * P],
                                       Q2[t // TB][:, k * D + h * HALF:k * D + (h + 1) * HALF],
                                       start=k == 0, stop=k == KT - 1)
                mm.then_inc(nat_mm, 1)
                if t >= 1:
                    turn_behind(t - 1, (t - 1) % 2)
            turn_behind(TT - 1, (TT - 1) % 2)

            pe.wait_ge(x_up, 2 * TT)
            pe.wait_ge(t_lo, 2 * TT)
            keys_values(1)

            pe.wait_ge(k_lo, 8)
            pe.wait_ge(v_act, 4)
            pe.wait_ge(v_dve, 4)
            pe.wait_ge(lqw_in, 16)
            pe.wait_ge(mean_step, 2 * B + 2)
            for k in range(KT):
                mm = pe.matmul(bank[4][:, 0:B], LQW[:, k * P:(k + 1) * P], mean[:, :, k], start=k == 0, stop=k == KT - 1)
            mm.then_inc(lq_mm, 1)

            def lora_hidden(u):
                b, j = divmod(u, JT)
                if u >= 4:
                    pe.wait_ge(h_lo, u - 3)
                for k in range(KT):
                    mm = triple([bank[u % 4][:, :]], down_h[:, k * ER + j * P:k * ER + (j + 1) * P],
                                down_l[:, k * ER + j * P:k * ER + (j + 1) * P],
                                [XTh[:, k * D + b * S:k * D + (b + 1) * S]], [XTl[:, k * D + b * S:k * D + (b + 1) * S]],
                                k == 0, k == KT - 1)
                mm.then_inc(h_mm, 1)

            pe.wait_ge(wt_done, WT_AT["org"])
            lora_hidden(0)
            pe.wait_ge(co_step, 1)
            for b in range(B):
                mm = pe.matmul(bank[5][0:1, b * E_LORA:(b + 1) * E_LORA], lq[:, b:b + 1], keys[:, :], start=True, stop=True)
            mm.then_inc(sc_mm, 1)
            lora_hidden(1)
            pe.wait_ge(co_step, 6)
            pe.matmul(bank[6][:, 0:B * E_LORA], onesf[0:1, :], coef[0:1, 3, :], start=True, stop=True).then_inc(bc_mm, 1)
            for u in range(2, B * JT):
                lora_hidden(u)

            def token_tile(m, t, par, w_h, w_l, lora):
                pe.wait_ge(x_up, 2 * (m - 1))
                outs = [bank[2 * par][:, :], bank[2 * par + 1][:, :]]
                for k in range(KT):
                    cols = bass.ds(k * D + t * P, P)
                    mm = triple(outs, XTh[:, cols], XTl[:, cols],
                                [w_h[:, k * D + h * HALF:k * D + (h + 1) * HALF] for h in range(2)],
                                [w_l[:, k * D + h * HALF:k * D + (h + 1) * HALF] for h in range(2)],
                                k == 0, k == KT - 1 and not lora)
                if lora:
                    for j in range(JT):
                        cols = bass.ds(j * D + t * P, P)
                        mm = triple(outs, HT_h[:, cols], HT_l[:, cols],
                                    [up_h[:, j * D + h * HALF:j * D + (h + 1) * HALF] for h in range(2)],
                                    [up_l[:, j * D + h * HALF:j * D + (h + 1) * HALF] for h in range(2)],
                                    False, j == JT - 1)
                mm.then_inc(nat_mm, 1)

            def token_phase(m0, w_h, w_l, lora):
                token_tile(m0, 0, 0, w_h, w_l, lora)
                with pe.Fori(0, TT // 2 - 1) as i:
                    token_tile(2 * i + (m0 + 1), 2 * i + 1, 1, w_h, w_l, lora)
                    turn_behind(2 * i + m0, 0)
                    token_tile(2 * i + (m0 + 2), 2 * i + 2, 0, w_h, w_l, lora)
                    turn_behind(2 * i + (m0 + 1), 1)
                token_tile(m0 + TT - 1, TT - 1, 1, w_h, w_l, lora)
                turn_behind(m0 + TT - 2, 0)
                turn_behind(m0 + TT - 1, 1)

            pe.wait_ge(h_lo, B * JT)
            pe.wait_ge(wt_done, WT_AT["q"])
            token_phase(TT, org_h, org_l, True)

            pe.wait_ge(wt_done, WT_AT["o"])
            pe.wait_ge(x_up, 4 * TT)
            pe.wait_ge(t_lo, 4 * TT)
            with pe.Fori(0, B) as b:
                for c in range(KT):
                    pe.wait_ge(q_lo, KT * b + (1 + max(c - 3, 0)))
                    for k in range(KT):
                        w, r = slice(k * D + c * P, k * D + (c + 1) * P), bass.ds(b * S + k * D, S)
                        mm = triple([bank[c % 4][:, :]], q_h[:, w], q_l[:, w], [XTh[:, r]], [XTl[:, r]],
                                    k == 0, k == KT - 1)
                    mm.then_inc(q_mm, 1)

            def score_step(g, n):
                h, qt, kh = n // 8, n // 2 % 4, n % 2
                u = STEPS * g + n
                if u >= 3:
                    pe.wait_ge(s_max, u - 2)
                pe.matmul(bank[s_bank[u % 3]][:, :], QS[g % 3][0:96, h * S + qt * P:h * S + (qt + 1) * P],
                          KS[g % 3][0:96, kh * HALF:(kh + 1) * HALF], start=True, stop=True).then_inc(s_mm, 1)

            def max_row(g, h):
                pe.wait_ge(nm_step, 3 * (REP * g + h + 1))
                if REP * g + h > 0:
                    pe.wait_ge(nm_row, REP * g + h)
                for qt in range(TB):
                    mm = pe.transpose(bank_b[4][96:98, qt * P:(qt + 1) * P], nm[:, h % 2, qt, :], identb[:, :])
                mm.then_inc(nm_turned, 1)

            def over_keys(out_bank, weights, probs, first, last):
                for h in range(REP):
                    mm = pe.matmul(out_bank[h * HD:(h + 1) * HD, :], weights, probs[:, h * S:(h + 1) * S],
                                   start=first, stop=last)
                return mm

            def weigh(g, kt):
                pe.wait_ge(exp_done, STEPS * g + REP * (kt + 1))
                if kt == 0:
                    pe.wait_ge(vs_done, g + 1)
                    if g > 0:
                        pe.wait_ge(o_out, g)
                over_keys(bank[5], VS[g % 2][:, kt * HD:(kt + 1) * HD], PB[kt % 4], kt == 0,
                          kt == KT - 1).then_inc(pv_mm, 1)

            def total(g, j):
                pe.wait_ge(p_add, 4 * g + j + 1)
                if j == 0 and g > 0:
                    pe.wait_ge(sum_out, g)
                over_keys(bank[6], onesf[:, 0:HD], PS[j % 2], j == 0, j == KT // 2 - 1).then_inc(one_mm, 1)

            def loaded(g):
                pe.wait_ge(qk_in[g % 3], 96 * (g // 3 + 1))

            def group(g):
                for t in range(STEPS):
                    kt, h = divmod(t, REP)
                    if g + 1 < GROUPS:
                        if t == 0:
                            loaded(g + 1)
                        for n in ((2 * t, 2 * t + 1) if t < 4 else (t + 4,) if t < STEPS - 4 else ()):
                            score_step(g + 1, n)
                    if t < REP:
                        pe.wait_ge(nm_row, REP * g + t + 1)
                    if STEPS * g + t >= 2:
                        pe.wait_ge(exp_done, STEPS * g + t - 1)
                    pe.matmul(bank[2 + t % 2][:, :], KS[g % 3][0:98, kt * P:(kt + 1) * P],
                              QS[g % 3][0:98, h * S:(h + 1) * S], start=True, stop=True).then_inc(st_mm, 1)
                    if g + 1 < GROUPS and t % 8 == 6:
                        max_row(g + 1, t // 8)
                    if t >= 5 and t % 4 == 1:
                        weigh(g, t // 4 - 1)
                    if t % 8 == 7:
                        if t > 8:
                            total(g, t // 8 - 1)
                        elif g > 0:
                            total(g - 1, KT // 2 - 1)
                weigh(g, KT - 1)

            pe.wait_ge(q_lo, 1 + B * KT)
            pe.wait_ge(ones_row, 3)
            loaded(0)
            for h in range(REP):
                for n in range(8 * h, 8 * h + 8):
                    score_step(0, n)
                max_row(0, h)
            for g in range(GROUPS):
                group(g)
            total(GROUPS - 1, KT // 2 - 1)

            pe.wait_ge(o_step, O_STEPS * GROUPS)
            pe.wait_ge(wt_done, N_WT)
            token_phase(2 * TT, o_h, o_l, False)

            pe.wait_ge(x_up, 6 * TT)
            pe.wait_ge(t_lo, 6 * TT)
            pe.wait_ge(am_done, 4)
            pe.matmul(bank[1][:, 0:2 * TT], onesf[:, :], AM[:, :, :].rearrange("p a t -> p (a t)"), start=True,
                      stop=True).then_inc(as_mm, 1)
            for t in range(TT):
                for k in range(KT):
                    cols = slice(k * D + t * P, k * D + (t + 1) * P)
                    e3 = slice(k * EXPERTS, (k + 1) * EXPERTS)
                    mm = triple([bank[0][:, t * EXPERTS:(t + 1) * EXPERTS]], XTh[:, cols], XTl[:, cols],
                                [gwh[:, e3]], [gwl[:, e3]], k == 0, k == KT - 1)
            mm.then_inc(lg_mm, 1)
            pe.wait_ge(rt_step, RT_READ)

            with pe.Fori(0, B) as b:
                with pe.Fori(0, TOPK) as j:
                    s = b * TOPK + j
                    for f in range(KT):
                        pe.wait_ge(act_done, KT * s + (1 + max(f - 3, 0)))
                        for k in range(KT):
                            if f == 0:
                                pe.wait_ge(wt_done, W_O_END + 2 * KT * s + (k + 1))
                            cols = bass.ds(b * S + k * D, S)
                            w = slice(k * D + f * P, k * D + (f + 1) * P)
                            mm = triple([bank[f % 4][:, :]], w1_h[:, w], w1_l[:, w], [XTh[:, cols]], [XTl[:, cols]],
                                        k == 0, k == KT - 1)
                        mm.then_inc(a_mm, 1)
                    for i in range(TB):
                        pe.wait_ge(eo_done, 2 * TB * s + (1 + 2 * max(i - 1, 0)))
                        outs = [bank[4 + 2 * (i % 2)][:, :], bank[5 + 2 * (i % 2)][:, :]]
                        for f in range(KT):
                            if i == 0:
                                pe.wait_ge(e_lo, KT * s + (f + 2))
                                pe.wait_ge(wt_done, W_O_END + 2 * KT * s + (KT + f + 1))
                            cols = slice(f * S + i * P, f * S + (i + 1) * P)
                            mm = triple(outs, HT_h[:, cols], HT_l[:, cols],
                                        [w2_h[:, f * D + h * HALF:f * D + (h + 1) * HALF] for h in range(2)],
                                        [w2_l[:, f * D + h * HALF:f * D + (h + 1) * HALF] for h in range(2)],
                                        f == 0, f == KT - 1)
                        mm.then_inc(b_mm, 1)

        @block.scalar
        def _(act):
            for counted in (abs_done, act_done, *q_out):
                act.sem_inc(counted, 1)
            act.wait_ge(const_in, 64)
            act.activation(tg[:, :], sc[:, SC_GX:SC_GX + 4], ACT.Tanh).then_inc(tg_done, 1)

            def chunk_hi(n, k):
                act.wait_ge(c_in[n % 2], 16 * (n // 2 + 1))
                act.activation(ct_h[:, k * D:(k + 1) * D], stage_c[n % 2][:, :], ACT.Copy).then_inc(c_act, 1)

            for k in range(KT):
                chunk_hi(k, k)
            act.wait_ge(qc_step, 2)

            def root(n, par):
                act.wait_ge(ln_step, 8 * n + 4)
                act.activation(lnv[par][:, 1:2], lnv[par][:, 0:1], ACT.Sqrt).then_inc(ln_sd, 1)

            for t in range(TT):
                root(t, t % 2)
                act.wait_ge(xn_done, t + 1)
                act.activation(xn[t % 2][:, :], xn[t % 2][:, :], ACT.Identity, bias=sc[:, SC_Z1:SC_Z1 + 1],
                               scale=rs1[:, 0:1]).then_inc(xq_sc, 1)

            def kv_out(b):
                act.wait_ge(kv_mm, b + 1)
                for i in range(4):
                    act.activation(kb_h[:, i * HALF:(i + 1) * HALF], bank[i][:, :], ACT.Copy).then_inc(k_hi, 1)
                for i in range(2):
                    at_v = b * KT * KVD + i * HALF
                    act.activation(V[:, at_v:at_v + HALF], bank[4 + i][:, :], ACT.Copy).then_inc(v_act, 1)

            act.wait_ge(xq_done, TT)
            kv_out(0)
            for t in range(TT):
                act.wait_ge(xq_turned, t + 1)
                act.activation(XTh[:, :].rearrange("p (k n) -> p k n", k=KT)[:, :, t * P:(t + 1) * P],
                               bank_b[6 + t % 2].rearrange("p (k n) -> p k n", k=KT), ACT.Copy).then_inc(xq_t, 1)
            for n in range(KT, 3 * KT):
                act.wait_ge(c_in[n % 2], 16 * (n // 2 + 1))
                act.activation(stage_c[n % 2][:, :], stage_c[n % 2][:, :], ACT.Identity, bias=sc[:, SC_Z2:SC_Z2 + 1],
                               scale=rs2[:, 0:1]).then_inc(c_act, 1)
            act.wait_ge(kv_mm, 1)
            for k in range(KT):
                chunk_hi(3 * KT + k, k)

            def normalise(n, t, par, sums):
                root(n + TT, par)
                if sums:
                    act.wait_ge(xn_done, TT + n + 1)
                    act.wait_ge(abs_done, t + 1)
                    act.activation(junk, xn[par][:, :], ACT.Abs, accum_out=rowabs[:, bass.ds(t, 1)]).then_inc(abs_done, 1)
                act.wait_ge(turned, n + 1)
                for i in range(2):
                    act.activation(xt_tile(XTh, t, i), bank[4 + i][:, :].rearrange("p (k n) -> p k n", k=4),
                                   ACT.Copy).then_inc(t_hi, 1)

            def normalise_all(n0, sums):
                with act.Fori(0, TT // 2) as i:
                    for j in range(2):
                        normalise(2 * i + (n0 + j), 2 * i + j, j, sums)

            normalise_all(0, False)
            kv_out(1)

            act.wait_ge(co_step, 3)
            act.activation(coef[0:1, 1, :], coef[0:1, 2, :], ACT.Exp, scale=float(K_LORA) ** -0.5).then_inc(co_exp, 1)
            act.wait_ge(cv_done, 2)
            for u in range(B * JT):
                b, j = divmod(u, JT)
                act.wait_ge(h_mm, u + 1)
                act.activation(HT_h[:, j * D + b * S:j * D + (b + 1) * S], bank[u % 4][:, :], ACT.Copy,
                               scale=cvec[:, u:u + 1]).then_inc(h_hi, 1)
            normalise_all(TT, False)

            act.wait_ge(nat_mm, 2 * TT)
            with act.Fori(0, B) as b:
                for c in range(KT):
                    act.wait_ge(q_mm, KT * b + (c + 1))
                    act.wait_ge(q_out[c % 4], 64 * b + (1 + 32 * (c // 4)))
                    act.activation(qb_h[:, (c % 4) * S:(c % 4 + 1) * S], bank[c % 4][:, :], ACT.Copy).then_inc(q_hi, 1)

            def row_out(g, h):
                act.wait_ge(nm_turned, REP * g + h + 1)
                act.activation(QS[g % 3][96:98, h * S:(h + 1) * S], bank_b[4][96:98, 0:S], ACT.Copy).then_inc(nm_row, 1)

            def outputs_out(g):
                act.wait_ge(pv_mm, KT * (g + 1))
                if g >= 2:
                    act.wait_ge(o_step, O_STEPS * (g - 2) + 1)
                act.activation(o_raw[g % 2], bank[5][:, :], ACT.Copy).then_inc(o_out, 1)

            def sums_out(g):
                act.wait_ge(one_mm, 4 * (g + 1))
                if g > 0:
                    act.wait_ge(rec_done, 4 * g)
                act.activation(p_sum, bank[6][:, :], ACT.Copy).then_inc(sum_out, 1)

            def exp_group(g):
                for t in range(STEPS):
                    kt, h = divmod(t, REP)
                    act.wait_ge(st_mm, STEPS * g + t + 1)
                    if h == 0 and KT * g + kt >= 4:
                        act.wait_ge(pv_mm, KT * g + kt - 3)
                        act.wait_ge(p_add, (KT * g + kt - 4) // 2 + 1)
                    act.activation(PB[kt % 4][:, h * S:(h + 1) * S], bank[2 + t % 2][:, :], ACT.Exp,
                                   scale=float(HD) ** -0.5).then_inc(exp_done, 1)
                    if g + 1 < GROUPS and t % 8 == 6:
                        row_out(g + 1, t // 8)
                    if g > 0 and t == 2:
                        outputs_out(g - 1)
                    if g > 0 and t == 9:
                        sums_out(g - 1)

            act.wait_ge(q_mm, B * KT)
            for h in range(REP):
                row_out(0, h)
            act.wait_ge(nat_mm, 2 * TT)
            for g in range(GROUPS):
                exp_group(g)
            outputs_out(GROUPS - 1)
            sums_out(GROUPS - 1)

            normalise_all(2 * TT, True)

            act.wait_ge(rt_step, RT_SHIFTED)
            act.activation(G[:, :, :], L[:, :, :], ACT.Exp).then_inc(rt_exp, 1)

            act.wait_ge(idx_done, 1)
            reg = act.alloc_register("expert_act")
            with act.Fori(0, B) as b:
                with act.Fori(0, TOPK) as j:
                    s = b * TOPK + j
                    act.reg_load(reg, idx[0:1, bass.ds(s, 1)])
                    for e, func in enumerate((ACT.Tanh, ACT.Gelu, ACT.Silu)):
                        with act.If_eq(reg, e):
                            for f in range(KT):
                                act.wait_ge(a_mm, KT * s + (f + 2))
                                act.wait_ge(e_lo, KT * s + 1)
                                act.activation(hid[:, f * S:(f + 1) * S], bank[f % 4][:, :], func,
                                               bias=b1t[:, e * KT + f:e * KT + f + 1]).then_inc(act_done, 1)
                for i in range(TB):
                    act.wait_ge(x_fin, 4 * TB * b + (2 * TB + 2 * (i + 1) + 1))
                    t = b * TB + i
                    act.dma_start(out[bass.ds(t, 1)].rearrange("o p n -> (o p) n"), X[:, ds(t, D)]).then_inc(x_out, 16)

        @block.vector
        def _(dve):
            for counted in (q_lo, eo_done, e_lo, x_fin):
                dve.sem_inc(counted, 1)
            dve.wait_ge(made, 4)
            dve.tensor_copy(identb[:, :], identf[:, :]).then_inc(madeb, 1)
            dve.tensor_copy(onesb[:, :], onesf[:, :]).then_inc(madeb, 1)
            dve.wait_ge(const_in, 64)
            dve.reciprocal(rs1[:, :], sc[:, SC_S1:SC_S1 + 1]).then_inc(qc_step, 1)
            dve.reciprocal(rs2[:, :], sc[:, SC_S2:SC_S2 + 1]).then_inc(qc_step, 1)
            dve.tensor_copy(gwh[:, :], gwf[:, :]).then_inc(qc_step, 1)
            dve.wait_ge(qc_step, 3)
            dve.tensor_tensor(gwl[:, :], gwf[:, :], gwh[:, :], ALU.subtract).then_inc(qc_step, 1)
            dve.wait_ge(tg_done, 1)
            dve.tensor_tensor(qc[:, 0:1], sc[:, SC_S1:SC_S1 + 1], sc[:, SC_S2:SC_S2 + 1], ALU.mult).then_inc(qc_step, 1)
            dve.tensor_scalar(qc[:, 1:2], sc[:, SC_Z1:SC_Z1 + 1], -1.0, MID, ALU.mult, ALU.add).then_inc(qc_step, 1)
            dve.tensor_scalar(qc[:, 2:3], sc[:, SC_Z2:SC_Z2 + 1], -1.0, MID, ALU.mult, ALU.add).then_inc(qc_step, 1)
            dve.wait_ge(qc_step, 7)
            dve.tensor_scalar(qc[:, 6:7], qc[:, 0:1], tg[:, 0:1], None, ALU.mult).then_inc(qc_step, 1)
            dve.tensor_scalar(qc[:, 5:6], qc[:, 1:2], float(D), None, ALU.mult).then_inc(qc_step, 1)
            dve.wait_ge(qc_step, 9)
            dve.tensor_tensor(qc[:, 3:4], qc[:, 6:7], qc[:, 1:2], ALU.mult).then_inc(qc_step, 1)
            dve.tensor_tensor(qc[:, 4:5], qc[:, 6:7], qc[:, 2:3], ALU.mult).then_inc(qc_step, 1)

            def chunk_lo(n, k):
                dve.wait_ge(c_act, n + 1)
                cols = slice(k * D, (k + 1) * D)
                dve.tensor_tensor(ct_l[:, cols], stage_c[n % 2][:, :], ct_h[:, cols], ALU.subtract).then_inc(c_done, 1)

            for k in range(KT):
                chunk_lo(k, k)

            def carry_wait():
                dve.memset(carrier[:, :], 0.0)

            def normalise(n, xt, par, free):
                v = lnv[par]
                carry_wait()
                for h in range(2):
                    dve.bn_stats(stats[par][:, h, :], xt(h)).then_inc(ln_step, 1)
                dve.wait_ge(ln_step, 8 * n + 2)
                carry_wait()
                dve.bn_aggr(mv[par][:, :], stats[par][:, :, :]).then_inc(ln_step, 1)
                dve.wait_ge(ln_step, 8 * n + 3)
                dve.tensor_scalar(v[:, 0:1], mv[par][:, 1:2], EPS, None, ALU.add).then_inc(ln_step, 1)
                dve.wait_ge(ln_sd, n + 1)
                dve.reciprocal(v[:, 2:3], v[:, 1:2]).then_inc(ln_step, 1)
                dve.wait_ge(ln_step, 8 * n + 5)
                dve.scalar_tensor_tensor(out=v[:, 3:4], in0=v[:, 2:3], scalar=v[:, 2:3], in1=v[:, 0:1],
                                         op0=ALU.mult, op1=ALU.mult).then_inc(ln_step, 1)
                dve.wait_ge(ln_step, 8 * n + 6)
                dve.tensor_scalar(v[:, 4:5], v[:, 3:4], -0.5, 1.5, ALU.mult, ALU.add).then_inc(ln_step, 1)
                dve.wait_ge(ln_step, 8 * n + 7)
                dve.tensor_tensor(v[:, 5:6], v[:, 4:5], v[:, 2:3], ALU.mult).then_inc(ln_step, 1)
                dve.wait_ge(ln_step, 8 * n + 8)
                free()
                dve.tensor_scalar(xn[par][:, :], xt(None), mv[par][:, 0:1], v[:, 5:6], ALU.subtract,
                                  ALU.mult).then_inc(xn_done, 1)

            def clip_round(buf, dst, clip, n, done):
                dve.tensor_scalar(buf, buf, 0.0, QMAX, ALU.max, ALU.min).then_inc(clip, 1)
                dve.wait_ge(clip, n + 1)
                dve.tensor_scalar(dst, buf, MAGIC, MAGIC + MID, ALU.add, ALU.subtract).then_inc(done, 1)

            for t in range(TT):
                dve.wait_ge(x_in[t], 16)
                normalise(t, lambda h, t=t: X[:, t * D + (h or 0) * HALF:t * D + ((h or 0) + 1) * HALF] if h is not None
                          else X[:, t * D:(t + 1) * D], t % 2, lambda t=t: dve.wait_ge(xq_done, t - 1) if t >= 2 else None)
                dve.wait_ge(xq_sc, t + 1)
                clip_round(xn[t % 2][:, :], XQ[:, t * D:(t + 1) * D], xq_clip, t, xq_done)

            def kv_out(b):
                for i in range(2):
                    dve.wait_ge(kv_mm, b + 1)
                    at_v = b * KT * KVD + (2 + i) * HALF
                    dve.tensor_copy(V[:, at_v:at_v + HALF], bank[6 + i][:, :]).then_inc(v_dve, 1)
                for i in range(4):
                    dve.wait_ge(k_hi, 4 * b + i + 1)
                    cols = slice(i * HALF, (i + 1) * HALF)
                    dve.tensor_tensor(kb_l[:, cols], bank[i][:, :], kb_h[:, cols], ALU.subtract).then_inc(k_lo, 1)

            kv_out(0)
            for n in range(KT, 3 * KT):
                dve.wait_ge(c_act, n + 1)
                b, k = divmod(n - KT, KT)
                clip_round(stage_c[n % 2][:, :], Q2[b][:, k * D:(k + 1) * D], c_clip, n - KT, c_done)
            dve.wait_ge(row_mm, 1)
            dve.wait_ge(qc_step, 11)
            dve.tensor_scalar(rterm[:, :], bank[3][:, 0:TT], qc[:, 5:6], qc[:, 4:5], ALU.add, ALU.mult).then_inc(rterm_done, 1)
            for b in range(B):
                dve.wait_ge(cs_mm, b + 1)
                for h in range(2):
                    dve.tensor_scalar(CB[:, b, h * HALF:(h + 1) * HALF], bank[4 + 2 * b + h][:, :], qc[:, 3:4], None,
                                      ALU.mult).then_inc(cb_done, 1)
            for k in range(KT):
                chunk_lo(3 * KT + k, k)

            def lo_parts(n, t):
                for i in range(2):
                    dve.wait_ge(t_hi, 2 * n + (i + 1))
                    dve.tensor_tensor(xt_tile(XTl, t, i), bank[4 + i][:, :].rearrange("p (k n) -> p k n", k=4),
                                      xt_tile(XTh, t, i), ALU.subtract).then_inc(t_lo, 1)

            dve.wait_ge(rterm_done, 1)
            dve.wait_ge(cb_done, 4)
            dve.wait_ge(k_out, 32)
            for t in range(TT):
                xt = X[:, t * D:(t + 1) * D]
                dve.scalar_tensor_tensor(out=xt, in0=xt, scalar=rterm[:, t:t + 1], in1=CB[:, t // TB, :],
                                         op0=ALU.add, op1=ALU.add).then_inc(x_pre, 1)
                dve.wait_ge(x_pre, t + 1)
                dve.wait_ge(nat_mm, t + 1)
                for h in range(2):
                    xh = X[:, t * D + h * HALF:t * D + (h + 1) * HALF]
                    dve.scalar_tensor_tensor(out=xh, in0=bank[2 * (t % 2) + h][:, :], scalar=qc[:, 6:7], in1=xh,
                                             op0=ALU.mult, op1=ALU.add).then_inc(x_up, 1)
                dve.wait_ge(x_up, 2 * (t + 1))
                normalise(TT + t, lambda h, t=t: X[:, t * D + (h or 0) * HALF:t * D + ((h or 0) + 1) * HALF] if h is not None
                          else X[:, t * D:(t + 1) * D], t % 2, lambda t=t: dve.wait_ge(turned, t - 1) if t >= 2 else None)
                lo_parts(t, t)

            for part, src in enumerate((XTh, XTl)):
                for b in range(B):
                    dve.tensor_reduce(msum[:, part, b * KT:(b + 1) * KT],
                                      src[:, :].rearrange("p (k n) -> p k n", k=KT)[:, :, b * S:(b + 1) * S],
                                      AX.X, ALU.add).then_inc(mean_step, 1)
                    if part == 0 and b == 0:
                        dve.wait_ge(t_lo, 2 * TT)
            dve.wait_ge(mean_step, 2 * B)
            dve.tensor_tensor(msum[:, 0, :], msum[:, 0, :], msum[:, 1, :], ALU.add).then_inc(mean_step, 1)
            dve.wait_ge(mean_step, 2 * B + 1)
            dve.tensor_scalar(mean[:, :, :].rearrange("p b k -> p (b k)"), msum[:, 0, :], 1.0 / S, None,
                              ALU.mult).then_inc(mean_step, 1)
            kv_out(1)

            dve.wait_ge(lq_mm, 1)
            dve.tensor_copy(lq[:, :], bank[4][:, 0:B]).then_inc(co_step, 1)
            dve.wait_ge(sc_mm, 1)
            c3 = [coef[0:1, i, :].rearrange("p (b e) -> p b e", b=B) for i in range(4)]
            s5 = bank[5][0:1, 0:B * E_LORA].rearrange("p (b e) -> p b e", b=B)

            def over_e(col):
                return coefs[0:1, col:col + B].rearrange("p (b o) -> p b o", o=1).to_broadcast([1, B, E_LORA])

            dve.tensor_reduce(coefs[0:1, 0:B], s5, AX.X, ALU.max).then_inc(co_step, 1)
            dve.wait_ge(co_step, 2)
            dve.tensor_tensor(c3[2], s5, over_e(0), ALU.subtract).then_inc(co_step, 1)
            dve.wait_ge(co_exp, 1)
            dve.tensor_reduce(coefs[0:1, B:2 * B], c3[1], AX.X, ALU.add).then_inc(co_step, 1)
            dve.wait_ge(co_step, 4)
            dve.reciprocal(coefs[0:1, 2 * B:3 * B], coefs[0:1, B:2 * B]).then_inc(co_step, 1)
            dve.wait_ge(co_step, 5)
            dve.tensor_tensor(c3[3], c3[1], over_e(2 * B), ALU.mult).then_inc(co_step, 1)
            dve.wait_ge(bc_mm, 1)
            for i in range(2):
                rows = slice(i * R_LORA, (i + 1) * R_LORA)
                dve.tensor_copy(cvec[rows, :], bank[6][rows, i:B * E_LORA:2]).then_inc(cv_done, 1)
            dve.wait_ge(cv_done, 2)
            for u in range(B * JT):
                b, j = divmod(u, JT)
                cols = slice(j * D + b * S, j * D + (b + 1) * S)
                dve.wait_ge(h_hi, u + 1)
                dve.scalar_tensor_tensor(out=HT_l[:, cols], in0=bank[u % 4][:, :], scalar=cvec[:, u:u + 1],
                                         in1=HT_h[:, cols], op0=ALU.mult, op1=ALU.subtract).then_inc(h_lo, 1)

            def token_phase(m0, gain, sums):
                with dve.Fori(0, TT // 2) as i:
                    for j in range(2):
                        t, m = 2 * i + j, 2 * i + (m0 + j)
                        dve.wait_ge(nat_mm, m + 1)
                        for h in range(2):
                            xh = X[:, bass.ds(t * D + h * HALF, HALF)]
                            dve.scalar_tensor_tensor(out=xh, in0=bank[2 * j + h][:, :], scalar=gain, in1=xh,
                                                     op0=ALU.mult, op1=ALU.add).then_inc(x_up, 1)
                        dve.wait_ge(x_up, 2 * (m + 1))

                        def free(m=m, t=t):
                            dve.wait_ge(turned, m - 1)
                            if sums:
                                dve.wait_ge(abs_done, t + 1)

                        normalise(m + TT, lambda h, t=t: X[:, bass.ds(t * D, D)] if h is None
                                  else X[:, bass.ds(t * D + h * HALF, HALF)], j, free)
                        lo_parts(m, t)

            dve.wait_ge(k_out, 64)
            token_phase(TT, tg[:, 2:3], False)

            with dve.Fori(0, B) as b:
                for c in range(KT):
                    cols = slice((c % 4) * S, (c % 4 + 1) * S)
                    dve.wait_ge(q_hi, KT * b + (c + 1))
                    dve.tensor_tensor(qb_l[:, cols], bank[c % 4][:, :], qb_h[:, cols], ALU.subtract).then_inc(q_lo, 1)

            dve.wait_ge(q_mm, B * KT)
            for ks in KS:
                dve.memset(ks[96:98, :], 1.0).then_inc(ones_row, 1)

            def invert(g, quarter):
                cols = slice(quarter * S // 4, (quarter + 1) * S // 4)
                if quarter == 0:
                    dve.wait_ge(sum_out, g + 1)
                    if g > 0:
                        dve.wait_ge(o_step, O_STEPS * (g - 1) + 1)
                dve.reciprocal(rec[:, cols], p_sum[:, cols]).then_inc(rec_done, 1)

            for g in range(GROUPS):
                for h in range(REP):
                    u = REP * g + h
                    for n in range(8 * h, 8 * h + 8):
                        dve.wait_ge(s_mm, STEPS * g + n + 1)
                        dve.tensor_reduce(mxp[:, h % 2, n // 2 % 4, n % 2:n % 2 + 1],
                                          bank[s_bank[(STEPS * g + n) % 3]][:, :], AX.X,
                                          ALU.max).then_inc(s_max, 1)
                        if g >= 2 and n >= STEPS // 2 and n % 4 == 2:
                            invert(g - 2, n // 4 - 4)
                    dve.wait_ge(s_max, STEPS * g + 8 * h + 8)
                    dve.tensor_tensor(mxc[:, h % 2, :], mxp[:, h % 2, :, 0], mxp[:, h % 2, :, 1], ALU.max).then_inc(nm_step, 1)
                    if u >= 2:
                        dve.wait_ge(nm_turned, u - 1)
                    dve.wait_ge(nm_step, 3 * u + 1)
                    dve.tensor_scalar(nm[:, h % 2, :, 0], mxc[:, h % 2, :], -1.0, None, ALU.mult).then_inc(nm_step, 1)
                    dve.wait_ge(nm_step, 3 * u + 2)
                    dve.scalar_tensor_tensor(out=nm[:, h % 2, :, 1], in0=mxc[:, h % 2, :], scalar=-1.0,
                                             in1=nm[:, h % 2, :, 0], op0=ALU.mult, op1=ALU.subtract).then_inc(nm_step, 1)
            for g in (GROUPS - 2, GROUPS - 1):
                for quarter in range(4):
                    invert(g, quarter)

            token_phase(2 * TT, tg[:, 1:2], True)

            dve.wait_ge(abs_done, 1 + TT)
            dve.memset(AM[:, 0, :], 0.0).then_inc(am_done, 1)
            dve.wait_ge(am_done, 1)
            dve.tensor_copy(AM[:, 0, 0:TT:TB], rowabs[:, 0:TT:TB]).then_inc(am_done, 1)
            dve.tensor_copy(AM[0:VISION - P, 0, 1:TT:TB], rowabs[0:VISION - P, 1:TT:TB]).then_inc(am_done, 1)
            dve.wait_ge(am_done, 3)
            dve.tensor_tensor(AM[:, 1, :], rowabs[:, :], AM[:, 0, :], ALU.subtract).then_inc(am_done, 1)

            done = [0]

            def nxt(instruction, after=None):
                instruction.then_inc(rt_step, 1)
                done[0] += 1
                dve.wait_ge(rt_step, done[0])

            dve.wait_ge(as_mm, 1)
            nxt(dve.tensor_reduce(AS[:, :, :].rearrange("p a b -> p (a b)"),
                                  bank[1][:, 0:2 * TT].rearrange("p (a t) -> p a t", t=TB), AX.X, ALU.add))
            nxt(dve.tensor_scalar(rt[:, 0:2], AS[:, 0, :], 1.0 / (VISION * D), 1e-8, ALU.mult, ALU.add))
            nxt(dve.reciprocal(rt[:, 2:4], rt[:, 0:2]))
            nxt(dve.tensor_scalar(rt[:, 4:6], AS[:, 1, :], 1.0 / ((S - VISION) * D), None, ALU.mult))
            nxt(dve.tensor_tensor(rt[:, 6:8], rt[:, 4:6], rt[:, 2:4], ALU.mult))
            for b in range(B):
                nxt(dve.scalar_tensor_tensor(out=rb[:, b, :], in0=sc[:, SC_GL:SC_GL + EXPERTS], scalar=rt[:, 6 + b:7 + b],
                                             in1=sc[:, SC_GB:SC_GB + EXPERTS], op0=ALU.mult, op1=ALU.add))
            dve.wait_ge(lg_mm, 1)
            for b in range(B):
                nxt(dve.tensor_tensor(L[:, b * TB:(b + 1) * TB, :],
                                      bank[0][:, b * TB * EXPERTS:(b + 1) * TB * EXPERTS].rearrange("p (t e) -> p t e", e=EXPERTS),
                                      rb[:, b:b + 1, :].to_broadcast([P, TB, EXPERTS]), ALU.add))
            assert done[0] == RT_READ

            def over_experts(v):
                return v.rearrange("p (t o) -> p t o", o=1).to_broadcast([P, TT, EXPERTS])

            nxt(dve.tensor_reduce(rv[:, 0, :], L[:, :, :], AX.X, ALU.max))
            nxt(dve.tensor_tensor(L[:, :, :], L[:, :, :], over_experts(rv[:, 0, :]), ALU.subtract))
            assert done[0] == RT_SHIFTED
            dve.wait_ge(rt_exp, 1)
            nxt(dve.tensor_reduce(rv[:, 1, :], G[:, :, :], AX.X, ALU.add))
            nxt(dve.reciprocal(rv[:, 2, :], rv[:, 1, :]))
            nxt(dve.tensor_tensor(G[:, :, :], G[:, :, :], over_experts(rv[:, 2, :]), ALU.mult))
            g0, g1, g2 = (G[:, :, e] for e in range(EXPERTS))
            nxt(dve.tensor_tensor(rv[:, 3, :], g0, g1, ALU.max))
            nxt(dve.tensor_tensor(rv[:, 4, :], g0, g1, ALU.min))
            nxt(dve.tensor_tensor(rv[:, 5, :], rv[:, 3, :], g2, ALU.max))
            nxt(dve.tensor_tensor(rv[:, 3, :], rv[:, 3, :], g2, ALU.min))
            nxt(dve.tensor_tensor(rv[:, 6, :], rv[:, 3, :], rv[:, 4, :], ALU.max))
            nxt(dve.tensor_tensor(rv[:, 7, :], rv[:, 5, :], rv[:, 6, :], ALU.add))
            nxt(dve.tensor_scalar(rv[:, 7, :], rv[:, 7, :], 1e-8, None, ALU.add))
            nxt(dve.reciprocal(rv[:, 8, :], rv[:, 7, :]))
            nxt(dve.tensor_scalar(rv[:, 8, :], rv[:, 8, :], tg[:, 3:4], None, ALU.mult))
            for j in range(TOPK):
                nxt(dve.tensor_tensor(TV[:, j * TT:(j + 1) * TT], rv[:, 5 + j, :], rv[:, 8, :], ALU.mult))
            f0, f1, f2 = (G[0:1, 0:TT:TB, e] for e in range(EXPERTS))
            nxt(dve.tensor_tensor(rk[0:1, 0, :], f0, f1, ALU.is_ge))
            nxt(dve.tensor_tensor(rk[0:1, 1, :], f0, f2, ALU.is_ge))
            nxt(dve.tensor_tensor(rk[0:1, 2, :], f1, f2, ALU.is_ge))
            nxt(dve.tensor_tensor(rk[0:1, 3, :], rk[0:1, 0, :], rk[0:1, 2, :], ALU.subtract))
            nxt(dve.tensor_scalar(rk[0:1, 3, :], rk[0:1, 3, :], 1.0, None, ALU.add))
            nxt(dve.tensor_tensor(rk[0:1, 4, :], rk[0:1, 1, :], rk[0:1, 2, :], ALU.add))
            for j in range(TOPK):
                nxt(dve.tensor_scalar(rk[0:1, 5, :], rk[0:1, 3, :], float(j), None, ALU.is_equal))
                nxt(dve.tensor_scalar(rk[0:1, 6, :], rk[0:1, 4, :], float(j), 2.0, ALU.is_equal, ALU.mult))
                nxt(dve.tensor_tensor(idxf[0:1, :, j], rk[0:1, 5, :], rk[0:1, 6, :], ALU.add))
            dve.tensor_copy(idx[:, :], idxf[:, :, :].rearrange("p b j -> p (b j)")).then_inc(idx_done, 1)

            with dve.Fori(0, B) as b:
                with dve.Fori(0, TOPK) as j:
                    s = b * TOPK + j
                    for f in range(KT):
                        cols = slice(f * S, (f + 1) * S)
                        dve.wait_ge(act_done, KT * s + (f + 2))
                        dve.tensor_copy(HT_h[:, cols], hid[:, cols]).then_inc(e_hi, 1)
                        dve.wait_ge(e_hi, KT * s + (f + 1))
                        dve.tensor_tensor(HT_l[:, cols], hid[:, cols], HT_h[:, cols], ALU.subtract).then_inc(e_lo, 1)
                    dve.wait_ge(b2_in, 16 * s + 16)
                    dve.wait_ge(x_fin, 2 * TB * s + 1)
                    for i in range(TB):
                        dve.wait_ge(b_mm, TB * s + (i + 2))
                        t = b * TB + i
                        for h in range(2):
                            hc = slice(h * HALF, (h + 1) * HALF)
                            xh = X[:, bass.ds(t * D + h * HALF, HALF)]
                            dve.tensor_tensor(eo[h], bank[4 + 2 * (i % 2) + h][:, :], b2b[:, hc], ALU.add).then_inc(eo_done, 1)
                            dve.wait_ge(eo_done, 2 * TB * s + (2 * i + h + 2))
                            dve.scalar_tensor_tensor(out=xh, in0=eo[h], scalar=TV[:, bass.ds(j * TT + t, 1)], in1=xh,
                                                     op0=ALU.mult, op1=ALU.add).then_inc(x_fin, 1)

    return nc


_SHAPES = {"x": (TT, P, D), "ctx_nat": (B, KT, P, D), "ctx_t": (B, KT, P, SC), "wts": (N_WT, P, D),
           "lora_q": (P, KT * P), "lora_keys": (P, E_LORA), "scalars": (1, N_SC), "gate_w": (P, KT * EXPERTS),
           "w1": (EXPERTS, KT, P, D), "b1": (P, EXPERTS * KT), "w2": (EXPERTS, KT, P, D), "b2": (EXPERTS, D)}


def kernel(**a):
    import concourse.bacc as bacc
    from concourse.bass_utils import run_bass_kernel_spmd

    a = {k: np.asarray(v) for k, v in a.items()}

    def chunks(w):
        n = D // w.shape[1]
        return w.reshape(-1, n, P, w.shape[1]).transpose(0, 2, 1, 3).reshape(-1, P, D)

    arrays = {
        "x": a["x"].reshape(TT, P, D),
        "ctx_nat": a["ctx_4096"].reshape(B, KT, P, D),
        "ctx_t": a["ctx_4096"].transpose(0, 2, 1).reshape(B, KT, P, SC),
        "wts": np.concatenate([
            chunks(np.concatenate([a["L1_xattn_Wk"], a["L1_xattn_Wv"]], axis=1)),
            chunks(a["L0_ffn_lora_down"].transpose(1, 0, 2).reshape(D, ER)),
            chunks(a["L0_ffn_W_org"].T),
            chunks(a["L0_ffn_lora_up"].reshape(ER, D)),
            chunks(a["L1_xattn_Wq"]),
            chunks(a["L1_xattn_Wo"])]),
        "lora_q": a["L0_ffn_Wq"].T.reshape(KT, P, K_LORA).transpose(1, 0, 2).reshape(P, KT * P),
        "lora_keys": a["L0_ffn_lora_keys"].T,
        "scalars": np.concatenate([
            a["L0_xattn_x1_scale"], a["L0_xattn_x1_zp"], a["L0_xattn_x2_scale"], a["L0_xattn_x2_zp"],
            a["g_xattn"], a["g_ffn"], a["L1_ffn_gate_b"], a["L1_ffn_gate_w"][D]]).reshape(1, N_SC),
        "gate_w": a["L1_ffn_gate_w"][:D].reshape(KT, P, EXPERTS).transpose(1, 0, 2).reshape(P, KT * EXPERTS),
        "w1": a["L1_ffn_w1"].reshape(EXPERTS, KT, P, D),
        "b1": a["L1_ffn_b1"].reshape(EXPERTS, KT, P).transpose(2, 0, 1).reshape(P, EXPERTS * KT),
        "w2": a["L1_ffn_w2"].reshape(EXPERTS, KT, P, D),
        "b2": a["L1_ffn_b2"],
    }
    nc = bacc.Bacc("TRN2", target_bir_lowering=False, num_devices=1)
    arrays = {k: np.ascontiguousarray(v) for k, v in arrays.items()}
    args = [nc.dram_tensor(f"{k}_in", _SHAPES[k], F32, kind="ExternalInput").ap() for k in _SHAPES]
    args.append(nc.dram_tensor("y_out", (TT, P, D), F32, kind="ExternalOutput").ap())
    build(nc, *args)
    r = run_bass_kernel_spmd(nc, [{f"{k}_in": arrays[k] for k in _SHAPES}], core_ids=[0])
    return r.results[0]["y_out"].reshape(B, S, D)
```

```python
from contextlib import ExitStack

import numpy as np
import concourse.bass as bass
from concourse import mybir

F32 = mybir.dt.float32
BF16 = mybir.dt.bfloat16
I32 = mybir.dt.int32
ALU = mybir.AluOpType
ACT = mybir.ActivationFunctionType
AX = mybir.AxisListType

P = 128
B, S, D = 2, 512, 1024
SC = 1024
KT = D // P
TT = B * S // P
TB = S // P
HALF = 512
E_LORA, R_LORA, K_LORA = 8, 64, 128
ER = E_LORA * R_LORA
JT = ER // P
HEADS, KV_HEADS, HD = 32, 8, 32
REP = HEADS // KV_HEADS
KVD = KV_HEADS * HD
GROUPS = B * KV_HEADS
STEPS = REP * SC // P
EXPERTS, TOPK = 3, 2
SLOTS = B * TOPK
VISION = int(S * 0.3)
MAGIC = 1.5 * 2.0 ** 23
MID = 128.0
QMAX = 255.0
EPS = 1e-5
WT_LAYOUT = [("kv", 4), ("down", 4), ("org", 8), ("up", 4), ("q", 8), ("o", 8)]
N_WT = sum(n for _, n in WT_LAYOUT)
WT_AT = {name: sum(n for _, n in WT_LAYOUT[:i]) for i, (name, _) in enumerate(WT_LAYOUT)}
SC_S1, SC_Z1, SC_S2, SC_Z2, SC_GX, SC_GF, SC_GB, SC_GL = 0, 1, 2, 3, 4, 6, 8, 11
N_SC = 14
RT_READ = 5 + 2 * B
O_STEPS = 3
RT_SHIFTED = RT_READ + 2


CHUNKS = [("T", 0, k) for k in range(KT)] + [("T", 1, 0), ("T", 1, 1)]
for _k in range(KT):
    CHUNKS += [("N", *divmod(2 * _k + j, KT)) for j in range(2)] + ([("T", 1, _k + 2)] if _k + 2 < KT else [])
RING = 6
CH0 = 2


Q_BANKS = (2, 3, 5, 6)
Q_S = 4
Q_TURN = {7: 0, 10: 1, 12: 2, 15: 3}


def scores_in(item):
    return range(3 * (item - Q_S), min(3 * (item - Q_S) + 3, STEPS)) if item >= Q_S else range(0)


TURN_AT = {10: 0, 18: 1, 26: 2}
LAST_TURN = 2


def ds(i, n):
    return bass.ds(i * n, n)


def per_tile(v):
    return v[:, :].rearrange("p (k n) -> p k n", k=KT)


def xt_tile(xt, t, i):
    return per_tile(xt)[:, 4 * i:4 * i + 4, ds(t, P)]


def build(nc, x, ctx_nat, ctx_t, wts, lora_q, lora_keys, scalars, gate_w, w1, b1, w2, b2, out):
    with ExitStack() as ctx:
        def sb(name, shape, dt):
            return ctx.enter_context(nc.sbuf_tensor(name, shape, dt))

        def sem(name):
            return ctx.enter_context(nc.semaphore(name))

        X = sb("X", [P, TT * D], F32)
        XTh = sb("XTh", [P, KT * TT * P], BF16)
        XTl = sb("XTl", [P, KT * TT * P], BF16)
        R = [sb(f"R{i}", [P, KT * D], BF16) for i in range(6)]
        V = sb("V", [P, B * KT * KVD], F32)
        stage_w = [sb(f"stage_w{i}", [P, D], F32) for i in range(2)]
        stage_c = [sb(f"stage_c{i}", [P, D], F32) for i in range(2)]
        xn = [sb(f"xn{i}", [P, D], F32) for i in range(2)]
        identf = sb("identf", [P, P], F32)
        identb = sb("identb", [P, P], BF16)
        onesf = sb("onesf", [P, P], F32)
        onesb = sb("onesb", [P, P], BF16)
        zero = sb("zero", [P, 1], F32)
        sc = sb("sc", [P, N_SC], F32)
        rs1 = sb("rs1", [P, 1], F32)
        rs2 = sb("rs2", [P, 1], F32)
        tg = sb("tg", [P, 4], F32)
        qc = sb("qc", [P, 8], F32)
        stats = [sb(f"stats{i}", [P, 2, 6], F32) for i in range(2)]
        mv = [sb(f"mv{i}", [P, 2], F32) for i in range(2)]
        lnv = [sb(f"lnv{i}", [P, 6], F32) for i in range(2)]
        carrier = sb("carrier", [P, 1], F32)
        rterm = sb("rterm", [P, TT], F32)
        rowq = sb("rowq", [P, TT], F32)
        mean = sb("mean", [P, B, KT], F32)
        lq = sb("lq", [P, B], F32)
        keys = sb("keys", [P, E_LORA], F32)
        coef = sb("coef", [1, 4, B * E_LORA], F32)
        coefs = sb("coefs", [1, 8], F32)
        cvec = sb("cvec", [P, B * JT], F32)
        mxp = sb("mxp", [P, 2, TB, 2], F32)
        mxc = sb("mxc", [P, 2, TB], F32)
        nm = sb("nm", [P, 2, TB, 2], BF16)
        gwf = sb("gwf", [P, KT * EXPERTS], F32)
        gwh = sb("gwh", [P, KT * EXPERTS], BF16)
        gwl = sb("gwl", [P, KT * EXPERTS], BF16)
        b1t = sb("b1t", [P, EXPERTS * KT], F32)
        rowabs = sb("rowabs", [P, TT], F32)
        AM = sb("AM", [P, 2, TT], F32)
        AS = sb("AS", [P, 2, B], F32)
        rt = sb("rt", [P, 8], F32)
        rb = sb("rb", [P, B, EXPERTS], F32)
        L = sb("L", [P, TT, EXPERTS], F32)
        G = sb("G", [P, TT, EXPERTS], F32)
        rv = sb("rv", [P, 9, TT], F32)
        TV = sb("TV", [P, TOPK * TT], F32)
        rk = sb("rk", [1, 9, B], F32)
        idxf = sb("idxf", [1, B, TOPK], F32)
        idx = sb("idx", [1, B * TOPK], I32)

        half_r = KT * D // 2
        kv_h, kv_l = R[0][:, 0:half_r], R[0][:, half_r:]
        down_h, down_l = R[0][:, 0:half_r], R[0][:, half_r:]
        ct_h, ct_l = R[2], R[3]
        Q2 = [R[4], R[5]]
        XQ = XTl
        ring = [st[:, :] for st in stage_c] + [XTh[:, :].bitcast(F32)[:, i * D:(i + 1) * D] for i in range(RING - 2)]
        kb = [[R[1][:, b * half_r + i * 2 * SC:b * half_r + (i + 1) * 2 * SC] for i in range(2)] for b in range(B)]
        junk_q = R[1][:, half_r:half_r + D]
        CB = R[1][:, 0:half_r].bitcast(F32).rearrange("p (b n) -> p b n", b=B)
        org_h, org_l = R[2], R[3]
        up_h, up_l = R[1][:, 0:half_r], R[1][:, half_r:]
        HT_h, HT_l = R[4][:, 0:half_r], R[4][:, half_r:]
        LQW = R[5][:, 0:2 * KT * P].bitcast(F32)
        q_h, q_l = R[0], R[5]
        qb_h, qb_l = R[4][:, 0:half_r], R[4][:, half_r:]
        o_h, o_l = R[2], R[3]
        PB = [R[i // 2][:, :].bitcast(F32)[:, (i % 2) * REP * S:(i % 2 + 1) * REP * S] for i in range(4)]
        QS = [stage_c[1][:, :].bitcast(BF16)] + [R[5][:, i * REP * S:(i + 1) * REP * S] for i in range(2)]
        KS = [xn[0][:, S:].bitcast(BF16)] + [R[5][:, 2 * REP * S + i * SC:2 * REP * S + (i + 1) * SC] for i in range(2)]
        at = 2 * REP * S + 2 * SC
        VS = [R[5][:, at + i * 2 * KT * HD:at + (i + 1) * 2 * KT * HD].bitcast(F32) for i in range(2)]
        PS = [R[4][:, :].bitcast(F32)[:, i * REP * S:(i + 1) * REP * S] for i in range(2)]
        o_raw = [stage_c[0][:, i * S:(i + 1) * S] for i in range(2)]
        p_sum = xn[0][:, 0:S]
        s_bank = (0, 1, 7)
        rec, onat = xn[1][:, 0:S], xn[1][:, S:]
        w1_h, w1_l, w2_h, w2_l = R[0], R[1], R[2], R[3]
        hid = R[5][:, :].bitcast(F32)
        b2b = xn[0]
        eo = [xn[1][:, 0:HALF], xn[1][:, HALF:]]
        junk = R[0][:, 0:D]

        bank = [ctx.enter_context(nc.psum_tensor(f"bank{i}", [P, HALF], F32)) for i in range(8)]
        bank_b = [b[:, :].bitcast(BF16) for b in bank]

        k_scr = nc.dram_tensor("k_scr", [B, 2, KVD, SC], BF16, kind="Internal").ap()
        q_scr = nc.dram_tensor("q_scr", [KT, B, 2, P, S], BF16, kind="Internal").ap()

        const_in = sem("const_in")
        w_in = [sem(f"w_in{i}") for i in range(2)]
        c_in = [sem(f"c_in{i}") for i in range(RING)]
        x_in = [sem(f"x_in{i}") for i in range(TT)]
        lqw_in = sem("lqw_in")
        wt_hi = sem("wt_hi")
        wt_done = sem("wt_done")
        made = sem("made")
        madeb = sem("madeb")
        qc_step = sem("qc_step")
        tg_done = sem("tg_done")
        c_act = sem("c_act")
        c_clip = sem("c_clip")
        c_done = sem("c_done")
        ln_step = sem("ln_step")
        ln_sd = sem("ln_sd")
        xn_done = sem("xn_done")
        xq_sc = sem("xq_sc")
        xq_clip = sem("xq_clip")
        xq_done = sem("xq_done")
        xq_turned = sem("xq_turned")
        xq_t = sem("xq_t")
        kv_step = sem("kv_step")
        rowq_done = sem("rowq_done")
        mean_mm = sem("mean_mm")
        k_hi = sem("k_hi")
        k_lo = sem("k_lo")
        v_act = sem("v_act")
        v_dve = sem("v_dve")
        k_out = sem("k_out")
        cs_mm = sem("cs_mm")
        cb_done = sem("cb_done")
        rterm_done = sem("rterm_done")
        x_pre = sem("x_pre")
        nat_mm = sem("nat_mm")
        x_up = sem("x_up")
        turned = sem("turned")
        t_hi = sem("t_hi")
        t_lo = sem("t_lo")
        mean_step = sem("mean_step")
        lq_mm = sem("lq_mm")
        sc_mm = sem("sc_mm")
        bc_mm = sem("bc_mm")
        co_step = sem("co_step")
        co_exp = sem("co_exp")
        cv_done = sem("cv_done")
        h_mm = sem("h_mm")
        h_hi = sem("h_hi")
        h_lo = sem("h_lo")
        q_mm = sem("q_mm")
        q_hi = sem("q_hi")
        q_lo = sem("q_lo")
        q_out = [sem(f"q_out{i}") for i in range(4)]
        minus_row = sem("minus_row")
        qk_in = [sem(f"qk_in{i}") for i in range(3)]
        vs_done = sem("vs_done")
        s_mm = sem("s_mm")
        s_max = sem("s_max")
        nm_step = sem("nm_step")
        nm_turned = sem("nm_turned")
        nm_row = sem("nm_row")
        st_mm = sem("st_mm")
        exp_done = sem("exp_done")
        pv_mm = sem("pv_mm")
        p_add = sem("p_add")
        one_mm = sem("one_mm")
        o_out = sem("o_out")
        sum_out = sem("sum_out")
        rec_done = sem("rec_done")
        o_step = sem("o_step")
        abs_done = sem("abs_done")
        lg_mm = sem("lg_mm")
        as_mm = sem("as_mm")
        am_done = sem("am_done")
        rt_step = sem("rt_step")
        rt_exp = sem("rt_exp")
        idx_done = sem("idx_done")
        a_mm = sem("a_mm")
        act_done = sem("act_done")
        e_hi = sem("e_hi")
        e_lo = sem("e_lo")
        b2_in = sem("b2_in")
        ew_hi = sem("ew_hi")
        b_mm = sem("b_mm")
        eo_done = sem("eo_done")
        x_fin = sem("x_fin")
        x_out = sem("x_out")

        block = ctx.enter_context(nc.Block())

        def W1_N(s):
            return N_WT + 2 * KT * s


        @block.sync
        def _(sp):
            sp.dma_start(sc[:, :], scalars.to_broadcast([P, N_SC])).then_inc(const_in, 16)
            sp.dma_start(keys[:, :], lora_keys).then_inc(const_in, 16)
            sp.dma_start(gwf[:, :], gate_w).then_inc(const_in, 16)
            sp.dma_start(b1t[:, :], b1).then_inc(const_in, 16)

            def load_weights(first, count):
                for n in range(first, first + count):
                    if n >= 2:
                        sp.wait_ge(wt_done, n - 1)
                    sp.dma_start(stage_w[n % 2][:, :], wts[n]).then_inc(w_in[n % 2], 16)

            def load_context(count):
                for _ in range(count):
                    n = loaded[0]
                    loaded[0] += 1
                    if n >= RING:
                        sp.wait_ge(c_done, n - RING + 1)
                    kind, b, k = CHUNKS[n]
                    sp.dma_start(ring[n % RING], (ctx_t if kind == "T" else ctx_nat)[b, k]).then_inc(c_in[n % RING], 16)

            def load_x(t):
                sp.dma_start(X[:, t * D:(t + 1) * D], x[t]).then_inc(x_in[t], 16)

            loaded = [0]
            load_weights(WT_AT["kv"], 1)
            load_context(2)
            load_weights(WT_AT["kv"] + 1, 1)
            load_x(0)
            load_context(2)
            load_x(1)
            load_weights(WT_AT["kv"] + 2, 1)
            load_context(1)
            load_x(2)
            load_weights(WT_AT["kv"] + 3, 1)
            for t in range(3, TT):
                load_context(1)
                load_x(t)

            def keys_out(b):
                sp.wait_ge(k_lo, 4 * (b + 1))
                for part, src in enumerate(kb[b]):
                    sp.dma_start(k_scr[b, part].rearrange("(c p) s -> p c s", c=2),
                                 src.rearrange("p (c s) -> p c s", c=2)).then_inc(k_out, 16)

            load_context(RING)
            keys_out(0)
            load_context(len(CHUNKS) - loaded[0])
            load_weights(WT_AT["down"], 4)
            load_weights(WT_AT["org"], 2)
            keys_out(1)
            load_weights(WT_AT["org"] + 2, 4)
            sp.wait_ge(nat_mm, TT)
            sp.dma_start(LQW, lora_q).then_inc(lqw_in, 16)
            load_weights(WT_AT["org"] + 6, 2)
            load_weights(WT_AT["up"], 4)
            load_weights(WT_AT["q"], 8)

            def queries_out(b, c):
                sp.wait_ge(q_lo, KT * b + c + 1)
                for part, src in enumerate((qb_h, qb_l)):
                    sp.dma_start(q_scr[c, bass.ds(b, 1), part].rearrange("o p s -> (o p) s"),
                                 src[:, (c % 4) * S:(c % 4 + 1) * S]).then_inc(q_out[c % 4], 16)

            def group_in(g):
                kv, b = divmod(g, B)
                if g >= 3:
                    sp.wait_ge(st_mm, STEPS * (g - 2))
                for row, part in ((0, 0), (32, 0), (64, 1)):
                    sp.dma_start(QS[g % 3][row:row + HD, :].rearrange("p (h s) -> p h s", h=REP),
                                 q_scr[kv, b, part].rearrange("(h d) s -> d h s", h=REP)).then_inc(qk_in[g % 3], 16)
                for row, part in ((0, 0), (32, 1), (64, 0)):
                    sp.dma_start(KS[g % 3][row:row + HD, :],
                                 k_scr[b, part, ds(kv, HD), :]).then_inc(qk_in[g % 3], 16)

            for b in range(B):
                for c in range(KT):
                    queries_out(b, c)
                    if c % 2 == 1:
                        load_weights(WT_AT["o"] + (b * KT + c) // 2, 1)
                    if b == 0 and c == 1:
                        sp.wait_ge(k_out, 16 * 2 * B)
                        sp.wait_ge(q_out[0], 16 * 2)
                        group_in(0)
            for slot in range(4):
                sp.wait_ge(q_out[slot], 16 * 2 * B * KT // 4)
            sp.wait_ge(q_mm, B * KT)
            for g in range(1, GROUPS):
                group_in(g)

            sp.wait_ge(idx_done, 1)
            reg = sp.alloc_register("expert_sp")

            def expert(s):
                sp.reg_load(reg, idx[0:1, s:s + 1])
                return sp.snap(reg, min_val=0, max_val=EXPERTS - 1)

            def load_expert(n, w, e):
                for c in range(KT):
                    sp.wait_ge(wt_done, n + c - 1)
                    sp.dma_start(stage_w[c % 2][:, :],
                                 w[bass.ds(e, 1), c].rearrange("o p n -> (o p) n")).then_inc(w_in[c % 2], 16)

            e = expert(0)
            load_expert(W1_N(0), w1, e)
            for s in range(SLOTS):
                if s > 0:
                    sp.wait_ge(eo_done, 2 * TB * s)
                sp.dma_start(b2b[:, :], b2[bass.ds(e, 1), :].to_broadcast([P, D])).then_inc(b2_in, 16)
                load_expert(W1_N(s) + KT, w2, e)
                if s + 1 < SLOTS:
                    e = expert(s + 1)
                    load_expert(W1_N(s + 1), w1, e)
            sp.wait_ge(x_out, 16 * TT)

        @block.gpsimd
        def _(pool):
            pool.memset(zero[:, :], 0.0).then_inc(made, 1)
            pool.memset(identf[:, :], 0.0).then_inc(made, 1)
            pool.memset(onesf[:, :], 1.0).then_inc(made, 1)
            pool.wait_ge(made, 3)
            pool.affine_select(out=identf[:, :], in_=identf[:, :], compare_op=ALU.not_equal, fill=1.0, base=0,
                               pattern=[[-1, P]], channel_multiplier=1).then_inc(made, 1)

            def split(n, stage, hi, lo):
                pool.wait_ge(w_in[stage], 16 * ((n - stage) // 2 + 1) if isinstance(n, int) else 8 * n - 8 * stage + 16)
                pool.tensor_tensor(hi, stage_w[stage][:, :], zero[:, :].to_broadcast([P, D]), ALU.add).then_inc(wt_hi, 1)
                pool.wait_ge(wt_hi, n + 1)
                pool.tensor_tensor(lo, stage_w[stage][:, :], hi, ALU.subtract).then_inc(wt_done, 1)

            def split_group(name, hi, lo):
                first, count = WT_AT[name], dict(WT_LAYOUT)[name]
                with pool.Fori(0, count // 2) as i:
                    for j in range(2):
                        at_col = bass.ds(i * (2 * D) + j * D, D)
                        split(first + 2 * i + j, j, hi[:, at_col], lo[:, at_col])

            split_group("kv", kv_h, kv_l)
            pool.wait_ge(kv_step, B * KT)
            split_group("down", down_h, down_l)
            split_group("org", org_h, org_l)
            pool.wait_ge(k_out, 64)
            pool.wait_ge(x_pre, TT)
            split_group("up", up_h, up_l)
            pool.wait_ge(h_mm, B * JT)
            pool.wait_ge(lq_mm, 1)
            split_group("q", q_h, q_l)
            pool.wait_ge(nat_mm, 2 * TT)
            split_group("o", o_h, o_l)

            def stage_values(g):
                if g >= 2:
                    pool.wait_ge(pv_mm, KT * (g - 1))
                kv, b = divmod(g, B)
                src = V[:, b * KT * KVD:(b + 1) * KT * KVD].rearrange("p (t n) -> p t n", t=KT)
                pool.tensor_copy(VS[b].rearrange("p (t n) -> p t n", t=KT), src[:, :, ds(kv, HD)]).then_inc(vs_done, 1)

            def divide(g):
                kv, b = divmod(g, B)
                cols = slice(kv * D + b * S, kv * D + (b + 1) * S)
                if g > 0:
                    pool.wait_ge(o_step, O_STEPS * g)
                pool.wait_ge(rec_done, 4 * (g + 1))
                pool.tensor_tensor(onat, o_raw[g % 2], rec, ALU.mult).then_inc(o_step, 1)
                pool.wait_ge(o_step, O_STEPS * g + 1)
                pool.tensor_tensor(XTh[:, cols], onat, zero[:, :].to_broadcast([P, S]), ALU.add).then_inc(o_step, 1)
                pool.wait_ge(o_step, O_STEPS * g + 2)
                pool.tensor_tensor(XTl[:, cols], onat, XTh[:, cols], ALU.subtract).then_inc(o_step, 1)

            pool.wait_ge(q_mm, B * KT)
            stage_values(0)
            stage_values(1)
            for g in range(GROUPS):
                for j in range(KT // 2):
                    pool.wait_ge(exp_done, STEPS * g + 2 * REP * (j + 1))
                    if 4 * g + j >= 2:
                        pool.wait_ge(one_mm, 4 * g + j - 1)
                    pool.tensor_tensor(PS[j % 2], PB[2 * j % 4], PB[2 * j % 4 + 1], ALU.add).then_inc(p_add, 1)
                    if j == 0 and 1 <= g < GROUPS - 1:
                        stage_values(g + 1)
                    if g > 0 and j == (1 if g == GROUPS - 1 else KT // 2 - 1):
                        divide(g - 1)
            divide(GROUPS - 1)

            for n in range(N_WT, N_WT + 2 * KT * SLOTS):
                hi, lo = ((w1_h, w1_l), (w2_h, w2_l))[(n - N_WT) // KT % 2]
                cols = ds((n - N_WT) % KT, D)
                pool.wait_ge(ew_hi, n - N_WT + 1)
                pool.tensor_tensor(lo[:, cols], stage_w[n % 2][:, :], hi[:, cols], ALU.subtract).then_inc(wt_done, 1)

        @block.tensor
        def _(pe):
            pe.wait_ge(madeb, 2)

            def triple(outs, ah, al, bh, bl, first, last):
                for a, bs in ((ah, bh), (ah, bl), (al, bh)):
                    for o, m in zip(outs, bs):
                        mm = pe.matmul(o, a, m, start=first and a is ah and bs is bh,
                                       stop=last and a is al)
                return mm

            def kv_tile(k, first):
                def c(t, n0, n):
                    return t[:, k * D + n0:k * D + n0 + n]

                def w(t, n0, n):
                    return t[:, k * HALF + n0:k * HALF + n0 + n]

                for m in range(2):
                    for a, r in ((kv_h, ct_h), (kv_h, ct_l), (kv_l, ct_h)):
                        for h in range(2):
                            mm = pe.matmul(bank[2 * m + h][:, :], w(a, m * P, P), c(r, h * HALF, HALF),
                                           start=first and a is kv_h and r is ct_h, stop=False, skip_group_check=True)
                for t in range(KT):
                    for a, r in ((ct_h, kv_h), (ct_h, kv_l), (ct_l, kv_h)):
                        mm = pe.matmul(bank[4 + t // 2][:, (t % 2) * KVD:(t % 2 + 1) * KVD], c(a, t * P, P),
                                       w(r, KVD, KVD), start=first and t % 2 == 0 and a is ct_h and r is kv_h,
                                       stop=False, skip_group_check=True)
                return mm

            def keys_values(b):
                for k in range(KT):
                    if b == 0:
                        pe.wait_ge(wt_done, k // 2 + 1)
                    pe.wait_ge(c_done, CHUNKS.index(("T", b, k)) + 1)
                    mm = kv_tile(k, k == 0)
                    mm.then_inc(kv_step, 1)

            keys_values(0)
            pe.wait_ge(k_lo, 4)
            pe.wait_ge(v_act, 2)
            pe.wait_ge(v_dve, 2)
            keys_values(1)

            pe.wait_ge(c_done, len(CHUNKS))
            pe.wait_ge(v_act, 4)
            pe.wait_ge(v_dve, 4)

            def column_sums(b):
                for h in range(2):
                    for k in range(KT):
                        mm = pe.matmul(bank[4 + 2 * b + h][:, :], onesb[:, :],
                                       Q2[b][:, k * D + h * HALF:k * D + (h + 1) * HALF], start=k == 0, stop=k == KT - 1)
                mm.then_inc(cs_mm, 1)

            def turn_quantised(t):
                if t >= 4:
                    pe.wait_ge(xq_t, t - 3)
                for k in range(KT):
                    mm = pe.transpose(bank_b[t % 4][:, k * P:(k + 1) * P], XQ[:, t * D + k * P:t * D + (k + 1) * P],
                                      identb[:, :])
                mm.then_inc(xq_turned, 1)

            column_sums(0)
            pe.wait_ge(xq_done, TT)
            pe.wait_ge(k_lo, 8)
            for t in range(4):
                turn_quantised(t)
            column_sums(1)
            for t in range(4, TT):
                turn_quantised(t)

            def pair(m):
                return bank[2 * (m % 2)], bank[2 * (m % 2) + 1]

            def turn_behind(n, par, mean_too=False):
                pe.wait_ge(xn_done, TT + n + 1)
                pe.wait_ge(t_lo, 2 * n)
                for k in range(KT):
                    mm = pe.transpose(bank[4 + k // 4][:, (k % 4) * P:(k % 4 + 1) * P], xn[par][:, k * P:(k + 1) * P],
                                      identf[:, :])
                if mean_too:
                    for k in range(KT):
                        c = (n // TB) * KT + k
                        mm = pe.matmul(bank[6][:, c:c + 1], xn[par][:, k * P:(k + 1) * P], onesf[:, 0:1],
                                       start=n == 0 and k == 0, stop=n % TB == TB - 1, skip_group_check=True)
                mm.then_inc(turned, 1)

            pe.wait_ge(xq_t, TT)
            pe.wait_ge(cb_done, 4)
            for t in range(TT):
                if t >= 2:
                    pe.wait_ge(x_up, 2 * (t - 1))
                for h in range(2):
                    for k in range(KT):
                        mm = pe.matmul(pair(t)[h][:, :], XTh[:, k * D + t * P:k * D + (t + 1) * P],
                                       Q2[t // TB][:, k * D + h * HALF:k * D + (h + 1) * HALF],
                                       start=k == 0, stop=k == KT - 1)
                mm.then_inc(nat_mm, 1)
                if t >= 1:
                    turn_behind(t - 1, (t - 1) % 2, True)
            turn_behind(TT - 1, (TT - 1) % 2, True)

            pe.wait_ge(lqw_in, 16)
            pe.wait_ge(x_up, 2 * TT)
            pe.wait_ge(t_lo, 2 * TT)
            pe.wait_ge(mean_step, 1)
            for k in range(KT):
                mm = pe.matmul(bank[4][:, 0:B], LQW[:, k * P:(k + 1) * P], mean[:, :, k], start=k == 0, stop=k == KT - 1)
            mm.then_inc(lq_mm, 1)

            def lora_hidden(u):
                b, j = divmod(u, JT)
                if u >= 4:
                    pe.wait_ge(h_lo, u - 3)
                for k in range(KT):
                    mm = triple([bank[u % 4][:, :]], down_h[:, k * ER + j * P:k * ER + (j + 1) * P],
                                down_l[:, k * ER + j * P:k * ER + (j + 1) * P],
                                [XTh[:, k * D + b * S:k * D + (b + 1) * S]], [XTl[:, k * D + b * S:k * D + (b + 1) * S]],
                                k == 0, k == KT - 1)
                mm.then_inc(h_mm, 1)

            pe.wait_ge(wt_done, WT_AT["org"])
            lora_hidden(0)
            pe.wait_ge(co_step, 1)
            for b in range(B):
                mm = pe.matmul(bank[5][0:1, b * E_LORA:(b + 1) * E_LORA], lq[:, b:b + 1], keys[:, :], start=True, stop=True)
            mm.then_inc(sc_mm, 1)
            lora_hidden(1)
            pe.wait_ge(co_step, 6)
            pe.matmul(bank[6][:, 0:B * E_LORA], onesf[0:1, :], coef[0:1, 3, :], start=True, stop=True).then_inc(bc_mm, 1)
            for u in range(2, B * JT):
                lora_hidden(u)

            def token_tile(m, t, par, w_h, w_l, lora):
                pe.wait_ge(x_up, 2 * (m - 1))
                outs = [bank[2 * par][:, :], bank[2 * par + 1][:, :]]
                for k in range(KT):
                    cols = bass.ds(k * D + t * P, P)
                    mm = triple(outs, XTh[:, cols], XTl[:, cols],
                                [w_h[:, k * D + h * HALF:k * D + (h + 1) * HALF] for h in range(2)],
                                [w_l[:, k * D + h * HALF:k * D + (h + 1) * HALF] for h in range(2)],
                                k == 0, k == KT - 1 and not lora)
                if lora:
                    for j in range(JT):
                        cols = bass.ds(j * D + t * P, P)
                        mm = triple(outs, HT_h[:, cols], HT_l[:, cols],
                                    [up_h[:, j * D + h * HALF:j * D + (h + 1) * HALF] for h in range(2)],
                                    [up_l[:, j * D + h * HALF:j * D + (h + 1) * HALF] for h in range(2)],
                                    False, j == JT - 1)
                mm.then_inc(nat_mm, 1)

            def token_phase(m0, w_h, w_l, lora, before_rest=lambda: None, before_last=lambda: None):
                token_tile(m0, 0, 0, w_h, w_l, lora)
                before_rest()
                with pe.Fori(0, TT // 2 - 1) as i:
                    token_tile(2 * i + (m0 + 1), 2 * i + 1, 1, w_h, w_l, lora)
                    turn_behind(2 * i + m0, 0)
                    token_tile(2 * i + (m0 + 2), 2 * i + 2, 0, w_h, w_l, lora)
                    turn_behind(2 * i + (m0 + 1), 1)
                token_tile(m0 + TT - 1, TT - 1, 1, w_h, w_l, lora)
                turn_behind(m0 + TT - 2, 0)
                before_last()
                turn_behind(m0 + TT - 1, 1)

            pe.wait_ge(h_lo, B * JT)
            pe.wait_ge(wt_done, WT_AT["q"])
            token_phase(TT, org_h, org_l, True)

            pe.wait_ge(wt_done, WT_AT["o"])
            pe.wait_ge(x_up, 4 * TT)
            pe.wait_ge(t_lo, 4 * TT)
            def score_step(g, n):
                h, qt, kh = n // 8, n // 2 % 4, n % 2
                u = STEPS * g + n
                if u >= 3:
                    pe.wait_ge(s_max, u - 2)
                pe.matmul(bank[s_bank[u % 3]][:, :], QS[g % 3][0:96, h * S + qt * P:h * S + (qt + 1) * P],
                          KS[g % 3][0:96, kh * HALF:(kh + 1) * HALF], start=True, stop=True).then_inc(s_mm, 1)

            def max_row(g, h):
                pe.wait_ge(nm_step, 3 * (REP * g + h + 1))
                if REP * g + h > 0:
                    pe.wait_ge(nm_row, REP * g + h)
                for qt in range(TB):
                    mm = pe.transpose(bank_b[4][96:98, qt * P:(qt + 1) * P], nm[:, h % 2, qt, :], identb[:, :])
                mm.then_inc(nm_turned, 1)

            def over_keys(out_bank, weights, probs, first, last):
                for h in range(REP):
                    mm = pe.matmul(out_bank[h * HD:(h + 1) * HD, :], weights, probs[:, h * S:(h + 1) * S],
                                   start=first, stop=last)
                return mm

            def weigh(g, kt):
                pe.wait_ge(exp_done, STEPS * g + REP * (kt + 1))
                if kt == 0:
                    pe.wait_ge(vs_done, g + 1)
                    if g > 0:
                        pe.wait_ge(o_out, g)
                over_keys(bank[5], VS[g % 2][:, kt * HD:(kt + 1) * HD], PB[kt % 4], kt == 0,
                          kt == KT - 1).then_inc(pv_mm, 1)

            def total(g, j):
                pe.wait_ge(p_add, 4 * g + j + 1)
                if j == 0 and g > 0:
                    pe.wait_ge(sum_out, g)
                over_keys(bank[6], onesf[:, 0:HD], PS[j % 2], j == 0, j == KT // 2 - 1).then_inc(one_mm, 1)

            def loaded(g):
                pe.wait_ge(qk_in[g % 3], 96 * (g // 3 + 1))

            def group(g):
                for t in range(STEPS):
                    kt, h = divmod(t, REP)
                    if g + 1 < GROUPS:
                        if t == 0:
                            loaded(g + 1)
                        score_step(g + 1, t)
                    if t < REP:
                        pe.wait_ge(nm_row, REP * g + t + 1)
                    if STEPS * g + t >= 2:
                        pe.wait_ge(exp_done, STEPS * g + t - 1)
                    pe.matmul(bank[2 + t % 2][:, :], KS[g % 3][0:98, kt * P:(kt + 1) * P],
                              QS[g % 3][0:98, h * S:(h + 1) * S], start=True, stop=True).then_inc(st_mm, 1)
                    if g > 0 and t == LAST_TURN:
                        max_row(g, REP - 1)
                    if g + 1 < GROUPS and t in TURN_AT:
                        max_row(g + 1, TURN_AT[t])
                    if t % 4 == 2:
                        if t > 4:
                            weigh(g, t // 4 - 1)
                        elif g > 0:
                            weigh(g - 1, KT - 1)
                    if t % 8 == 0:
                        if t > 8:
                            total(g, t // 8 - 2)
                        elif g > 0:
                            total(g - 1, KT // 2 - 2 + t // 8)

            for item in range(B * KT):
                b, c = divmod(item, KT)
                if item == Q_S:
                    loaded(0)
                for n in scores_in(item):
                    score_step(0, n)
                if item in Q_TURN:
                    max_row(0, Q_TURN[item])
                if item >= 4:
                    pe.wait_ge(q_lo, item - 3)
                for k in range(KT):
                    w, r = slice(k * D + c * P, k * D + (c + 1) * P), slice(b * S + k * D, b * S + k * D + S)
                    mm = triple([bank[Q_BANKS[item % 4]][:, :]], q_h[:, w], q_l[:, w], [XTh[:, r]], [XTl[:, r]],
                                k == 0, k == KT - 1)
                mm.then_inc(q_mm, 1)
            pe.wait_ge(q_lo, B * KT)
            pe.wait_ge(minus_row, 3)
            for g in range(GROUPS):
                group(g)
            total(GROUPS - 1, KT // 2 - 2)
            weigh(GROUPS - 1, KT - 1)
            total(GROUPS - 1, KT // 2 - 1)

            def gate_logits(first, end):
                pe.wait_ge(t_lo, 2 * (2 * TT + end))
                for t in range(first, end):
                    for k in range(KT):
                        cols = slice(k * D + t * P, k * D + (t + 1) * P)
                        e3 = slice(k * EXPERTS, (k + 1) * EXPERTS)
                        mm = triple([bank[6][:, t * EXPERTS:(t + 1) * EXPERTS]], XTh[:, cols], XTl[:, cols],
                                    [gwh[:, e3]], [gwl[:, e3]], k == 0, k == KT - 1)
                return mm

            pe.wait_ge(o_step, O_STEPS * (GROUPS - 1))
            pe.wait_ge(wt_done, N_WT)
            token_phase(2 * TT, o_h, o_l, False, lambda: pe.wait_ge(o_step, O_STEPS * GROUPS),
                        lambda: gate_logits(0, TT - 2))

            gate_logits(TT - 2, TT).then_inc(lg_mm, 1)
            pe.wait_ge(am_done, 4)
            pe.matmul(bank[7][:, 0:2 * TT], onesf[:, :], AM[:, :, :].rearrange("p a t -> p (a t)"), start=True,
                      stop=True).then_inc(as_mm, 1)
            pe.wait_ge(rt_step, RT_READ)

            def first_layer(s, b):
                for f in range(KT):
                    pe.wait_ge(act_done, KT * s + (f - 3))
                    for k in range(KT):
                        if f == 0:
                            pe.wait_ge(wt_done, W1_N(s) + (k + 1))
                        cols = bass.ds(b * S + k * D, S)
                        w = slice(k * D + f * P, k * D + (f + 1) * P)
                        mm = triple([bank[f % 4][:, :]], w1_h[:, w], w1_l[:, w], [XTh[:, cols]], [XTl[:, cols]],
                                    k == 0, k == KT - 1)
                    mm.then_inc(a_mm, 1)

            def second_layer(s):
                for i in range(TB):
                    if not isinstance(s, int) or s > 0 or i >= 2:
                        pe.wait_ge(eo_done, 2 * TB * s + (2 * i - 2))
                    else:
                        pe.wait_ge(act_done, 6 + 2 * i)
                    outs = [bank[4 + 2 * (i % 2)][:, :], bank[5 + 2 * (i % 2)][:, :]]
                    for f in range(KT):
                        if i == 0:
                            pe.wait_ge(e_lo, KT * s + (f + 1))
                            pe.wait_ge(wt_done, W1_N(s) + (KT + f + 1))
                        cols = slice(f * S + i * P, f * S + (i + 1) * P)
                        mm = triple(outs, HT_h[:, cols], HT_l[:, cols],
                                    [w2_h[:, f * D + h * HALF:f * D + (h + 1) * HALF] for h in range(2)],
                                    [w2_l[:, f * D + h * HALF:f * D + (h + 1) * HALF] for h in range(2)],
                                    f == 0, f == KT - 1)
                    mm.then_inc(b_mm, 1)

            for k in range(KT):
                pe.wait_ge(wt_done, W1_N(0) + k + 1)
                for f in range(KT):
                    w = slice(k * D + f * P, k * D + (f + 1) * P)
                    mm = triple([bank[f][:, :]], w1_h[:, w], w1_l[:, w], [XTh[:, k * D:k * D + S]],
                                [XTl[:, k * D:k * D + S]], k == 0, k == KT - 1)
                    if k == KT - 1:
                        mm.then_inc(a_mm, 1)
            second_layer(0)
            first_layer(1, 0)
            second_layer(1)
            with pe.Fori(TOPK, SLOTS) as s:
                first_layer(s, 1)
                second_layer(s)

        @block.scalar
        def _(act):
            act.sem_inc(abs_done, 1)
            act.wait_ge(const_in, 64)
            act.activation(tg[:, :], sc[:, SC_GX:SC_GX + 4], ACT.Tanh).then_inc(tg_done, 1)

            def chunk(n):
                kind, b, k = CHUNKS[n]
                act.wait_ge(c_in[n % RING], 16 * (n // RING + 1))
                if kind == "T":
                    if b == 1:
                        act.wait_ge(kv_step, k + 1)
                    act.activation(ct_h[:, k * D:(k + 1) * D], ring[n % RING], ACT.Copy).then_inc(c_act, 1)
                else:
                    act.activation(ring[n % RING], ring[n % RING], ACT.Identity, bias=sc[:, SC_Z2:SC_Z2 + 1],
                                   scale=rs2[:, 0:1]).then_inc(c_act, 1)

            def root(n, par):
                act.wait_ge(ln_step, 8 * n + 4)
                act.activation(lnv[par][:, 1:2], lnv[par][:, 0:1], ACT.Sqrt).then_inc(ln_sd, 1)

            def scale_x(t):
                act.wait_ge(xn_done, t + 1)
                act.activation(xn[t % 2][:, :], xn[t % 2][:, :], ACT.Identity, bias=sc[:, SC_Z1:SC_Z1 + 1],
                               scale=rs1[:, 0:1]).then_inc(xq_sc, 1)

            def row_sum(t):
                act.wait_ge(xq_done, t + 1)
                if t > 0:
                    act.wait_ge(rowq_done, t)
                act.activation(junk_q, XQ[:, t * D:(t + 1) * D], ACT.Copy, accum_out=rowq[:, t:t + 1]).then_inc(rowq_done, 1)

            def kv_out(b):
                act.wait_ge(kv_step, KT * (b + 1))
                for i in range(4):
                    act.activation(kb[b][0][:, i * HALF:(i + 1) * HALF], bank[i][:, :], ACT.Copy).then_inc(k_hi, 1)
                for i in range(2):
                    at_v = b * KT * KVD + i * HALF
                    act.activation(V[:, at_v:at_v + HALF], bank[4 + i][:, :], ACT.Copy).then_inc(v_act, 1)

            act.wait_ge(qc_step, 2)
            for n in range(CH0):
                chunk(n)
            for t in range(TT):
                root(t, t % 2)
                chunk(CH0 + t)
                scale_x(t)
                if t > 0:
                    row_sum(t - 1)
            row_sum(TT - 1)
            kv_out(0)
            for n in range(CH0 + TT, len(CHUNKS)):
                chunk(n)
            act.wait_ge(rowq_done, TT)
            kv_out(1)
            for t in range(TT):
                act.wait_ge(xq_turned, t + 1)
                act.activation(per_tile(XTh)[:, :, t * P:(t + 1) * P],
                               bank_b[t % 4].rearrange("p (k n) -> p k n", k=KT), ACT.Copy).then_inc(xq_t, 1)

            def normalise(n, t, par, sums):
                root(n + TT, par)
                if sums:
                    act.wait_ge(xn_done, TT + n + 1)
                    act.wait_ge(abs_done, t + 1)
                    act.activation(junk, xn[par][:, :], ACT.Abs, accum_out=rowabs[:, bass.ds(t, 1)]).then_inc(abs_done, 1)
                act.wait_ge(turned, n + 1)
                for i in range(2):
                    act.activation(xt_tile(XTh, t, i), bank[4 + i][:, :].rearrange("p (k n) -> p k n", k=4),
                                   ACT.Copy).then_inc(t_hi, 1)

            def normalise_all(n0, sums):
                with act.Fori(0, TT // 2) as i:
                    for j in range(2):
                        normalise(2 * i + (n0 + j), 2 * i + j, j, sums)

            normalise_all(0, False)

            act.wait_ge(co_step, 3)
            act.activation(coef[0:1, 1, :], coef[0:1, 2, :], ACT.Exp, scale=float(K_LORA) ** -0.5).then_inc(co_exp, 1)
            act.wait_ge(cv_done, 2)
            for u in range(B * JT):
                b, j = divmod(u, JT)
                act.wait_ge(h_mm, u + 1)
                act.activation(HT_h[:, j * D + b * S:j * D + (b + 1) * S], bank[u % 4][:, :], ACT.Copy,
                               scale=cvec[:, u:u + 1]).then_inc(h_hi, 1)
            normalise_all(TT, False)

            def row_out(g, h):
                act.wait_ge(nm_turned, REP * g + h + 1)
                act.activation(QS[g % 3][96:98, h * S:(h + 1) * S], bank_b[4][96:98, 0:S], ACT.Copy).then_inc(nm_row, 1)

            def outputs_out(g):
                act.wait_ge(pv_mm, KT * (g + 1))
                if g >= 2:
                    act.wait_ge(o_step, O_STEPS * (g - 2) + 1)
                act.activation(o_raw[g % 2], bank[5][:, :], ACT.Copy).then_inc(o_out, 1)

            def sums_out(g):
                act.wait_ge(one_mm, 4 * (g + 1))
                if g > 0:
                    act.wait_ge(rec_done, 4 * g)
                act.activation(p_sum, bank[6][:, :], ACT.Copy).then_inc(sum_out, 1)

            def exp_group(g):
                for t in range(STEPS):
                    kt, h = divmod(t, REP)
                    act.wait_ge(st_mm, STEPS * g + t + 1)
                    if h == 0 and KT * g + kt >= 4:
                        act.wait_ge(pv_mm, KT * g + kt - 3)
                        act.wait_ge(p_add, (KT * g + kt - 4) // 2 + 1)
                    act.activation(PB[kt % 4][:, h * S:(h + 1) * S], bank[2 + t % 2][:, :], ACT.Exp,
                                   scale=float(HD) ** -0.5).then_inc(exp_done, 1)
                    if g > 0 and t == LAST_TURN:
                        row_out(g, REP - 1)
                    if g + 1 < GROUPS and t in TURN_AT:
                        row_out(g + 1, TURN_AT[t])
                    if g > 0 and t == 3:
                        outputs_out(g - 1)
                    if g > 0 and t == 10:
                        sums_out(g - 1)

            act.wait_ge(nat_mm, 2 * TT)
            for item in range(B * KT):
                if item in Q_TURN:
                    row_out(0, Q_TURN[item])
                act.wait_ge(q_mm, item + 1)
                if item >= 4:
                    act.wait_ge(q_out[item % 4], 32 * (item // 4))
                act.activation(qb_h[:, (item % 4) * S:(item % 4 + 1) * S], bank[Q_BANKS[item % 4]][:, :],
                               ACT.Copy).then_inc(q_hi, 1)
            for g in range(GROUPS):
                exp_group(g)
            outputs_out(GROUPS - 1)
            sums_out(GROUPS - 1)

            normalise_all(2 * TT, True)

            act.wait_ge(rt_step, RT_SHIFTED)
            act.activation(G[:, :, :], L[:, :, :], ACT.Exp).then_inc(rt_exp, 1)

            act.wait_ge(idx_done, 1)
            reg = act.alloc_register("expert_act")
            for s in range(SLOTS):
                b = s // TOPK
                act.reg_load(reg, idx[0:1, s:s + 1])
                for e, func in enumerate((ACT.Tanh, ACT.Gelu, ACT.Silu)):
                    with act.If_eq(reg, e):
                        for f in range(KT):
                            act.wait_ge(a_mm, KT * s + f + 1)
                            if s > 0:
                                act.wait_ge(e_lo, KT * (s - 1) + f + 1)
                            act.activation(hid[:, f * S:(f + 1) * S], bank[f % (4 if s > 0 else 8)][:, :], func,
                                           bias=b1t[:, e * KT + f:e * KT + f + 1]).then_inc(act_done, 1)
                if s % TOPK == TOPK - 1:
                    for t in range(b * TB, (b + 1) * TB):
                        act.wait_ge(x_fin, 2 * (TB * s + t - b * TB + 1))
                        act.dma_start(out[t], X[:, t * D:(t + 1) * D]).then_inc(x_out, 16)

        @block.vector
        def _(dve):
            dve.wait_ge(made, 4)
            dve.tensor_copy(identb[:, :], identf[:, :]).then_inc(madeb, 1)
            dve.tensor_copy(onesb[:, :], onesf[:, :]).then_inc(madeb, 1)
            dve.wait_ge(const_in, 64)
            dve.reciprocal(rs1[:, :], sc[:, SC_S1:SC_S1 + 1]).then_inc(qc_step, 1)
            dve.reciprocal(rs2[:, :], sc[:, SC_S2:SC_S2 + 1]).then_inc(qc_step, 1)
            dve.tensor_copy(gwh[:, :], gwf[:, :]).then_inc(qc_step, 1)
            dve.wait_ge(qc_step, 3)
            dve.tensor_tensor(gwl[:, :], gwf[:, :], gwh[:, :], ALU.subtract).then_inc(qc_step, 1)
            dve.wait_ge(tg_done, 1)
            dve.tensor_tensor(qc[:, 0:1], sc[:, SC_S1:SC_S1 + 1], sc[:, SC_S2:SC_S2 + 1], ALU.mult).then_inc(qc_step, 1)
            dve.tensor_scalar(qc[:, 1:2], sc[:, SC_Z1:SC_Z1 + 1], -1.0, MID, ALU.mult, ALU.add).then_inc(qc_step, 1)
            dve.tensor_scalar(qc[:, 2:3], sc[:, SC_Z2:SC_Z2 + 1], -1.0, MID, ALU.mult, ALU.add).then_inc(qc_step, 1)
            dve.wait_ge(qc_step, 7)
            dve.tensor_scalar(qc[:, 6:7], qc[:, 0:1], tg[:, 0:1], None, ALU.mult).then_inc(qc_step, 1)
            dve.tensor_scalar(qc[:, 5:6], qc[:, 1:2], float(D), None, ALU.mult).then_inc(qc_step, 1)
            dve.wait_ge(qc_step, 9)
            dve.tensor_tensor(qc[:, 3:4], qc[:, 6:7], qc[:, 1:2], ALU.mult).then_inc(qc_step, 1)
            dve.tensor_tensor(qc[:, 4:5], qc[:, 6:7], qc[:, 2:3], ALU.mult).then_inc(qc_step, 1)

            def chunk(n):
                kind, b, k = CHUNKS[n]
                cols = slice(k * D, (k + 1) * D)
                dve.wait_ge(c_act, n + 1)
                if kind == "T":
                    dve.tensor_tensor(ct_l[:, cols], ring[n % RING], ct_h[:, cols], ALU.subtract).then_inc(c_done, 1)
                else:
                    clip_round(ring[n % RING], Q2[b][:, cols], c_clip, b * KT + k, c_done)

            def carry_wait():
                dve.memset(carrier[:, :], 0.0)

            def statistics(n, xt, par):
                v = lnv[par]
                carry_wait()
                for h in range(2):
                    dve.bn_stats(stats[par][:, h, :], xt(h)).then_inc(ln_step, 1)
                dve.wait_ge(ln_step, 8 * n + 2)
                carry_wait()
                dve.bn_aggr(mv[par][:, :], stats[par][:, :, :]).then_inc(ln_step, 1)
                dve.wait_ge(ln_step, 8 * n + 3)
                dve.tensor_scalar(v[:, 0:1], mv[par][:, 1:2], EPS, None, ALU.add).then_inc(ln_step, 1)

            def apply(n, xt, par, free):
                v = lnv[par]
                dve.wait_ge(ln_sd, n + 1)
                dve.reciprocal(v[:, 2:3], v[:, 1:2]).then_inc(ln_step, 1)
                dve.wait_ge(ln_step, 8 * n + 5)
                dve.scalar_tensor_tensor(out=v[:, 3:4], in0=v[:, 2:3], scalar=v[:, 2:3], in1=v[:, 0:1],
                                         op0=ALU.mult, op1=ALU.mult).then_inc(ln_step, 1)
                dve.wait_ge(ln_step, 8 * n + 6)
                dve.tensor_scalar(v[:, 4:5], v[:, 3:4], -0.5, 1.5, ALU.mult, ALU.add).then_inc(ln_step, 1)
                dve.wait_ge(ln_step, 8 * n + 7)
                dve.tensor_tensor(v[:, 5:6], v[:, 4:5], v[:, 2:3], ALU.mult).then_inc(ln_step, 1)
                dve.wait_ge(ln_step, 8 * n + 8)
                free()
                dve.tensor_scalar(xn[par][:, :], xt(None), mv[par][:, 0:1], v[:, 5:6], ALU.subtract,
                                  ALU.mult).then_inc(xn_done, 1)

            def clip_round(buf, dst, clip, n, done):
                dve.tensor_scalar(buf, buf, 0.0, QMAX, ALU.max, ALU.min).then_inc(clip, 1)
                dve.wait_ge(clip, n + 1)
                dve.tensor_scalar(dst, buf, MAGIC, MAGIC + MID, ALU.add, ALU.subtract).then_inc(done, 1)

            def normalise(n, xt, par, free):
                statistics(n, xt, par)
                apply(n, xt, par, free)

            def x_tile(t):
                return lambda h: X[:, t * D:(t + 1) * D] if h is None else X[:, t * D + h * HALF:t * D + (h + 1) * HALF]

            def quantise_x(t):
                dve.wait_ge(xq_sc, t + 1)
                clip_round(xn[t % 2][:, :], XQ[:, t * D:(t + 1) * D], xq_clip, t, xq_done)

            def kv_out(b):
                for i in range(2):
                    dve.wait_ge(kv_step, KT * (b + 1))
                    at_v = b * KT * KVD + (2 + i) * HALF
                    dve.tensor_copy(V[:, at_v:at_v + HALF], bank[6 + i][:, :]).then_inc(v_dve, 1)
                for i in range(4):
                    dve.wait_ge(k_hi, 4 * b + i + 1)
                    cols = slice(i * HALF, (i + 1) * HALF)
                    dve.tensor_tensor(kb[b][1][:, cols], bank[i][:, :], kb[b][0][:, cols], ALU.subtract).then_inc(k_lo, 1)

            for n in range(CH0):
                chunk(n)
            for t in range(TT):
                dve.wait_ge(x_in[t], 16)
                statistics(t, x_tile(t), t % 2)
                if t > 0:
                    quantise_x(t - 1)
                apply(t, x_tile(t), t % 2, lambda: None)
                chunk(CH0 + t)
            quantise_x(TT - 1)
            kv_out(0)
            for n in range(CH0 + TT, len(CHUNKS)):
                chunk(n)
            dve.wait_ge(rowq_done, TT)
            dve.wait_ge(qc_step, 11)
            dve.tensor_scalar(rterm[:, :], rowq[:, :], qc[:, 5:6], qc[:, 4:5], ALU.add, ALU.mult).then_inc(rterm_done, 1)
            kv_out(1)
            dve.wait_ge(k_out, 32)
            for b in range(B):
                dve.wait_ge(cs_mm, b + 1)
                for h in range(2):
                    dve.tensor_scalar(CB[:, b, h * HALF:(h + 1) * HALF], bank[4 + 2 * b + h][:, :], qc[:, 3:4], None,
                                      ALU.mult).then_inc(cb_done, 1)

            def lo_parts(n, t):
                for i in range(2):
                    dve.wait_ge(t_hi, 2 * n + (i + 1))
                    dve.tensor_tensor(xt_tile(XTl, t, i), bank[4 + i][:, :].rearrange("p (k n) -> p k n", k=4),
                                      xt_tile(XTh, t, i), ALU.subtract).then_inc(t_lo, 1)

            dve.wait_ge(rterm_done, 1)
            dve.wait_ge(cb_done, 4)
            for t in range(TT):
                xt = X[:, t * D:(t + 1) * D]
                dve.scalar_tensor_tensor(out=xt, in0=xt, scalar=rterm[:, t:t + 1], in1=CB[:, t // TB, :],
                                         op0=ALU.add, op1=ALU.add).then_inc(x_pre, 1)
                dve.wait_ge(x_pre, t + 1)
                dve.wait_ge(nat_mm, t + 1)
                for h in range(2):
                    xh = X[:, t * D + h * HALF:t * D + (h + 1) * HALF]
                    dve.scalar_tensor_tensor(out=xh, in0=bank[2 * (t % 2) + h][:, :], scalar=qc[:, 6:7], in1=xh,
                                             op0=ALU.mult, op1=ALU.add).then_inc(x_up, 1)
                dve.wait_ge(x_up, 2 * (t + 1))
                statistics(TT + t, x_tile(t), t % 2)
                if t > 0:
                    lo_parts(t - 1, t - 1)
                apply(TT + t, x_tile(t), t % 2, lambda t=t: dve.wait_ge(turned, t - 1) if t >= 2 else None)
            lo_parts(TT - 1, TT - 1)

            dve.wait_ge(turned, TT)
            dve.tensor_scalar(mean[:, :, :].rearrange("p b k -> p (b k)"), bank[6][:, 0:B * KT], 1.0 / S, None,
                              ALU.mult).then_inc(mean_step, 1)

            dve.wait_ge(lq_mm, 1)
            dve.tensor_copy(lq[:, :], bank[4][:, 0:B]).then_inc(co_step, 1)
            dve.wait_ge(sc_mm, 1)
            c3 = [coef[0:1, i, :].rearrange("p (b e) -> p b e", b=B) for i in range(4)]
            s5 = bank[5][0:1, 0:B * E_LORA].rearrange("p (b e) -> p b e", b=B)

            def over_e(col):
                return coefs[0:1, col:col + B].rearrange("p (b o) -> p b o", o=1).to_broadcast([1, B, E_LORA])

            dve.tensor_reduce(coefs[0:1, 0:B], s5, AX.X, ALU.max).then_inc(co_step, 1)
            dve.wait_ge(co_step, 2)
            dve.tensor_tensor(c3[2], s5, over_e(0), ALU.subtract).then_inc(co_step, 1)
            dve.wait_ge(co_exp, 1)
            dve.tensor_reduce(coefs[0:1, B:2 * B], c3[1], AX.X, ALU.add).then_inc(co_step, 1)
            dve.wait_ge(co_step, 4)
            dve.reciprocal(coefs[0:1, 2 * B:3 * B], coefs[0:1, B:2 * B]).then_inc(co_step, 1)
            dve.wait_ge(co_step, 5)
            dve.tensor_tensor(c3[3], c3[1], over_e(2 * B), ALU.mult).then_inc(co_step, 1)
            dve.wait_ge(bc_mm, 1)
            for i in range(2):
                rows = slice(i * R_LORA, (i + 1) * R_LORA)
                dve.tensor_copy(cvec[rows, :], bank[6][rows, i:B * E_LORA:2]).then_inc(cv_done, 1)
            dve.wait_ge(cv_done, 2)
            for u in range(B * JT):
                b, j = divmod(u, JT)
                cols = slice(j * D + b * S, j * D + (b + 1) * S)
                dve.wait_ge(h_hi, u + 1)
                dve.scalar_tensor_tensor(out=HT_l[:, cols], in0=bank[u % 4][:, :], scalar=cvec[:, u:u + 1],
                                         in1=HT_h[:, cols], op0=ALU.mult, op1=ALU.subtract).then_inc(h_lo, 1)

            def token_phase(m0, gain, sums):
                with dve.Fori(0, TT // 2) as i:
                    for j in range(2):
                        t, m = 2 * i + j, 2 * i + (m0 + j)
                        dve.wait_ge(nat_mm, m + 1)
                        for h in range(2):
                            xh = X[:, bass.ds(t * D + h * HALF, HALF)]
                            dve.scalar_tensor_tensor(out=xh, in0=bank[2 * j + h][:, :], scalar=gain, in1=xh,
                                                     op0=ALU.mult, op1=ALU.add).then_inc(x_up, 1)
                        dve.wait_ge(x_up, 2 * (m + 1))

                        def free(m=m, t=t):
                            dve.wait_ge(turned, m - 1)
                            if sums:
                                dve.wait_ge(abs_done, t + 1)

                        normalise(m + TT, lambda h, t=t: X[:, bass.ds(t * D, D)] if h is None
                                  else X[:, bass.ds(t * D + h * HALF, HALF)], j, free)
                        lo_parts(m, t)

            token_phase(TT, tg[:, 2:3], False)

            def invert(g, quarter):
                cols = slice(quarter * S // 4, (quarter + 1) * S // 4)
                if quarter == 0:
                    dve.wait_ge(sum_out, g + 1)
                    if g > 0:
                        dve.wait_ge(o_step, O_STEPS * (g - 1) + 1)
                dve.reciprocal(rec[:, cols], p_sum[:, cols]).then_inc(rec_done, 1)

            def head_maximum(u):
                dve.wait_ge(s_max, 8 * u + 8)
                if u >= 2:
                    dve.wait_ge(nm_turned, u - 1)
                    dve.wait_ge(nm_step, 3 * u - 3)
                m = u % 2
                dve.tensor_tensor(mxc[:, m, :], mxp[:, m, :, 0], mxp[:, m, :, 1], ALU.max).then_inc(nm_step, 1)
                dve.tensor_tensor(nm[:, m, :, 0], mxp[:, m, :, 0], mxp[:, m, :, 1], ALU.max).then_inc(nm_step, 1)

            def head_lo(u):
                m = u % 2
                dve.wait_ge(nm_step, 3 * u + 2)
                dve.tensor_tensor(nm[:, m, :, 1], mxc[:, m, :], nm[:, m, :, 0], ALU.subtract).then_inc(nm_step, 1)

            def maximum(g, n):
                u = REP * g + n // 8
                dve.wait_ge(s_mm, STEPS * g + n + 1)
                dve.tensor_reduce(mxp[:, u % 2, n // 2 % 4, n % 2:n % 2 + 1], bank[s_bank[(STEPS * g + n) % 3]][:, :],
                                  AX.X, ALU.max).then_inc(s_max, 1)
                if n % 8 == 7:
                    head_maximum(u)
                    head_lo(u)

            dve.memset(KS[0][96:98, :], -1.0).then_inc(minus_row, 1)
            for item in range(B * KT):
                for n in scores_in(item):
                    maximum(0, n)
                cols = slice((item % 4) * S, (item % 4 + 1) * S)
                dve.wait_ge(q_hi, item + 1)
                dve.tensor_tensor(qb_l[:, cols], bank[Q_BANKS[item % 4]][:, :], qb_h[:, cols], ALU.subtract).then_inc(q_lo, 1)
            dve.wait_ge(q_mm, B * KT)
            for ks in KS[1:]:
                dve.memset(ks[96:98, :], -1.0).then_inc(minus_row, 1)

            for g in range(1, GROUPS):
                for n in range(STEPS):
                    maximum(g, n)
                    if g >= 2 and n >= STEPS // 2 and n % 4 == 2:
                        invert(g - 2, n // 4 - 4)
            for g in (GROUPS - 2, GROUPS - 1):
                for quarter in range(4):
                    invert(g, quarter)

            token_phase(2 * TT, tg[:, 1:2], True)

            dve.wait_ge(abs_done, 1 + TT)
            dve.memset(AM[:, 0, :], 0.0).then_inc(am_done, 1)
            dve.wait_ge(am_done, 1)
            dve.tensor_copy(AM[:, 0, 0:TT:TB], rowabs[:, 0:TT:TB]).then_inc(am_done, 1)
            dve.tensor_copy(AM[0:VISION - P, 0, 1:TT:TB], rowabs[0:VISION - P, 1:TT:TB]).then_inc(am_done, 1)
            dve.wait_ge(am_done, 3)
            dve.tensor_tensor(AM[:, 1, :], rowabs[:, :], AM[:, 0, :], ALU.subtract).then_inc(am_done, 1)

            done = [0]

            def nxt(instruction, after=None):
                instruction.then_inc(rt_step, 1)
                done[0] += 1
                dve.wait_ge(rt_step, done[0])

            dve.wait_ge(as_mm, 1)
            nxt(dve.tensor_reduce(AS[:, :, :].rearrange("p a b -> p (a b)"),
                                  bank[7][:, 0:2 * TT].rearrange("p (a t) -> p a t", t=TB), AX.X, ALU.add))
            nxt(dve.tensor_scalar(rt[:, 0:2], AS[:, 0, :], 1.0 / (VISION * D), 1e-8, ALU.mult, ALU.add))
            nxt(dve.reciprocal(rt[:, 2:4], rt[:, 0:2]))
            nxt(dve.tensor_scalar(rt[:, 4:6], AS[:, 1, :], 1.0 / ((S - VISION) * D), None, ALU.mult))
            nxt(dve.tensor_tensor(rt[:, 6:8], rt[:, 4:6], rt[:, 2:4], ALU.mult))
            for b in range(B):
                nxt(dve.scalar_tensor_tensor(out=rb[:, b, :], in0=sc[:, SC_GL:SC_GL + EXPERTS], scalar=rt[:, 6 + b:7 + b],
                                             in1=sc[:, SC_GB:SC_GB + EXPERTS], op0=ALU.mult, op1=ALU.add))
            dve.wait_ge(lg_mm, 1)
            for b in range(B):
                nxt(dve.tensor_tensor(L[:, b * TB:(b + 1) * TB, :],
                                      bank[6][:, b * TB * EXPERTS:(b + 1) * TB * EXPERTS].rearrange("p (t e) -> p t e", e=EXPERTS),
                                      rb[:, b:b + 1, :].to_broadcast([P, TB, EXPERTS]), ALU.add))
            assert done[0] == RT_READ

            def over_experts(v):
                return v.rearrange("p (t o) -> p t o", o=1).to_broadcast([P, TT, EXPERTS])

            nxt(dve.tensor_reduce(rv[:, 0, :], L[:, :, :], AX.X, ALU.max))
            nxt(dve.tensor_tensor(L[:, :, :], L[:, :, :], over_experts(rv[:, 0, :]), ALU.subtract))
            assert done[0] == RT_SHIFTED
            dve.wait_ge(rt_exp, 1)
            nxt(dve.tensor_reduce(rv[:, 1, :], G[:, :, :], AX.X, ALU.add))
            nxt(dve.reciprocal(rv[:, 2, :], rv[:, 1, :]))
            nxt(dve.tensor_tensor(G[:, :, :], G[:, :, :], over_experts(rv[:, 2, :]), ALU.mult))
            f0, f1, f2 = (G[0:1, 0:TT:TB, e] for e in range(EXPERTS))
            nxt(dve.tensor_tensor(rk[0:1, 0, :], f0, f1, ALU.is_ge))
            nxt(dve.tensor_tensor(rk[0:1, 1, :], f0, f2, ALU.is_ge))
            nxt(dve.tensor_tensor(rk[0:1, 2, :], f1, f2, ALU.is_ge))
            nxt(dve.tensor_tensor(rk[0:1, 3, :], rk[0:1, 0, :], rk[0:1, 2, :], ALU.subtract))
            nxt(dve.tensor_scalar(rk[0:1, 3, :], rk[0:1, 3, :], 1.0, None, ALU.add))
            nxt(dve.tensor_tensor(rk[0:1, 4, :], rk[0:1, 1, :], rk[0:1, 2, :], ALU.add))
            for j in range(TOPK):
                nxt(dve.tensor_scalar(rk[0:1, 5, :], rk[0:1, 3, :], float(j), None, ALU.is_equal))
                nxt(dve.tensor_scalar(rk[0:1, 6, :], rk[0:1, 4, :], float(j), 2.0, ALU.is_equal, ALU.mult))
                nxt(dve.tensor_tensor(idxf[0:1, :, j], rk[0:1, 5, :], rk[0:1, 6, :], ALU.add))
            dve.tensor_copy(idx[:, :], idxf[:, :, :].rearrange("p b j -> p (b j)")).then_inc(idx_done, 1)
            g0, g1, g2 = (G[:, :, e] for e in range(EXPERTS))
            nxt(dve.tensor_tensor(rv[:, 3, :], g0, g1, ALU.max))
            nxt(dve.tensor_tensor(rv[:, 4, :], g0, g1, ALU.min))
            nxt(dve.tensor_tensor(rv[:, 5, :], rv[:, 3, :], g2, ALU.max))
            nxt(dve.tensor_tensor(rv[:, 3, :], rv[:, 3, :], g2, ALU.min))
            nxt(dve.tensor_tensor(rv[:, 6, :], rv[:, 3, :], rv[:, 4, :], ALU.max))
            nxt(dve.tensor_tensor(rv[:, 7, :], rv[:, 5, :], rv[:, 6, :], ALU.add))
            nxt(dve.tensor_scalar(rv[:, 7, :], rv[:, 7, :], 1e-8, None, ALU.add))
            nxt(dve.reciprocal(rv[:, 8, :], rv[:, 7, :]))
            nxt(dve.tensor_scalar(rv[:, 8, :], rv[:, 8, :], tg[:, 3:4], None, ALU.mult))
            for j in range(TOPK):
                nxt(dve.tensor_tensor(TV[:, j * TT:(j + 1) * TT], rv[:, 5 + j, :], rv[:, 8, :], ALU.mult))

            def weight_hi(n):
                m = n - N_WT
                dve.wait_ge(w_in[n % 2], 16 * (n // 2 + 1))
                dve.tensor_copy((w1_h, w2_h)[m // KT % 2][:, ds(m % KT, D)], stage_w[n % 2][:, :]).then_inc(ew_hi, 1)

            for c in range(KT):
                weight_hi(W1_N(0) + c)
            for s in range(SLOTS):
                b, j = divmod(s, TOPK)
                if s > 0:
                    dve.wait_ge(b_mm, TB * s)
                ahead = 6 if s == 0 else 2
                for f in range(ahead):
                    weight_hi(W1_N(s) + KT + f)
                for f in range(KT):
                    if f + ahead < KT:
                        weight_hi(W1_N(s) + KT + f + ahead)
                    cols = slice(f * S, (f + 1) * S)
                    dve.wait_ge(act_done, KT * s + f + 1)
                    dve.tensor_copy(HT_h[:, cols], hid[:, cols]).then_inc(e_hi, 1)
                    dve.wait_ge(e_hi, KT * s + f + 1)
                    dve.tensor_tensor(HT_l[:, cols], hid[:, cols], HT_h[:, cols], ALU.subtract).then_inc(e_lo, 1)
                dve.wait_ge(b2_in, 16 * (s + 1))
                for i in range(TB):
                    if s + 1 < SLOTS:
                        if i == 0:
                            dve.wait_ge(a_mm, KT * (s + 1))
                        for c in (2 * i, 2 * i + 1):
                            weight_hi(W1_N(s + 1) + c)
                    dve.wait_ge(b_mm, TB * s + i + 1)
                    t = b * TB + i
                    for h in range(2):
                        hc = slice(h * HALF, (h + 1) * HALF)
                        xh = X[:, t * D + h * HALF:t * D + (h + 1) * HALF]
                        u = 2 * (TB * s + i) + h
                        if u >= 2:
                            dve.wait_ge(x_fin, u - 1)
                        dve.tensor_tensor(eo[h], bank[4 + 2 * (i % 2) + h][:, :], b2b[:, hc], ALU.add).then_inc(eo_done, 1)
                        dve.wait_ge(eo_done, u + 1)
                        dve.scalar_tensor_tensor(out=xh, in0=eo[h], scalar=TV[:, j * TT + t:j * TT + t + 1], in1=xh,
                                                 op0=ALU.mult, op1=ALU.add).then_inc(x_fin, 1)

    return nc


_SHAPES = {"x": (TT, P, D), "ctx_nat": (B, KT, P, D), "ctx_t": (B, KT, P, SC), "wts": (N_WT, P, D),
           "lora_q": (P, KT * P), "lora_keys": (P, E_LORA), "scalars": (1, N_SC), "gate_w": (P, KT * EXPERTS),
           "w1": (EXPERTS, KT, P, D), "b1": (P, EXPERTS * KT), "w2": (EXPERTS, KT, P, D), "b2": (EXPERTS, D)}


def kernel(**a):
    import concourse.bacc as bacc
    from concourse.bass_utils import run_bass_kernel_spmd

    a = {k: np.asarray(v) for k, v in a.items()}

    def chunks(w):
        n = D // w.shape[1]
        return w.reshape(-1, n, P, w.shape[1]).transpose(0, 2, 1, 3).reshape(-1, P, D)

    arrays = {
        "x": a["x"].reshape(TT, P, D),
        "ctx_nat": a["ctx_4096"].reshape(B, KT, P, D),
        "ctx_t": a["ctx_4096"].transpose(0, 2, 1).reshape(B, KT, P, SC),
        "wts": np.concatenate([
            chunks(np.concatenate([a["L1_xattn_Wk"], a["L1_xattn_Wv"]], axis=1)),
            chunks(a["L0_ffn_lora_down"].transpose(1, 0, 2).reshape(D, ER)),
            chunks(a["L0_ffn_W_org"].T),
            chunks(a["L0_ffn_lora_up"].reshape(ER, D)),
            chunks(a["L1_xattn_Wq"]),
            chunks(a["L1_xattn_Wo"])]),
        "lora_q": a["L0_ffn_Wq"].T.reshape(KT, P, K_LORA).transpose(1, 0, 2).reshape(P, KT * P),
        "lora_keys": a["L0_ffn_lora_keys"].T,
        "scalars": np.concatenate([
            a["L0_xattn_x1_scale"], a["L0_xattn_x1_zp"], a["L0_xattn_x2_scale"], a["L0_xattn_x2_zp"],
            a["g_xattn"], a["g_ffn"], a["L1_ffn_gate_b"], a["L1_ffn_gate_w"][D]]).reshape(1, N_SC),
        "gate_w": a["L1_ffn_gate_w"][:D].reshape(KT, P, EXPERTS).transpose(1, 0, 2).reshape(P, KT * EXPERTS),
        "w1": a["L1_ffn_w1"].reshape(EXPERTS, KT, P, D),
        "b1": a["L1_ffn_b1"].reshape(EXPERTS, KT, P).transpose(2, 0, 1).reshape(P, EXPERTS * KT),
        "w2": a["L1_ffn_w2"].reshape(EXPERTS, KT, P, D),
        "b2": a["L1_ffn_b2"],
    }
    nc = bacc.Bacc("TRN2", target_bir_lowering=False, num_devices=1)
    arrays = {k: np.ascontiguousarray(v) for k, v in arrays.items()}
    args = [nc.dram_tensor(f"{k}_in", _SHAPES[k], F32, kind="ExternalInput").ap() for k in _SHAPES]
    args.append(nc.dram_tensor("y_out", (TT, P, D), F32, kind="ExternalOutput").ap())
    build(nc, *args)
    r = run_bass_kernel_spmd(nc, [{f"{k}_in": arrays[k] for k in _SHAPES}], core_ids=[0])
    return r.results[0]["y_out"].reshape(B, S, D)
```
